# Optimizing a Trainium2 kernel written in Bass

```python
import numpy as np
import jax
import jax.numpy as jnp

def _softmax(x, axis=-1):
    return jax.nn.softmax(x, axis=axis)

def _gelu(x):
    return jax.nn.gelu(x, approximate=True)

def _silu(x):
    return jax.nn.silu(x)

def _sigmoid(x):
    return jax.nn.sigmoid(x)

def _layernorm(x, axis=-1, eps=1e-05):
    m = jnp.mean(x, axis=axis, keepdims=True)
    v = jnp.var(x, axis=axis, keepdims=True)
    return (x - m) / jnp.sqrt(v + eps)

def _scatter_add(tgt, idx, src, axis=0):
    return tgt.at[idx].add(src)

def _segment_sum(src, seg, n):
    return jax.ops.segment_sum(src, seg, n)
kernel_name = 'mk_recurrent_d1_jaxref_r8_01f5e1'

def setup_inputs(seed: int=0):
    np.random.seed(seed)
    _w = jnp.asarray

    def _L0_attn_setup():
        import jax, jax.numpy as jnp
        import numpy as np
        DIMS = 128
        HEAD = 16
        HD = DIMS // HEAD
        MAX_ITER = 3
        MIN_SIZE = 64
        MAX_SIZE = 256
        UP_WIN, DOWN_WIN = (1.1, 0.9)
        UP_DIFF, DOWN_DIFF = (0.05, 0.001)
        B, T = (2, 128)

        def _ln(x, w, eps=1e-05):
            m = jnp.mean(x, axis=-1, keepdims=True)
            v = jnp.var(x, axis=-1, keepdims=True)
            return (x - m) * jax.lax.rsqrt(v + eps) * w

        def _focus(x, Wq, bq, Wk, Wv, bv, Wo, bo, lna_w, lnb_w, lnc_w, lnd_w, lq_w, lq_b, lk_w, lk_b, lv_w, lv_b, threshold, temp_base, factor):
            b, t, d = x.shape
            q = _ln(x, lna_w) @ Wq.T + bq
            kk = _ln(x, lnb_w) @ Wk.T
            v = _ln(x, lnb_w) @ Wv.T + bv
            sc = HD ** (-0.25)

            def _shape(u):
                return u.reshape(b, t, HEAD, HD).transpose(0, 2, 1, 3)
            q_full = _shape(q * sc)
            k_full = _shape(kk * sc)
            v_full = _shape(v)
            thr = jax.lax.stop_gradient(threshold)
            fac = jax.lax.stop_gradient(factor)
            t0 = jax.lax.stop_gradient(temp_base)
            cw0 = jnp.int32(max(min(t, MAX_SIZE), MIN_SIZE))
            inv_sqrt_e = jnp.float32(1.0 / np.sqrt(HD))
            pos = jnp.arange(t)

            def step(carry, i):
                qcur, prev, attn, cw, temp, done = carry
                qp = qcur @ lq_w.T + lq_b
                kp = k_full @ lk_w.T + lk_b
                vp = v_full @ lv_w.T + lv_b
                sq = _ln(qp, lnc_w)
                sk = _ln(kp, lnd_w)
                tscale = jnp.where(temp > 0, jax.lax.rsqrt(temp), jnp.float32(1.0))
                sq = sq * tscale
                scores = jnp.einsum('bhqd,bhkd->bhqk', sq, sk) * inv_sqrt_e
                in_win = pos < cw
                scores = jnp.where(in_win[None, None, None, :], scores, -jnp.inf)
                probs = jax.nn.softmax(scores, axis=-1)
                out = jnp.einsum('bhqk,bhkd->bhqd', probs, vp)
                iter_out = jnp.where(in_win[None, None, :, None], out, 0.0)
                diff = jnp.mean(jnp.abs(iter_out - prev))
                converged = (diff < thr + fac * diff) & (i > 0)
                upd = ~done & ~converged
                new_done = done | converged
                attn_n = jnp.where(done, attn, iter_out)
                prev_n = jnp.where(upd, iter_out, prev)
                qcur_n = jnp.where(upd, qcur + iter_out, qcur)
                up = (cw.astype(jnp.float32) * UP_WIN).astype(jnp.int32)
                down = (cw.astype(jnp.float32) * DOWN_WIN).astype(jnp.int32)
                nw = jnp.where(diff > UP_DIFF, up, jnp.where((diff < DOWN_DIFF) & (cw > MIN_SIZE), down, cw))
                nw = jnp.clip(nw, MIN_SIZE, t)
                cw_n = jnp.where(upd, nw, cw)
                temp_n = jnp.where(upd, temp + jnp.float32(0.005), temp)
                return ((qcur_n, prev_n, attn_n, cw_n, temp_n, new_done), None)
            zeros = jnp.zeros_like(q_full)
            carry0 = (q_full, zeros, zeros, cw0, t0, jnp.array(False))
            (_, _, attn_out, _, _, _), _ = jax.lax.scan(step, carry0, jnp.arange(MAX_ITER))
            output = attn_out.transpose(0, 2, 1, 3).reshape(b, t, d)
            return output @ Wo.T + bo
        key = jax.random.key(seed)
        ks = jax.random.split(key, 12)

        def lin_w(k, o, i):
            return (jax.random.normal(k, (o, i), dtype=jnp.float32) / np.sqrt(i)).astype(jnp.float32)
        return {'x': jax.random.normal(ks[0], (B, T, DIMS), dtype=jnp.float32), 'Wq': lin_w(ks[1], DIMS, DIMS), 'bq': jnp.zeros((DIMS,), jnp.float32), 'Wk': lin_w(ks[2], DIMS, DIMS), 'Wv': lin_w(ks[3], DIMS, DIMS), 'bv': jnp.zeros((DIMS,), jnp.float32), 'Wo': lin_w(ks[4], DIMS, DIMS), 'bo': jnp.zeros((DIMS,), jnp.float32), 'lna_w': jnp.ones((DIMS,), jnp.float32), 'lnb_w': jnp.ones((DIMS,), jnp.float32), 'lnc_w': jnp.ones((HD,), jnp.float32), 'lnd_w': jnp.ones((HD,), jnp.float32), 'lq_w': lin_w(ks[5], HD, HD), 'lq_b': jnp.zeros((HD,), jnp.float32), 'lk_w': lin_w(ks[6], HD, HD), 'lk_b': jnp.zeros((HD,), jnp.float32), 'lv_w': lin_w(ks[7], HD, HD), 'lv_b': jnp.zeros((HD,), jnp.float32), 'threshold': jnp.float32(0.01), 'temp_base': jnp.float32(1.0), 'factor': jnp.float32(0.1)}
    _L0_attn_in = _L0_attn_setup()

    def _L0_ffn_setup():
        import jax, jax.numpy as jnp
        import numpy as np
        D_MODEL, D_FF, D2, DL = (128, 512, 64, 64)
        D1 = D_FF // D2
        BATCH, SEQ = (2, 128)
        KERNEL_SCALE = D2 ** 0.5
        key = jax.random.key(seed)
        ks = jax.random.split(key, 7)
        xav = lambda k, shape, fan: jax.random.normal(k, shape, jnp.float32) * (2.0 / sum(fan)) ** 0.5
        x = jax.random.normal(ks[0], (BATCH, SEQ, D_MODEL), jnp.float32)
        m1 = xav(ks[1], (D_MODEL, DL), (D_MODEL, DL))
        m2 = xav(ks[2], (DL, D1, D2), (DL, D_FF))
        mb = jax.random.normal(ks[3], (D1, D2), jnp.float32)
        w1 = xav(ks[4], (D_MODEL, D1, D2), (D_MODEL, D_FF))
        w2 = xav(ks[5], (D2, D1, D_MODEL), (D_FF, D_MODEL)) * KERNEL_SCALE
        b2 = jax.random.normal(ks[6], (D_MODEL,), jnp.float32)
        return {'x': x, 'm1': m1, 'm2': m2, 'mb': mb, 'w1': w1, 'w2': w2, 'b2': b2}
    _L0_ffn_in = _L0_ffn_setup()
    _d = {'L0_attn_x': _L0_attn_in['x'], 'L0_attn_Wq': _L0_attn_in['Wq'], 'L0_attn_bq': _L0_attn_in['bq'], 'L0_attn_Wk': _L0_attn_in['Wk'], 'L0_attn_Wv': _L0_attn_in['Wv'], 'L0_attn_bv': _L0_attn_in['bv'], 'L0_attn_Wo': _L0_attn_in['Wo'], 'L0_attn_bo': _L0_attn_in['bo'], 'L0_attn_lna_w': _L0_attn_in['lna_w'], 'L0_attn_lnb_w': _L0_attn_in['lnb_w'], 'L0_attn_lnc_w': _L0_attn_in['lnc_w'], 'L0_attn_lnd_w': _L0_attn_in['lnd_w'], 'L0_attn_lq_w': _L0_attn_in['lq_w'], 'L0_attn_lq_b': _L0_attn_in['lq_b'], 'L0_attn_lk_w': _L0_attn_in['lk_w'], 'L0_attn_lk_b': _L0_attn_in['lk_b'], 'L0_attn_lv_w': _L0_attn_in['lv_w'], 'L0_attn_lv_b': _L0_attn_in['lv_b'], 'L0_attn_threshold': _L0_attn_in['threshold'], 'L0_attn_temp_base': _L0_attn_in['temp_base'], 'L0_attn_factor': _L0_attn_in['factor'], 'L0_ffn_m1': _L0_ffn_in['m1'], 'L0_ffn_m2': _L0_ffn_in['m2'], 'L0_ffn_mb': _L0_ffn_in['mb'], 'L0_ffn_w1': _L0_ffn_in['w1'], 'L0_ffn_w2': _L0_ffn_in['w2'], 'L0_ffn_b2': _L0_ffn_in['b2']}
    _x0 = _d['L0_attn_x']
    _d['L0_attn_x'] = jax.random.normal(jax.random.fold_in(jax.random.key(seed), 1), (8, 256, 128), dtype=_x0.dtype)
    del _x0
    return _d

def reference(L0_attn_x, L0_attn_Wq, L0_attn_bq, L0_attn_Wk, L0_attn_Wv, L0_attn_bv, L0_attn_Wo, L0_attn_bo, L0_attn_lna_w, L0_attn_lnb_w, L0_attn_lnc_w, L0_attn_lnd_w, L0_attn_lq_w, L0_attn_lq_b, L0_attn_lk_w, L0_attn_lk_b, L0_attn_lv_w, L0_attn_lv_b, L0_attn_threshold, L0_attn_temp_base, L0_attn_factor, L0_ffn_m1, L0_ffn_m2, L0_ffn_mb, L0_ffn_w1, L0_ffn_w2, L0_ffn_b2):

    def _L0_attn_ref(x, Wq, bq, Wk, Wv, bv, Wo, bo, lna_w, lnb_w, lnc_w, lnd_w, lq_w, lq_b, lk_w, lk_b, lv_w, lv_b, threshold, temp_base, factor):
        import jax, jax.numpy as jnp
        import numpy as np
        DIMS = 128
        HEAD = 16
        HD = DIMS // HEAD
        MAX_ITER = 3
        MIN_SIZE = 64
        MAX_SIZE = 256
        UP_WIN, DOWN_WIN = (1.1, 0.9)
        UP_DIFF, DOWN_DIFF = (0.05, 0.001)
        B, T = (2, 128)

        def _ln(x, w, eps=1e-05):
            m = jnp.mean(x, axis=-1, keepdims=True)
            v = jnp.var(x, axis=-1, keepdims=True)
            return (x - m) * jax.lax.rsqrt(v + eps) * w

        def _focus(x, Wq, bq, Wk, Wv, bv, Wo, bo, lna_w, lnb_w, lnc_w, lnd_w, lq_w, lq_b, lk_w, lk_b, lv_w, lv_b, threshold, temp_base, factor):
            b, t, d = x.shape
            q = _ln(x, lna_w) @ Wq.T + bq
            kk = _ln(x, lnb_w) @ Wk.T
            v = _ln(x, lnb_w) @ Wv.T + bv
            sc = HD ** (-0.25)

            def _shape(u):
                return u.reshape(b, t, HEAD, HD).transpose(0, 2, 1, 3)
            q_full = _shape(q * sc)
            k_full = _shape(kk * sc)
            v_full = _shape(v)
            thr = jax.lax.stop_gradient(threshold)
            fac = jax.lax.stop_gradient(factor)
            t0 = jax.lax.stop_gradient(temp_base)
            cw0 = jnp.int32(max(min(t, MAX_SIZE), MIN_SIZE))
            inv_sqrt_e = jnp.float32(1.0 / np.sqrt(HD))
            pos = jnp.arange(t)

            def step(carry, i):
                qcur, prev, attn, cw, temp, done = carry
                qp = qcur @ lq_w.T + lq_b
                kp = k_full @ lk_w.T + lk_b
                vp = v_full @ lv_w.T + lv_b
                sq = _ln(qp, lnc_w)
                sk = _ln(kp, lnd_w)
                tscale = jnp.where(temp > 0, jax.lax.rsqrt(temp), jnp.float32(1.0))
                sq = sq * tscale
                scores = jnp.einsum('bhqd,bhkd->bhqk', sq, sk) * inv_sqrt_e
                in_win = pos < cw
                scores = jnp.where(in_win[None, None, None, :], scores, -jnp.inf)
                probs = jax.nn.softmax(scores, axis=-1)
                out = jnp.einsum('bhqk,bhkd->bhqd', probs, vp)
                iter_out = jnp.where(in_win[None, None, :, None], out, 0.0)
                diff = jnp.mean(jnp.abs(iter_out - prev))
                converged = (diff < thr + fac * diff) & (i > 0)
                upd = ~done & ~converged
                new_done = done | converged
                attn_n = jnp.where(done, attn, iter_out)
                prev_n = jnp.where(upd, iter_out, prev)
                qcur_n = jnp.where(upd, qcur + iter_out, qcur)
                up = (cw.astype(jnp.float32) * UP_WIN).astype(jnp.int32)
                down = (cw.astype(jnp.float32) * DOWN_WIN).astype(jnp.int32)
                nw = jnp.where(diff > UP_DIFF, up, jnp.where((diff < DOWN_DIFF) & (cw > MIN_SIZE), down, cw))
                nw = jnp.clip(nw, MIN_SIZE, t)
                cw_n = jnp.where(upd, nw, cw)
                temp_n = jnp.where(upd, temp + jnp.float32(0.005), temp)
                return ((qcur_n, prev_n, attn_n, cw_n, temp_n, new_done), None)
            zeros = jnp.zeros_like(q_full)
            carry0 = (q_full, zeros, zeros, cw0, t0, jnp.array(False))
            (_, _, attn_out, _, _, _), _ = jax.lax.scan(step, carry0, jnp.arange(MAX_ITER))
            output = attn_out.transpose(0, 2, 1, 3).reshape(b, t, d)
            return output @ Wo.T + bo
        return _focus(x, Wq, bq, Wk, Wv, bv, Wo, bo, lna_w, lnb_w, lnc_w, lnd_w, lq_w, lq_b, lk_w, lk_b, lv_w, lv_b, threshold, temp_base, factor)

    def _L0_ffn_ref(x, m1, m2, mb, w1, w2, b2):
        import jax, jax.numpy as jnp
        import numpy as np
        D_MODEL, D_FF, D2, DL = (128, 512, 64, 64)
        D1 = D_FF // D2
        BATCH, SEQ = (2, 128)
        KERNEL_SCALE = D2 ** 0.5
        x_shape = x.shape
        xf = x.reshape(-1, x_shape[-1])
        d1 = w1.shape[1]
        lr = xf @ m1
        mask_logits = jnp.einsum('bl,lxy->bxy', lr, m2) + mb
        quant_mask = jnp.argmax(mask_logits, axis=-1)
        w1p = jnp.transpose(w1, (1, 2, 0))
        w2p = jnp.transpose(w2, (1, 0, 2))
        j = jnp.arange(d1)[None, :]
        w = w1p[j, quant_mask]
        mid = jnp.einsum('ai,aji->aj', xf, w)
        relu = jax.nn.relu(mid)
        v = w2p[j, quant_mask]
        res = jnp.einsum('ai,aij->aj', relu, v) + b2
        return res.reshape(x_shape)
    x = L0_attn_x
    xn = _layernorm(x, axis=-1)
    s = _L0_attn_ref(xn, L0_attn_Wq, L0_attn_bq, L0_attn_Wk, L0_attn_Wv, L0_attn_bv, L0_attn_Wo, L0_attn_bo, L0_attn_lna_w, L0_attn_lnb_w, L0_attn_lnc_w, L0_attn_lnd_w, L0_attn_lq_w, L0_attn_lq_b, L0_attn_lk_w, L0_attn_lk_b, L0_attn_lv_w, L0_attn_lv_b, L0_attn_threshold, L0_attn_temp_base, L0_attn_factor)
    g = _silu(_L0_ffn_ref(xn, L0_ffn_m1, L0_ffn_m2, L0_ffn_mb, L0_ffn_w1, L0_ffn_w2, L0_ffn_b2))
    x = x + s * g
    return x

_drawn_inputs = setup_inputs


def setup_inputs(seed=0):
    import zlib

    import numpy as np

    out = dict(_drawn_inputs(seed))
    spreads = {'L0_attn_bq': (0.0, 0.8),
     'L0_attn_bv': (0.0, 0.1),
     'L0_attn_bo': (0.0, 0.1),
     'L0_attn_lna_w': (1.0, 0.6),
     'L0_attn_lnb_w': (1.0, 0.6),
     'L0_attn_lnc_w': (1.0, 0.6),
     'L0_attn_lnd_w': (1.0, 0.6),
     'L0_attn_lq_b': (0.0, 0.728),
     'L0_attn_lk_b': (0.0, 0.8),
     'L0_attn_lv_b': (0.0, 0.1)}
    factors = {}
    for name, (base, spread) in spreads.items():
        noise = np.random.default_rng([zlib.crc32(name.encode()), seed]).standard_normal(out[name].shape)
        drawn = base * np.exp(spread * noise) if base else spread * noise
        out[name] = jnp.asarray(drawn.astype(out[name].dtype))
    for name, factor in factors.items():
        out[name] = (out[name] * factor).astype(out[name].dtype)
    return out
```

```python
from contextlib import ExitStack

import concourse.bass as bass
import numpy as np
from concourse import mybir

F32 = mybir.dt.float32
BF16 = mybir.dt.bfloat16
I32 = mybir.dt.int32
ALU = mybir.AluOpType
ACT = mybir.ActivationFunctionType
AX_X = mybir.AxisListType.X

P = 128
B, T, D = 8, 256, 128
H = 16
HD = D // H
QT = T // P
NT = B * QT
ITERS = 3
MIN_WIN, MAX_WIN = 64, 256
EPS = 1e-5
QK_SCALE = float(HD) ** -0.25
INV_SQRT_E = float(np.float32(1.0 / np.sqrt(HD)))
UP_DIFF, DOWN_DIFF = 0.05, 0.001
TEMP_STEP = 0.005
RSQRT_SEED = 0x5F3759DF
PENALTY = -1e30

D1, D2, DL = 8, 64, 64
F = D1 * D2
FT = F // P


def window_after(cw, factor):
    return int(np.clip(int(np.float32(cw) * np.float32(factor)), MIN_WIN, T))


CW0 = max(min(T, MAX_WIN), MIN_WIN)
CW_DOWN = window_after(CW0, 0.9)
CW_DOWN_UP = window_after(CW_DOWN, 1.1)
CW_DOWN_DOWN = window_after(CW_DOWN, 0.9)
assert window_after(CW0, 1.1) == CW0 == T and CW_DOWN > MIN_WIN
LEVELS = [CW_DOWN_DOWN, CW_DOWN, CW_DOWN_UP]
assert LEVELS == sorted(LEVELS) and LEVELS[-1] < T

Q_PARTS = [0, 0, 0, 1, 1, 2]
K_PARTS = [0, 1, 2, 0, 1, 0]
PAIR = 2 * HD
WIN_ROW = len(Q_PARTS) * PAIR
MAX_ROW = WIN_ROW + len(LEVELS)
STACK = MAX_ROW + 6
BANDS = [(0, 3, 0), (3, 2, 1), (5, 1, 2)]

UH = 8
UNITS = B * H // UH
CH = 2
CHUNKS = UH // CH
GH = 4
VC = 2 * HD + 1
QB = 4
EB = 8

COLS = ["bq", "bv", "lna", "lnb", "lqb", "lkb", "lvb", "thr", "temp", "fac", "level"]


class Steps:

    def __init__(self, eng, sem, base=0):
        self.eng, self.sem, self.base, self.n = eng, sem, base, 0

    def done(self, instruction):
        instruction.then_inc(self.sem, 1)
        self.n += 1

    def wait(self):
        self.eng.wait_ge(self.sem, self.base + self.n)


def build(nc, x, wq, wk, wv, wo_t, lq, lk, lv, lv_t, cols, lnc, lnd, bo, m1, m2, mb, w1, w2, b2,
          ident, blocks, centre, slots, token_pos, key_side, parity, out):
    ctx = ExitStack()
    with ctx:
        def sb(name, shape, dt=F32):
            return ctx.enter_context(nc.sbuf_tensor(name, shape, dt))

        def psum(name, shape, dt=F32):
            return ctx.enter_context(nc.psum_tensor(name, shape, dt))

        def sem(name):
            return ctx.enter_context(nc.semaphore(name))

        x_sb = sb("x_sb", [P, NT, D])
        xn = sb("xn", [P, NT, D])
        z = sb("z", [P, NT, D])
        xn_t = sb("xn_t", [P, NT * P])
        z_t = sb("z_t", [P, 2, P])
        kc, qc = z, xn
        attn = xn_t[:, :].rearrange("p (n d) -> p n d", n=NT)
        work = sb("work", [P, NT, D])
        gate = sb("gate", [P, NT, D])
        parts = sb("parts", [P, 3, NT, D], BF16)
        k_res = sb("k_res", [P, B, H * T], BF16)
        v_res = sb("v_res", [P, NT, H, VC])
        q_st = sb("q_st", [P, QB, UH // 2 * T], BF16)
        e_sb = sb("e_sb", [P, EB, QT * T])
        o_t = sb("o_t", [P, 2, 2 * T])
        tt = sb("tt", [P, QT, H, VC])
        mx = sb("mx", [P, 2, QT, UH])
        mr = sb("mr", [P, 2, QT, UH])
        mp = sb("mp", [P, 2, QT, UH, 3], BF16)
        m_t = sb("m_t", [P, 2, T], BF16)
        tp = sb("tp", [P, 2, 3, T], BF16)
        stat = sb("stat", [P, NT, 6])
        mv = sb("mv", [P, NT, 2])
        var = sb("var", [P, NT * H])
        y = sb("y", [P, NT * H])
        tmp = sb("tmp", [P, NT * H])
        tvar = sb("tvar", [P, QT * H])
        ty = sb("ty", [P, QT * H])
        ttmp = sb("ttmp", [P, QT * H])
        rden = sb("rden", [P, QT, H])
        o_new = sb("o_new", [P, QT, D])
        d_new = sb("d_new", [P, QT, D])
        r_new = sb("r_new", [P, QT, D])
        q_n = sb("q_n", [P, QT, D])
        pt = sb("pt", [P, 3, QT, D], BF16)
        dsum = sb("dsum", [P, B])
        dall = sb("dall", [P, 1])
        ctl = sb("ctl", [P, 16])
        notdone = sb("notdone", [P, 1], I32)
        rowmask = sb("rowmask", [P, QT])
        temps = sb("temps", [P, ITERS + 1])
        tsc = sb("tsc", [P, ITERS + 1])
        tsv = sb("tsv", [P, ITERS + 1])
        tst = sb("tst", [P, ITERS + 1])
        tsc_now = sb("tsc_now", [P, 1])
        zero_rows = sb("zero_rows", [P, 1], BF16)
        w_all = sb("w_all", [P, 4 * D])
        bias = sb("bias", [P, 4 * D])
        comp = e_sb[:, 6:8, :].rearrange("p a (b d) -> p (a b) d", d=D)
        bcol = sb("bcol", [P, 1])
        ones = sb("ones", [P, P])
        ident_b = sb("ident_b", [P, P], BF16)
        lr_t = parts[:, :, :, :].rearrange("p s n d -> p (s n d)").bitcast(F32)[0:DL + 1, 0:NT * P]
        gm = sb("gm", [P, 2, D1])
        lg, hot, hh, h_t = (e_sb[:, 2 * i:2 * i + 2, :] for i in range(4))
        at_t = sb("at_t", [P, 2, P])
        wq_s, wk_s, wv_s, wo_s = (sb(n, [P, D]) for n in ("wq_s", "wk_s", "wv_s", "wo_s"))
        lq_s, lk_s, lv_s, lvt_s = (sb(n, [P, D]) for n in ("lq_s", "lk_s", "lv_s", "lvt_s"))
        col_s = sb("col_s", [P, len(COLS)])
        lnc_s, lnd_s, bo_s, b2_s = (sb(n, [P, D]) for n in ("lnc_s", "lnd_s", "bo_s", "b2_s"))
        wkd = sb("wkd", [P, D])
        m1_s = sb("m1_s", [P, DL])
        m2_s = sb("m2_s", [DL + 1, F])
        w1_s = sb("w1_s", [P, F])
        w2_s = sb("w2_s", [P, FT, D])
        id_s, blk_s, cen_s = (sb(n, [P, P]) for n in ("id_s", "blk_s", "cen_s"))
        slot_s = sb("slot_s", [P, D2])
        pos_s = sb("pos_s", [P, QT])
        par_s = sb("par_s", [P, 2])

        q_scr = nc.dram_tensor("q_scr", [B, 3, D, T], BF16, kind="Internal").ap()
        k_scr = nc.dram_tensor("k_scr", [B, 2, 3, D, T], BF16, kind="Internal").ap()

        s1 = psum("s1", [P, 4, 512])
        st = psum("st", [P, 2, 512])
        po = psum("po", [P, 512])
        px = psum("px", [P, 512])
        px_b = px[:, :].bitcast(BF16)

        col = {n: col_s[:, i:i + 1] for i, n in enumerate(COLS)}

        consts_in = sem("consts_in")
        x_in = sem("x_in")
        dve_step, pool_step, act_step = sem("dve_step"), sem("pool_step"), sem("act_step")
        ready = sem("ready")
        pe_prep = sem("pe_prep")
        act_prep = sem("act_prep")
        pe_proj = sem("pe_proj")
        xt_full, xt_copied = sem("xt_full"), sem("xt_copied")
        zt_copied = sem("zt_copied")
        pj_full, pj_q, pj_v = sem("pj_full"), sem("pj_q"), sem("pj_v")
        kt_full, kt_copied, kt_stored, k_loaded = sem("kt_full"), sem("kt_copied"), sem("kt_stored"), sem("k_loaded")
        qt_full, qt_copied = sem("qt_full"), sem("qt_copied")
        q_stored = [sem(f"q_stored{i}") for i in range(2)]
        key_rows = sem("key_rows")
        q_loaded = [sem(f"q_loaded{i}") for i in range(QB)]
        m_loaded = [sem(f"m_loaded{i}") for i in range(QB)]
        window_ready = sem("window_ready")
        s1_full, max_taken = sem("s1_full"), sem("max_taken")
        mp_ready, mt_full, mt_copied = sem("mp_ready"), sem("mt_full"), sem("mt_copied")
        st_full, exp_done = sem("st_full"), sem("exp_done")
        pv_done, o_copied = sem("pv_done"), sem("o_copied")
        tt_full, tt_copied = sem("tt_full"), sem("tt_copied")
        rden_ready, pool_out, pool_sq, var_ready, parts_ready = (
            sem(n) for n in ("rden_ready", "pool_out", "pool_sq", "var_ready", "parts_ready"))
        diff_ready, diff_full = sem("diff_ready"), sem("diff_full")
        lr_full, lr_copied = sem("lr_full"), sem("lr_copied")
        lg_full, lg_copied, gm_ready, hot_pre, gm2_ready, hot_ready = (
            sem(n) for n in ("lg_full", "lg_copied", "gm_ready", "hot_pre", "gm2_ready", "hot_ready"))
        mid_full, h_ready, ht_full, ht_copied, res_full, res_copied, gate_ready, gate_exp = (
            sem(n) for n in ("mid_full", "h_ready", "ht_full", "ht_copied", "res_full", "res_copied", "gate_ready",
                             "gate_exp"))
        at_full, at_copied, s_full, y_ready, y_stored = (
            sem(n) for n in ("at_full", "at_copied", "s_full", "y_ready", "y_stored"))

        block = ctx.enter_context(nc.Block())

        loads = [(wq_s[:, :], wq), (wk_s[:, :], wk), (wv_s[:, :], wv), (wo_s[:, :], wo_t), (lq_s[:, :], lq),
                 (lk_s[:, :], lk), (lv_s[:, :], lv), (lvt_s[:, :], lv_t), (col_s[:, :], cols),
                 (lnc_s[:, :], lnc), (lnd_s[:, :], lnd), (bo_s[:, :], bo), (m1_s[:, :], m1),
                 (m2_s[0:DL, :], m2), (m2_s[DL:DL + 1, :], mb), (w1_s[:, :], w1),
                 (w2_s[:, :, :], w2), (b2_s[:, :], b2), (id_s[:, :], ident), (blk_s[:, :], blocks),
                 (cen_s[:, :], centre), (slot_s[:, :], slots), (pos_s[:, :], token_pos), (par_s[:, :], parity)]

        def misc_order():
            order = [("m", 0)]
            for n in range(UNITS):
                b = n // 2
                for c in range(CHUNKS):
                    order += in_body(n, c)
            return order + [("t", QT * (B - 1)), ("t", QT * (B - 1) + 1), ("q", B - 2), ("q", B - 1)]

        def in_body(n, c):
            b = n // 2
            found = []
            if c == 0 and n % 2 == 1 and b >= 2:
                found.append(("q", b - 2))
            if c == 1 and n + 1 < UNITS:
                found.append(("m", n + 1))
            if n % 2 == 0 and b >= 1 and c >= 2:
                found.append(("t", QT * (b - 1) + c - 2))
            return found

        ORDER = misc_order()
        COPIED = {"m": (mt_copied, UNITS), "t": (tt_copied, NT), "q": (qt_copied, B)}

        @block.sync
        def _(sp):
            sp.dma_start(x_sb[:, :, :], x.rearrange("(n p) d -> p n d", p=P)).then_inc(x_in, 16)
            for dst, src in loads:
                sp.dma_start(dst, src).then_inc(consts_in, 16)
            sp.dma_start(k_res[WIN_ROW:STACK, :, :], key_side).then_inc(key_rows, 16)
            for b in range(B):
                sp.wait_ge(kt_copied, 2 * (b + 1))
                sp.dma_start(k_scr[b].rearrange("e s d t -> d e s t"), tp[:, :, :, :]).then_inc(kt_stored, 16)
                sp.wait_ge(kt_stored, 16 * (b + 1))
                for e in range(2):
                    dst = k_res[0:WIN_ROW, b, :].rearrange("r (p e t) -> r p e t", e=2, t=T)[:, :, e, :]
                    for first, count, _ in BANDS:
                        for j in range(first, first + count):
                            sp.dma_start(
                                dst[j * PAIR:(j + 1) * PAIR],
                                k_scr[b, e, K_PARTS[j]].rearrange("(p r) t -> r p t", r=PAIR),
                            ).then_inc(k_loaded, 16)

            def store_q(b, count):
                sp.wait_ge(qt_copied, count)
                sp.dma_start(q_scr[b].rearrange("s d t -> d s t"), tp[:, b % 2, :, :]).then_inc(q_stored[b % 2], 16)

            for b in range(B):
                store_q(b, b + 1)

            def load_q(it, n):
                b, half = n // 2, n % 2
                if n >= QB:
                    sp.wait_ge(st_full, it * UNITS * UH + (n - QB + 1) * UH)
                for j, part in enumerate(Q_PARTS):
                    src = q_scr[b, part, half * D // 2:(half + 1) * D // 2, :]
                    sp.dma_start(
                        q_st[j * PAIR:(j + 1) * PAIR, n % QB, :].rearrange("r (p t) -> r p t", t=T),
                        src.rearrange("(p r) t -> r p t", r=PAIR),
                    ).then_inc(q_loaded[n % QB], 16)

            def load_max(it, n):
                sp.wait_ge(mt_copied, it * UNITS + n + 1)
                for p in range(UH // 2):
                    sp.dma_start(q_st[MAX_ROW:STACK, n % QB, p * T:(p + 1) * T],
                                 m_t[6 * p:6 * p + 6, n % 2, :]).then_inc(m_loaded[n % QB], 16)

            with sp.Fori(0, ITERS) as it:
                stored = 16 * (it * (B // 2) + B // 2)
                sp.wait_ge(q_stored[0], stored)
                sp.wait_ge(q_stored[1], stored)
                for n in range(QB):
                    load_q(it, n)
                load_max(it, 0)
                for n in range(UNITS):
                    if n + 1 < UNITS:
                        load_max(it, n + 1)
                    for kind, b in in_body(n, 0):
                        if kind == "q":
                            store_q(b, B + it * B + b + 1)
                    if n + QB < UNITS:
                        load_q(it, n + QB)
                store_q(B - 2, B + it * B + B - 1)
                store_q(B - 1, B + it * B + B)
            for t in range(NT):
                sp.wait_ge(y_ready, t + 1)
                sp.dma_start(out[t * P:(t + 1) * P, :], work[:, t, :]).then_inc(y_stored, 16)
            sp.wait_ge(y_stored, 16 * NT)
            for i in range(2):
                sp.wait_ge(q_stored[i], 16 * B // 2 * (ITERS + 1))

        def rsqrt(eng, steps, v, yy, t):
            steps.done(eng.tensor_scalar(yy.bitcast(I32), v.bitcast(I32), 1, None, ALU.arith_shift_right))
            steps.wait()
            steps.done(eng.tensor_scalar(yy.bitcast(I32), yy.bitcast(I32), -1.0, float(RSQRT_SEED), ALU.mult, ALU.add))
            steps.done(eng.tensor_scalar(v, v, -0.5, None, ALU.mult))
            for _ in range(3):
                steps.wait()
                steps.done(eng.tensor_tensor(t, yy, yy, ALU.mult))
                steps.wait()
                steps.done(eng.tensor_tensor(t, t, v, ALU.mult))
                steps.wait()
                steps.done(eng.scalar_tensor_tensor(yy, t, 1.5, yy, ALU.add, ALU.mult))
            steps.wait()

        C_DIFF, C_RHS, C_CONV, C_DONE, C_GATE, C_UP, C_DOWN, C_IS, C_CW, C_T, C_PEN, C_DU, C_DD = range(13)

        def c(i):
            return ctl[:, i:i + 1]

        @block.vector
        def _(dve):
            steps = Steps(dve, dve_step)
            dve.memset(ones[:, :], 1.0)
            dve.memset(zero_rows[:, :], 0.0)
            dve.memset(v_res[:, :, :, :], 1.0)
            dve.memset(po[:, :], 0.0)
            dve.memset(c(C_GATE), 0.0)
            dve.memset(c(C_DONE), 0.0)
            dve.memset(c(C_CW), float(CW0))
            dve.memset(rowmask[:, :], 1.0)
            dve.memset(notdone[:, :], 1)
            steps.done(dve.memset(q_st[WIN_ROW:, :, :], 0.0))
            steps.wait()
            dve.wait_ge(consts_in, 16 * len(loads))
            steps.done(dve.tensor_copy(ident_b[:, :], id_s[:, :]))
            for i, w in enumerate((lq_s, lk_s, lv_s, lvt_s)):
                steps.done(dve.tensor_tensor(comp[:, i, :], w[:, :], blk_s[:, :], ALU.mult))
            steps.done(dve.tensor_scalar(bcol[:, :], col["bq"], QK_SCALE, None, ALU.mult))
            steps.done(dve.scalar_tensor_tensor(wkd[:, :], lnc_s[:, :], INV_SQRT_E, lnd_s[:, :], ALU.mult, ALU.mult))
            steps.done(dve.tensor_copy(temps[:, 0:1], col["temp"]))
            for i in range(ITERS):
                steps.wait()
                steps.done(dve.tensor_scalar(temps[:, i + 1:i + 2], temps[:, i:i + 1], TEMP_STEP, None, ALU.add))
            steps.wait()
            steps.done(dve.tensor_scalar(tsv[:, :], temps[:, :], 0.0, None, ALU.is_gt))
            steps.wait()
            steps.done(dve.tensor_tensor(temps[:, :], temps[:, :], tsv[:, :], ALU.mult))
            steps.done(dve.tensor_scalar(tst[:, :], tsv[:, :], -1.0, 1.0, ALU.mult, ALU.add))
            steps.wait()
            steps.done(dve.tensor_tensor(tsv[:, :], temps[:, :], tst[:, :], ALU.add))
            steps.wait()
            rsqrt(dve, steps, tsv[:, :], tsc[:, :], tst[:, :])
            steps.done(dve.tensor_copy(tsc_now[:, :], tsc[:, 0:1]))
            steps.wait()
            dve.memset(dsum[:, :], 0.0).then_inc(ready, 1)
            dve.wait_ge(pe_prep, 1)
            dve.tensor_copy(comp[:, 4:6, :], s1[:, 0, 0:2 * D].rearrange("p (a d) -> p a d", a=2)).then_inc(ready, 1)
            dve.wait_ge(pe_prep, 2)
            dve.tensor_copy(comp[:, 7, :], s1[:, 1, 0:D]).then_inc(ready, 1)
            dve.wait_ge(pe_prep, 3)
            steps.done(dve.tensor_scalar(w_all[:, 0:D], s1[:, 2, 0:D], col["lna"], QK_SCALE, ALU.mult, ALU.mult))
            steps.done(dve.tensor_scalar(w_all[:, D:2 * D], s1[:, 2, D:2 * D], col["lnb"], QK_SCALE, ALU.mult, ALU.mult))
            steps.done(dve.tensor_scalar(w_all[:, 2 * D:], s1[:, 2, 2 * D:], col["lnb"], None, ALU.mult))
            steps.done(dve.tensor_copy(bias[0:1, :], s1[0:1, 3, :]))
            steps.wait()
            dve.wait_ge(x_in, 16)

            def layer_norm(dst, src):
                for t in range(NT):
                    last = dve.bn_stats(stat[:, t, :], src[:, t, :])
                steps.done(last)
                steps.wait()
                for t in range(NT):
                    last = dve.bn_aggr(mv[:, t, :], stat[:, t, :])
                steps.done(last)
                steps.wait()
                steps.done(dve.tensor_scalar(var[:, 0:NT], mv[:, :, 1], EPS, None, ALU.add))
                steps.wait()
                rsqrt(dve, steps, var[:, 0:NT], y[:, 0:NT], tmp[:, 0:NT])
                for t in range(NT):
                    last = dve.tensor_scalar(dst[:, t, :], src[:, t, :], mv[:, t, 0:1], y[:, t:t + 1],
                                             ALU.subtract, ALU.mult)
                steps.done(last)
                steps.wait()

            layer_norm(xn, x_sb)
            layer_norm(z, xn)
            dve.memset(bcol[:, :], 0.0).then_inc(ready, 1)
            for t in range(NT):
                dve.wait_ge(pj_full, t + 1)
                v_part = s1[:, t % 2, 2 * D:].rearrange("p (a h e) -> p h a e", a=2, h=H)
                dve.tensor_copy(v_res[:, t, :, 0:2 * HD].rearrange("p h (a e) -> p h a e", a=2), v_part)\
                   .then_inc(pj_v, 1)
            dve.wait_ge(pj_q, 2 * NT)

            def head_norm(src, scale_by, parts_to):
                steps.done(dve.tensor_tensor(work[:, :, :], src[:, :, :], src[:, :, :], ALU.mult))
                steps.wait()
                steps.done(dve.tensor_reduce(var[:, :], work[:, :, :].rearrange("p n (h e) -> p (n h) e", h=H),
                                             AX_X, ALU.add))
                steps.wait()
                steps.done(dve.tensor_scalar(var[:, :], var[:, :], 1.0 / HD, EPS, ALU.mult, ALU.add))
                steps.wait()
                rsqrt(dve, steps, var[:, :], y[:, :], tmp[:, :])
                if scale_by is None:
                    steps.done(dve.tensor_scalar(y[:, :], y[:, :], tsc_now[:, 0:1], None, ALU.mult))
                    steps.wait()
                steps.done(dve.tensor_tensor(
                    work[:, :, :].rearrange("p n (h e) -> p (n h) e", h=H),
                    src[:, :, :].rearrange("p n (h e) -> p (n h) e", h=H),
                    y[:, :].unsqueeze(2).to_broadcast([P, NT * H, HD]), ALU.mult))
                steps.wait()
                if scale_by is not None:
                    steps.done(dve.tensor_tensor(work[:, :, :], work[:, :, :],
                                                 scale_by[:, :].unsqueeze(1).to_broadcast([P, NT, D]), ALU.mult))
                    steps.wait()
                for i in range(3):
                    steps.done(dve.tensor_copy(parts_to[:, i, :, :], work[:, :, :]))
                    steps.wait()
                    if i < 2:
                        steps.done(dve.tensor_tensor(work[:, :, :], work[:, :, :], parts_to[:, i, :, :], ALU.subtract))
                        steps.wait()

            head_norm(kc, wkd, parts)
            dve.memset(bcol[:, :], 0.0).then_inc(ready, 1)
            for b in range(B):
                dve.wait_ge(kt_full, b + 1)
                if b >= 1:
                    dve.wait_ge(kt_stored, 16 * b)
                for e in range(2):
                    dve.tensor_scalar(tp[:, e, :, :], px_b[:, 0:3 * T].rearrange("p (s t) -> p s t", s=3),
                                      par_s[:, e:e + 1], None, ALU.mult).then_inc(kt_copied, 1)
            head_norm(qc, None, parts)
            dve.memset(bcol[:, :], 0.0).then_inc(ready, 1)

            def copy_q(b, full, stored):
                dve.wait_ge(qt_full, full)
                if stored is not None:
                    dve.wait_ge(q_stored[b % 2], stored)
                dve.tensor_copy(tp[:, b % 2, :, :], px_b[:, 0:3 * T].rearrange("p (s t) -> p s t", s=3))\
                   .then_inc(qt_copied, 1)

            dve.wait_ge(kt_stored, 16 * B)
            for b in range(B):
                copy_q(b, b + 1, 16 * (b // 2) if b >= 2 else None)
            steps.done(dve.memset(lr_t[DL:DL + 1, :], 1.0))
            steps.wait()
            dve.memset(bcol[:, :], 0.0).then_inc(window_ready, 1)

            for t in range(NT):
                dve.wait_ge(lg_copied, t + 1)
                blockwise = lg[:, t % 2, :].rearrange("p (j q) -> p j q", j=D1)
                steps.done(dve.tensor_reduce(gm[:, t % 2, :], blockwise, AX_X, ALU.max))
                steps.wait()
                steps.done(dve.tensor_tensor(hot[:, t % 2, :].rearrange("p (j q) -> p j q", j=D1), blockwise,
                                             gm[:, t % 2, :].unsqueeze(2).to_broadcast([P, D1, D2]), ALU.is_equal))
                steps.wait()
                marked = hot[:, t % 2, :].rearrange("p (j q) -> p j q", j=D1)
                steps.done(dve.tensor_tensor(marked, marked, slot_s[:, :].unsqueeze(1).to_broadcast([P, D1, D2]),
                                             ALU.mult))
                steps.wait()
                steps.done(dve.tensor_reduce(gm[:, t % 2, :], marked, AX_X, ALU.max))
                steps.wait()
                steps.done(dve.tensor_tensor(marked, marked, gm[:, t % 2, :].unsqueeze(2).to_broadcast([P, D1, D2]),
                                             ALU.is_equal))
                steps.wait()
                dve.wait_ge(mid_full, t + 1)
                if t >= 2:
                    dve.wait_ge(ht_full, t - 1)
                dve.scalar_tensor_tensor(hh[:, t % 2, :], s1[:, 2 + t % 2, :], 0.0, hot[:, t % 2, :],
                                         ALU.max, ALU.mult).then_inc(h_ready, 1)
                dve.wait_ge(res_full, t + 1)
                dve.tensor_tensor(work[:, t, :], s1[:, t % 2, 0:D], b2_s[:, :], ALU.add).then_inc(res_copied, 1)
            for t in range(NT):
                dve.wait_ge(gate_exp, t + 1)
            steps.done(dve.tensor_scalar(gate[:, :, :], gate[:, :, :], 1.0, None, ALU.add))
            steps.wait()
            steps.done(dve.reciprocal(gate[:, :, :], gate[:, :, :]))
            steps.wait()
            dve.tensor_tensor(gate[:, :, :], gate[:, :, :], work[:, :, :], ALU.mult).then_inc(gate_ready, 1)

            steps.done(dve.memset(attn[:, :, :], 0.0))
            steps.wait()
            before = steps.n
            with dve.Fori(0, ITERS) as it:
                rnd = Steps(dve, dve_step, before + it * VECTOR_STEPS)

                def maxima(n, cc):
                    i = n * CHUNKS + cc
                    dve.wait_ge(s1_full, it * UNITS * CHUNKS + i + 1)
                    if cc == 0:
                        if n >= 2:
                            dve.wait_ge(mp_ready, it * UNITS + n - 1)
                    dve.tensor_reduce(
                        mx[:, n % 2, :, CH * cc:CH * cc + CH].rearrange("p q h -> p h q"),
                        s1[:, 2 * (i % 2):2 * (i % 2) + 2, :].rearrange("p h (q k) -> p h q k", q=QT),
                        AX_X, ALU.max).then_inc(max_taken, 1)

                def split_max(n):
                    m, r, w = mx[:, n % 2], mr[:, n % 2], mp[:, n % 2]
                    dve.wait_ge(max_taken, it * UNITS * CHUNKS + (n + 1) * CHUNKS)
                    if n >= 2:
                        dve.wait_ge(mt_full, it * UNITS + n - 1)
                    rnd.done(dve.tensor_scalar(w[:, :, :, 0], m, -1.0, None, ALU.mult))
                    rnd.wait()
                    rnd.done(dve.scalar_tensor_tensor(r, m, -1.0, w[:, :, :, 0], ALU.mult, ALU.subtract))
                    rnd.wait()
                    rnd.done(dve.tensor_copy(w[:, :, :, 1], r))
                    rnd.wait()
                    dve.tensor_tensor(w[:, :, :, 2], r, w[:, :, :, 1], ALU.subtract).then_inc(mp_ready, 1)

                def inverse_sums(b):
                    dve.wait_ge(tt_copied, it * NT + QT * (b + 1))
                    rnd.done(dve.reciprocal(rden[:, :, :], tt[:, :, :, VC - 1]))
                    rnd.wait()
                    for q in range(QT):
                        last = dve.tensor_scalar(rden[:, q, :], rden[:, q, :], rowmask[:, q:q + 1], None, ALU.mult)
                    last.then_inc(rden_ready, 1)

                def variance(b):
                    dve.wait_ge(pool_sq, it * B + b + 1)
                    rnd.done(dve.tensor_reduce(tvar[:, :], r_new[:, :, :].rearrange("p q (h e) -> p (q h) e", h=H),
                                               AX_X, ALU.add))
                    rnd.wait()
                    rnd.done(dve.tensor_scalar(tvar[:, :], tvar[:, :], 1.0 / HD, EPS, ALU.mult, ALU.add))
                    rnd.wait()
                    rsqrt(dve, rnd, tvar[:, :], ty[:, :], ttmp[:, :])
                    dve.tensor_scalar(ty[:, :], ty[:, :], tsc_now[:, 0:1], None, ALU.mult).then_inc(var_ready, 1)

                def difference(b):
                    dve.wait_ge(pool_out, it * B + b + 1)
                    rnd.done(dve.tensor_reduce(dsum[:, b:b + 1], d_new[:, :, :].rearrange("p q d -> p (q d)"), AX_X,
                                               ALU.add, apply_absolute_value=True))
                    rnd.done(dve.copy_predicated(attn[:, QT * b:QT * b + QT, :].rearrange("p q d -> p (q d)"),
                                                 notdone[:, 0:1].to_broadcast([P, QT * D]),
                                                 o_new[:, :, :].rearrange("p q d -> p (q d)")))
                    dve.wait_ge(dve_step, rnd.base + rnd.n)
                    dve.memset(bcol[:, :], 0.0).then_inc(diff_ready, 1)

                rnd.done(dve.tensor_copy(tsc_now[:, :], tsc[:, bass.ds(it + 1, 1)]))
                rnd.wait()
                for n in range(2):
                    for cc in range(CHUNKS):
                        maxima(n, cc)
                    split_max(n)
                for n in range(UNITS):
                    b = n // 2
                    for cc in range(CHUNKS):
                        if n + 2 < UNITS:
                            maxima(n + 2, cc)
                        if n % 2 == 1 and b >= 1:
                            if cc == 0:
                                inverse_sums(b - 1)
                            if cc == 3:
                                variance(b - 1)
                            if cc == 1 and b >= 2:
                                copy_q(b - 2, B + it * B + b - 1, 16 * (it * (B // 2) + (B + b - 2) // 2))
                        if n % 2 == 0 and b >= 2 and cc == 1:
                            difference(b - 2)
                    if n + 2 < UNITS:
                        split_max(n + 2)
                difference(B - 2)
                copy_q(B - 2, B + it * B + B - 1, 16 * (it * (B // 2) + (2 * B - 2) // 2))
                inverse_sums(B - 1)
                variance(B - 1)
                difference(B - 1)
                copy_q(B - 1, B + it * B + B, 16 * (it * (B // 2) + (2 * B - 1) // 2))
                rnd.done(dve.tensor_reduce(dall[:, :], dsum[:, :], AX_X, ALU.add))
                rnd.wait()
                dve.memset(bcol[:, :], 0.0).then_inc(diff_ready, 1)
                dve.wait_ge(diff_full, it + 1)
                rnd.done(dve.tensor_scalar(c(C_DIFF), px[:, 0:1], 1.0 / (B * T * D), None, ALU.mult))
                rnd.done(dve.tensor_scalar(c(C_IS), c(C_CW), float(T), None, ALU.is_lt))
                rnd.wait()
                rnd.done(dve.tensor_scalar(c(C_RHS), c(C_DIFF), col["fac"], col["thr"], ALU.mult, ALU.add))
                rnd.done(dve.tensor_scalar(c(C_UP), c(C_DIFF), UP_DIFF, float(CW_DOWN_UP - CW_DOWN),
                                           ALU.is_gt, ALU.mult))
                rnd.done(dve.tensor_scalar(c(C_DOWN), c(C_DIFF), DOWN_DIFF, None, ALU.is_lt))
                rnd.done(dve.tensor_scalar(c(C_DD), c(C_IS), float((CW_DOWN_DOWN - CW_DOWN) - (CW_DOWN - CW0)),
                                           float(CW_DOWN - CW0), ALU.mult, ALU.add))
                rnd.wait()
                rnd.done(dve.tensor_tensor(c(C_CONV), c(C_DIFF), c(C_RHS), ALU.is_lt))
                rnd.done(dve.scalar_tensor_tensor(c(C_CW), c(C_UP), c(C_IS), c(C_CW), ALU.mult, ALU.add))
                rnd.wait()
                rnd.done(dve.scalar_tensor_tensor(c(C_DONE), c(C_CONV), c(C_GATE), c(C_DONE), ALU.mult, ALU.max))
                rnd.done(dve.scalar_tensor_tensor(c(C_CW), c(C_DOWN), c(C_DD), c(C_CW), ALU.mult, ALU.add))
                rnd.wait()
                rnd.done(dve.memset(c(C_GATE), 1.0))
                rnd.done(dve.tensor_scalar(notdone[:, :], c(C_DONE), 0.0, None, ALU.is_equal))
                rnd.done(dve.tensor_scalar(rowmask[:, :], pos_s[:, :], c(C_CW), None, ALU.is_lt))
                rnd.done(dve.tensor_scalar(c(C_PEN), col["level"], c(C_CW), PENALTY, ALU.is_ge, ALU.mult))
                rnd.wait()
                for i in range(QB):
                    last = dve.tensor_scalar(q_st[WIN_ROW:MAX_ROW, i, :], zero_rows[WIN_ROW:MAX_ROW, :].to_broadcast([len(LEVELS), UH // 2 * T]),
                                             ctl[WIN_ROW:MAX_ROW, C_PEN:C_PEN + 1], None, ALU.add)
                last.then_inc(window_ready, 1)
                assert rnd.n == VECTOR_STEPS, rnd.n

            total = before + ITERS * VECTOR_STEPS
            for t in range(NT):
                dve.wait_ge(s_full, t + 1)
                out_steps = Steps(dve, dve_step, total)
                out_steps.done(dve.tensor_tensor(work[:, t, :], s1[:, t % 2, 0:D], bo_s[:, :], ALU.add))
                out_steps.wait()
                out_steps.done(dve.tensor_tensor(work[:, t, :], work[:, t, :], gate[:, t, :], ALU.mult))
                out_steps.wait()
                dve.tensor_tensor(work[:, t, :], work[:, t, :], x_sb[:, t, :], ALU.add).then_inc(y_ready, 1)
                total += 2

        @block.gpsimd
        def _(pool):
            with pool.Fori(0, ITERS) as it:
                rnd = Steps(pool, pool_step, it * POOL_STEPS)
                for b in range(B):
                    tiles = slice(QT * b, QT * b + QT)
                    heads = "p q (h e) -> p q h e"
                    pool.wait_ge(rden_ready, it * B + b + 1)
                    if b >= 1:
                        pool.wait_ge(diff_ready, it * (B + 1) + b)
                    over = rden[:, :, :].unsqueeze(3).to_broadcast([P, QT, H, HD])
                    rnd.done(pool.tensor_tensor(r_new[:, :, :].rearrange(heads, h=H), tt[:, :, :, HD:2 * HD], over,
                                                ALU.mult))
                    rnd.done(pool.tensor_tensor(o_new[:, :, :].rearrange(heads, h=H), tt[:, :, :, 0:HD], over,
                                                ALU.mult))
                    rnd.wait()
                    rnd.done(pool.tensor_tensor(qc[:, tiles, :], qc[:, tiles, :], r_new[:, :, :], ALU.add))
                    rnd.wait()
                    pool.tensor_tensor(r_new[:, :, :], qc[:, tiles, :], qc[:, tiles, :], ALU.mult).then_inc(pool_sq, 1)
                    pool.tensor_tensor(d_new[:, :, :], o_new[:, :, :], attn[:, tiles, :], ALU.subtract)\
                        .then_inc(pool_out, 1)
                    pool.wait_ge(var_ready, it * B + b + 1)
                    rnd.done(pool.tensor_tensor(
                        q_n[:, :, :].rearrange(heads, h=H), qc[:, tiles, :].rearrange(heads, h=H),
                        ty[:, :].rearrange("p (q h) -> p q h", q=QT).unsqueeze(3).to_broadcast([P, QT, H, HD]),
                        ALU.mult))
                    rnd.wait()
                    pool.wait_ge(qt_full, B + it * B + b)
                    for i in range(2):
                        rnd.done(pool.tensor_tensor(pt[:, i, :, :], q_n[:, :, :],
                                                    zero_rows[:, :].unsqueeze(2).to_broadcast([P, QT, D]), ALU.add))
                        rnd.wait()
                        if i == 0:
                            rnd.done(pool.tensor_tensor(q_n[:, :, :], q_n[:, :, :], pt[:, i, :, :], ALU.subtract))
                            rnd.wait()
                    pool.tensor_tensor(pt[:, 2, :, :], q_n[:, :, :], pt[:, 1, :, :], ALU.subtract)\
                        .then_inc(parts_ready, 1)
                assert rnd.n == POOL_STEPS, rnd.n

        @block.scalar
        def _(act):
            for t in range(NT):
                act.wait_ge(xt_full, t + 1)
                if t >= 2:
                    act.wait_ge(pj_full, t - 1)
                act.activation(z_t[:, t % 2, :], px[:, P:2 * P], ACT.Copy).then_inc(zt_copied, 1)
                act.activation(xn_t[:, t * P:(t + 1) * P], px[:, 0:P], ACT.Copy).then_inc(xt_copied, 1)
                act.wait_ge(pj_full, t + 1)
                act.wait_ge(pj_v, t + 1)
                act.activation(qc[:, t, :], s1[:, t % 2, 0:D], ACT.Copy).then_inc(pj_q, 1)
                act.activation(kc[:, t, :], s1[:, t % 2, D:2 * D], ACT.Copy).then_inc(pj_q, 1)
            for i in range(NT * P // 512):
                act.wait_ge(lr_full, i + 1)
                act.activation(lr_t[0:DL, 512 * i:512 * i + 512], s1[0:DL, i, :], ACT.Copy).then_inc(lr_copied, 1)
            for t in range(NT):
                act.wait_ge(lg_full, t + 1)
                if t >= 2:
                    act.wait_ge(h_ready, t - 1)
                act.activation(lg[:, t % 2, :], st[:, t % 2, :], ACT.Copy).then_inc(lg_copied, 1)
                act.wait_ge(ht_full, t + 1)
                act.activation(h_t[:, t % 2, :], px[:, :], ACT.Copy).then_inc(ht_copied, 1)
                act.wait_ge(res_copied, t + 1)
                act.activation(gate[:, t, :], work[:, t, :], ACT.Exp, scale=-1.0).then_inc(gate_exp, 1)

            with act.Fori(0, ITERS) as it:
                def copy_max(n):
                    act.wait_ge(mt_full, it * UNITS + n + 1)
                    if n >= 2:
                        act.wait_ge(m_loaded[(n - 2) % QB], 16 * (UH // 2) * (it * (UNITS // QB) + (n - 2) // QB + 1))
                    act.activation(m_t[0:3 * UH, n % 2, :], px_b[0:3 * UH, 0:T], ACT.Copy).then_inc(mt_copied, 1)

                def copy_outputs(n):
                    act.wait_ge(pv_done, it * 2 * UNITS + 2 * (n + 1))
                    if n >= 2:
                        act.wait_ge(tt_full, it * NT + QT * (n // 2))
                    act.activation(o_t[:, n % 2, :], po[:, :], ACT.Copy).then_inc(o_copied, 1)

                def copy_tokens(t):
                    act.wait_ge(tt_full, it * NT + t + 1)
                    if t % QT == 0 and t:
                        act.wait_ge(pool_sq, it * B + t // QT)
                        act.wait_ge(pool_out, it * B + t // QT)
                    act.activation(tt[:, t % QT, :, :],
                                   px[:, :].rearrange("p (h r) -> p h r", h=H)[:, :, 0:VC], ACT.Copy)\
                       .then_inc(tt_copied, 1)

                copy_max(0)
                for n in range(UNITS):
                    for cc in range(CHUNKS):
                        for h in (2 * cc, 2 * cc + 1):
                            i = n * UH + h
                            act.wait_ge(st_full, it * UNITS * UH + i + 1)
                            if i >= EB and h % GH == 0:
                                act.wait_ge(pv_done, it * 2 * UNITS + (i - EB) // GH + 1)
                            act.activation(e_sb[:, i % EB, :], st[:, i % 2, :], ACT.Exp).then_inc(exp_done, 1)
                        if cc == 1 and n >= 1:
                            copy_outputs(n - 1)
                        for kind, i in in_body(n, cc):
                            if kind == "m":
                                copy_max(i)
                            if kind == "t":
                                copy_tokens(i)
                copy_outputs(UNITS - 1)
                copy_tokens(NT - 2)
                copy_tokens(NT - 1)
            for t in range(NT):
                act.wait_ge(at_full, t + 1)
                if t >= 2:
                    act.wait_ge(s_full, t - 1)
                act.activation(at_t[:, t % 2, :], px[:, 0:P], ACT.Copy).then_inc(at_copied, 1)

        @block.tensor
        def _(pe):
            def mm(out_, l, r, start=True, stop=True):
                return pe.matmul(out_, l, r, start=start, stop=stop)

            bdq, bdk, bdv, bv_t, bq_c, bk_c, _, bvq = (comp[:, i, :] for i in range(8))
            pe.wait_ge(ready, 1)
            mm(s1[:, 0, 0:D], bdq, cen_s[:, :])
            mm(s1[:, 0, D:2 * D], bdk, cen_s[:, :]).then_inc(pe_prep, 1)
            pe.wait_ge(ready, 2)
            mm(s1[:, 1, 0:D], bdv, bq_c).then_inc(pe_prep, 1)
            pe.wait_ge(ready, 3)
            mm(s1[:, 2, 0:D], wq_s[:, :], bq_c)
            mm(s1[:, 2, D:2 * D], wk_s[:, :], bk_c)
            mm(s1[:, 2, 2 * D:3 * D], wv_s[:, :], bv_t)
            mm(s1[:, 2, 3 * D:4 * D], wv_s[:, :], bvq)
            mm(s1[0:1, 3, 0:D], bcol[:, :], bq_c, stop=False)
            mm(s1[0:1, 3, 0:D], col["lqb"], cen_s[:, :], start=False)
            mm(s1[0:1, 3, D:2 * D], col["lkb"], cen_s[:, :])
            mm(s1[0:1, 3, 2 * D:3 * D], col["bv"], bv_t, stop=False)
            mm(s1[0:1, 3, 2 * D:3 * D], col["lvb"], id_s[:, :], start=False)
            mm(s1[0:1, 3, 3 * D:4 * D], col["bv"], bvq, stop=False)
            mm(s1[0:1, 3, 3 * D:4 * D], col["lvb"], bq_c, start=False).then_inc(pe_prep, 1)
            pe.wait_ge(ready, 4)
            for t in range(NT):
                if t >= 1:
                    pe.wait_ge(xt_copied, t)
                    pe.wait_ge(zt_copied, t)
                pe.transpose(px[:, 0:P], xn[:, t, :], id_s[:, :])
                pe.transpose(px[:, P:2 * P], z[:, t, :], id_s[:, :]).then_inc(xt_full, 1)
                pe.wait_ge(zt_copied, t + 1)
                if t >= 2:
                    pe.wait_ge(pj_q, 2 * (t - 1))
                    pe.wait_ge(pj_v, t - 1)
                mm(s1[:, t % 2, :], z_t[:, t % 2, :], w_all[:, :], stop=False)
                mm(s1[:, t % 2, :], ones[0:1, :], bias[0:1, :], start=False).then_inc(pj_full, 1)

            def by_feature(src, b, full):
                for i in range(3):
                    for q in range(QT):
                        last = pe.transpose(px_b[:, i * T + q * P:i * T + (q + 1) * P],
                                            src(i, q), ident_b[:, :])
                last.then_inc(full, 1)

            pe.wait_ge(ready, 5)
            pe.wait_ge(zt_copied, NT)
            pe.wait_ge(xt_copied, NT)
            for b in range(B):
                if b >= 1:
                    pe.wait_ge(kt_copied, 2 * b)
                by_feature(lambda i, q: parts[:, i, QT * b + q, :], b, kt_full)
            pe.wait_ge(ready, 6)
            pe.wait_ge(kt_copied, 2 * B)
            for b in range(B):
                if b >= 1:
                    pe.wait_ge(qt_copied, b)
                by_feature(lambda i, q: parts[:, i, QT * b + q, :], b, qt_full)

            pe.wait_ge(pj_q, 2 * NT)
            pe.wait_ge(pj_v, NT)
            for i in range(NT * P // 512):
                mm(s1[0:DL, i, :], m1_s[:, :], xn_t[:, 512 * i:512 * i + 512]).then_inc(lr_full, 1)
            pe.wait_ge(lr_copied, NT * P // 512)
            pe.wait_ge(window_ready, 1)
            pe.wait_ge(qt_copied, B)
            for t in range(NT):
                if t >= 2:
                    pe.wait_ge(lg_copied, t - 1)
                    pe.wait_ge(h_ready, t - 1)
                tok = slice(t * P, (t + 1) * P)
                mm(st[:, t % 2, :], lr_t[:, tok], m2_s[:, :]).then_inc(lg_full, 1)
                mm(s1[:, 2 + t % 2, :], xn_t[:, tok], w1_s[:, :]).then_inc(mid_full, 1)
                pe.wait_ge(h_ready, t + 1)
                if t >= 1:
                    pe.wait_ge(ht_copied, t)
                for f in range(FT):
                    last = pe.transpose(px[:, f * P:(f + 1) * P], hh[:, t % 2, f * P:(f + 1) * P], id_s[:, :])
                last.then_inc(ht_full, 1)
                pe.wait_ge(ht_copied, t + 1)
                if t >= 2:
                    pe.wait_ge(res_copied, t - 1)
                for f in range(FT):
                    last = mm(s1[:, t % 2, 0:D], h_t[:, t % 2, f * P:(f + 1) * P], w2_s[:, f, :],
                              start=f == 0, stop=f == FT - 1)
                last.then_inc(res_full, 1)
            pe.wait_ge(h_ready, NT)
            pe.wait_ge(res_copied, NT)
            pe.wait_ge(k_loaded, 16 * 2 * len(K_PARTS) * B)
            pe.wait_ge(key_rows, 16)

            with pe.Fori(0, ITERS) as it:
                def misc_free(kind, i):
                    at = ORDER.index((kind, i))
                    if at:
                        was, j = ORDER[at - 1]
                        s, per = COPIED[was]
                        base = B if was == "q" else 0
                        pe.wait_ge(s, base + it * per + j + 1)
                    else:
                        pe.wait_ge(qt_copied, B + it * B)
                        pe.wait_ge(window_ready, it + 1)

                def scores_by_query(n, cc):
                    i = n * CHUNKS + cc
                    b, buf = n // 2, n % QB
                    if cc == 0:
                        pe.wait_ge(q_loaded[buf], 16 * len(Q_PARTS) * (it * (UNITS // QB) + n // QB + 1))
                    if i >= 2:
                        pe.wait_ge(max_taken, it * UNITS * CHUNKS + i - 1)
                    for hl in range(CH):
                        h = (n % 2) * UH + CH * cc + hl
                        for q in range(QT):
                            last = mm(s1[:, 2 * (i % 2) + hl, q * T:(q + 1) * T],
                                      q_st[0:MAX_ROW, buf, cc * T + q * P:cc * T + (q + 1) * P],
                                      k_res[0:MAX_ROW, b, h * T:(h + 1) * T])
                    last.then_inc(s1_full, 1)

                def scores_by_key(n, hl):
                    i = n * UH + hl
                    b, buf = n // 2, n % QB
                    h = (n % 2) * UH + hl
                    if hl == 0:
                        pe.wait_ge(m_loaded[buf], 16 * (UH // 2) * (it * (UNITS // QB) + n // QB + 1))
                    if i >= 2:
                        pe.wait_ge(exp_done, it * UNITS * UH + i - 1)
                    for k in range(QT):
                        last = mm(st[:, i % 2, k * T:(k + 1) * T],
                                  k_res[0:STACK, b, h * T + k * P:h * T + (k + 1) * P],
                                  q_st[0:STACK, buf, hl // 2 * T:(hl // 2 + 1) * T])
                    last.then_inc(st_full, 1)

                def outputs(g):
                    b, n = g // 4, g // 2
                    pe.wait_ge(exp_done, it * UNITS * UH + GH * (g + 1))
                    if g % 2 == 0 and n >= 1:
                        pe.wait_ge(o_copied, it * UNITS + n)
                    for k in range(QT):
                        for j in range(GH):
                            h = (g % 4) * GH + j
                            last = pe.matmul(po[32 * j:32 * j + VC, (g % 2) * T:(g % 2 + 1) * T],
                                             v_res[:, QT * b + k, h, :],
                                             e_sb[:, (GH * g + j) % EB, k * T:(k + 1) * T],
                                             start=k == 0, stop=k == QT - 1)
                    last.then_inc(pv_done, 1)

                def misc(kind, i):
                    misc_free(kind, i)
                    if kind == "m":
                        pe.wait_ge(mp_ready, it * UNITS + i + 1)
                        for q in range(QT):
                            last = pe.transpose(px_b[0:3 * UH, q * P:(q + 1) * P],
                                                mp[:, i % 2, q, :, :].rearrange("p h s -> p (h s)"), ident_b[:, :])
                        last.then_inc(mt_full, 1)
                    if kind == "t":
                        pe.wait_ge(o_copied, it * UNITS + 2 * (i // QT + 1))
                        for g in range(4):
                            last = pe.transpose(
                                px[:, g * P:(g + 1) * P],
                                o_t[:, g // 2, (g % 2) * T + (i % QT) * P:(g % 2) * T + (i % QT + 1) * P], id_s[:, :])
                        last.then_inc(tt_full, 1)
                    if kind == "q":
                        pe.wait_ge(parts_ready, it * B + i + 1)
                        by_feature(lambda s, q: pt[:, s, q, :], i, qt_full)

                for n in range(2):
                    for cc in range(CHUNKS):
                        if n == 0 and cc == 0:
                            pe.wait_ge(window_ready, it + 1)
                        scores_by_query(n, cc)
                misc("m", 0)
                for n in range(UNITS):
                    for cc in range(CHUNKS):
                        if n + 2 < UNITS:
                            scores_by_query(n + 2, cc)
                        scores_by_key(n, 2 * cc)
                        scores_by_key(n, 2 * cc + 1)
                        if cc == 0 and n >= 1:
                            outputs(2 * n - 1)
                        if cc == 2:
                            outputs(2 * n)
                        for kind, i in in_body(n, cc):
                            misc(kind, i)
                outputs(2 * UNITS - 1)
                for kind, i in ORDER[-4:]:
                    misc(kind, i)
                pe.wait_ge(diff_ready, (it + 1) * (B + 1))
                pe.wait_ge(qt_copied, B + (it + 1) * B)
                mm(px[:, 0:1], ones[:, :], dall[:, :]).then_inc(diff_full, 1)

            pe.wait_ge(window_ready, ITERS + 1)
            for t in range(NT):
                if t >= 1:
                    pe.wait_ge(at_copied, t)
                pe.transpose(px[:, 0:P], attn[:, t, :], id_s[:, :]).then_inc(at_full, 1)
                pe.wait_ge(at_copied, t + 1)
                if t >= 2:
                    pe.wait_ge(y_ready, t - 1)
                mm(s1[:, t % 2, 0:D], at_t[:, t % 2, :], wo_s[:, :]).then_inc(s_full, 1)


VECTOR_STEPS = 200
POOL_STEPS = 56


def kernel(**inputs):
    import concourse.bacc as bacc
    from concourse.bass_utils import run_bass_kernel_spmd

    a = {k.removeprefix("L0_attn_").removeprefix("L0_ffn_"): np.asarray(v) for k, v in inputs.items()}
    f32 = np.float32

    def rows(v):
        return np.ascontiguousarray(np.broadcast_to(v.reshape(1, -1), (P, v.size)))

    def heads(v):
        return np.tile(v, H)

    level = np.zeros(P, f32)
    level[WIN_ROW:MAX_ROW] = LEVELS
    columns = {"bq": a["bq"], "bv": a["bv"], "lna": a["lna_w"], "lnb": a["lnb_w"], "lqb": heads(a["lq_b"]),
               "lkb": heads(a["lk_b"]), "lvb": heads(a["lv_b"]), "level": level}
    for n, k in (("thr", "threshold"), ("temp", "temp_base"), ("fac", "factor")):
        columns[n] = np.broadcast_to(a[k].reshape(1), (P,))
    blocks = np.kron(np.eye(H, dtype=f32), np.ones((HD, HD), f32))
    key_side = np.zeros((STACK - WIN_ROW, B, H, T), f32)
    for i, lv in enumerate(LEVELS):
        key_side[i, :, :, lv:] = 1
    for e in range(2):
        key_side[len(LEVELS) + 3 * e:len(LEVELS) + 3 * e + 3, :, e::2, :] = 1
    import ml_dtypes
    even = (np.arange(D) // HD % 2 == 0).astype(f32)

    arrays = {
        "x": a["x"].reshape(B * T, D), "wq": a["Wq"], "wk": a["Wk"], "wv": a["Wv"], "wo_t": a["Wo"].T,
        "lq": np.tile(a["lq_w"], (H, H)), "lk": np.tile(a["lk_w"], (H, H)), "lv": np.tile(a["lv_w"], (H, H)),
        "lv_t": np.tile(a["lv_w"].T, (H, H)),
        "cols": np.stack([columns[n] for n in COLS], axis=1),
        "lnc": rows(heads(a["lnc_w"])), "lnd": rows(heads(a["lnd_w"])), "bo": rows(a["bo"]),
        "m1": a["m1"], "m2": a["m2"].reshape(DL, F), "mb": a["mb"].reshape(1, F), "w1": a["w1"].reshape(D, F),
        "w2": a["w2"].transpose(1, 0, 2).reshape(FT, P, D).transpose(1, 0, 2), "b2": rows(a["b2"]),
        "ident": np.eye(P, dtype=f32), "blocks": blocks, "centre": np.eye(P, dtype=f32) - blocks / HD,
        "slots": rows(np.arange(D2, 0, -1, dtype=f32)),
        "token_pos": np.arange(T, dtype=f32).reshape(QT, P).T,
        "key_side": key_side.reshape(STACK - WIN_ROW, B, H * T).astype(ml_dtypes.bfloat16),
        "parity": np.stack([even, 1 - even], axis=1),
    }
    arrays = {k: np.ascontiguousarray(v) for k, v in arrays.items()}
    nc = bacc.Bacc("TRN2", target_bir_lowering=False, num_devices=1)
    aps = [nc.dram_tensor(f"in_{n}", v.shape, mybir.dt.from_np(v.dtype), kind="ExternalInput").ap()
           for n, v in arrays.items()]
    out = nc.dram_tensor("out", (B * T, D), F32, kind="ExternalOutput").ap()
    build(nc, *aps, out)
    r = run_bass_kernel_spmd(nc, [{f"in_{n}": v for n, v in arrays.items()}], core_ids=[0])
    return r.results[0]["out"].reshape(B, T, D)
```

```python
from contextlib import ExitStack

import concourse.bass as bass
import numpy as np
from concourse import mybir

F32 = mybir.dt.float32
BF16 = mybir.dt.bfloat16
I32 = mybir.dt.int32
ALU = mybir.AluOpType
ACT = mybir.ActivationFunctionType
AX_X = mybir.AxisListType.X

P = 128
B, T, D = 8, 256, 128
H = 16
HD = D // H
QT = T // P
NT = B * QT
ITERS = 3
MIN_WIN, MAX_WIN = 64, 256
EPS = 1e-5
QK_SCALE = float(HD) ** -0.25
INV_SQRT_E = float(np.float32(1.0 / np.sqrt(HD)))
UP_DIFF, DOWN_DIFF = 0.05, 0.001
TEMP_STEP = 0.005
RSQRT_SEED = 0x5F3759DF
PENALTY = -1e30

D1, D2, DL = 8, 64, 64
F = D1 * D2
FT = F // P
GT = 4
GROUPS = NT // GT
SLOTS = GROUPS * FT
LEAD = FT + 1


def window_after(cw, factor):
    return int(np.clip(int(np.float32(cw) * np.float32(factor)), MIN_WIN, T))


CW0 = max(min(T, MAX_WIN), MIN_WIN)
CW_DOWN = window_after(CW0, 0.9)
CW_DOWN_UP = window_after(CW_DOWN, 1.1)
CW_DOWN_DOWN = window_after(CW_DOWN, 0.9)
assert window_after(CW0, 1.1) == CW0 == T and CW_DOWN > MIN_WIN
LEVELS = [CW_DOWN_DOWN, CW_DOWN, CW_DOWN_UP]
assert LEVELS == sorted(LEVELS) and LEVELS[-1] < T

Q_PARTS = [0, 1, 2, 0, 1, 0]
K_PARTS = [0, 0, 0, 1, 1, 2]
PAIR = 2 * HD
WIN_ROW = len(Q_PARTS) * PAIR
MAX_ROW = WIN_ROW + len(LEVELS)
STACK = MAX_ROW + 6
BANDS = [(0, 3, 0), (3, 2, 1), (5, 1, 2)]

UH = 8
UNITS = B * H // UH
CH = 2
CHUNKS = UH // CH
GH = 4
VC = 2 * HD + 1
QB = 6
BUFS = QB // 2
EB = 8

COLS = ["bq", "bv", "lna", "lnb", "lqb", "lkb", "lvb", "thr", "temp", "fac", "level", "b2"]
BIASES = ["bq", "lqb", "lkb", "bv", "lvb"]


class Steps:

    def __init__(self, eng, sem, base=0):
        self.eng, self.sem, self.base, self.n = eng, sem, base, 0

    def done(self, instruction):
        instruction.then_inc(self.sem, 1)
        self.n += 1

    def wait(self):
        self.eng.wait_ge(self.sem, self.base + self.n)


def build(nc, x, wq, wk, wv, wo_t, lq, lk, lv, lv_t, cols, lnc, lnd, bo, m1, m2, mb, w1, w2,
          ident, ident_bf, blocks, centre, first_hit, token_pos, key_side, parity, out):
    ctx = ExitStack()
    with ctx:
        def sb(name, shape, dt=F32):
            return ctx.enter_context(nc.sbuf_tensor(name, shape, dt))

        def psum(name, shape, dt=F32):
            return ctx.enter_context(nc.psum_tensor(name, shape, dt))

        def sem(name):
            return ctx.enter_context(nc.semaphore(name))

        x_sb = sb("x_sb", [P, NT, D])
        qk = sb("qk", [P, 2, NT, D])
        qc, kc = qk[:, 0], qk[:, 1]
        xn = qc
        xn_t = sb("xn_t", [P, NT * P])
        attn = xn_t[:, :].rearrange("p (n d) -> p n d", n=NT)
        gate = sb("gate", [P, NT, D])
        k_res = sb("k_res", [P, B, H * T], BF16)
        v_res = sb("v_res", [P, NT, H, VC])
        q_st = sb("q_st", [P, QB, UH // 2 * T], BF16)
        e_sb = sb("e_sb", [P, EB, QT * T])
        o_t = sb("o_t", [P, 2, 2 * T])
        tt = sb("tt", [P, QT, H, VC])
        mx = sb("mx", [P, 2, QT, UH])
        mr = sb("mr", [P, 2, QT, UH])
        mp = sb("mp", [P, 2, QT, UH // 2, STACK - WIN_ROW], BF16)
        pen = sb("pen", [P, len(LEVELS)])
        tp = sb("tp", [P, 2, 3, T], BF16)
        tpk = sb("tpk", [P, 3, 2, T], BF16)
        stat = sb("stat", [P, NT, 6])
        mv = sb("mv", [P, NT, 2])
        v1, v2, y1, y2, tmp = (sb(n, [P, NT]) for n in ("v1", "v2", "y1", "y2", "tmp"))
        kn, ksq = o_t[:, 0, :].rearrange("p (b q d) -> p b q d", b=2, q=QT), o_t[:, 1, :].rearrange("p (b x) -> p b x", b=2)
        kvar, klnv, khv, ky, ktmp = (sb(n, [P, 2, QT * H]) for n in ("kvar", "klnv", "khv", "ky", "ktmp"))
        layers = sb("layers", [P, 7, D])
        kp = layers[:, 0:6, :].rearrange("p n d -> p (n d)").bitcast(BF16).rearrange("p (b s q d) -> p b s q d", b=2, s=3, q=QT)
        ge = sb("ge", [P, 2, D])
        tvar = sb("tvar", [P, 2, QT * H])
        ty = sb("ty", [P, 2, QT * H])
        ttmp = sb("ttmp", [P, QT * H])
        lnv = sb("lnv", [P, 2, QT * H])
        hv = sb("hv", [P, 2, QT * H])
        eps, eps_h, c15 = (sb(n, [P, 1]) for n in ("eps", "eps_h", "c15"))
        rden = sb("rden", [P, QT, H])
        o_new = sb("o_new", [P, QT, D])
        d_new = sb("d_new", [P, QT, D])
        r_new = sb("r_new", [P, QT, D])
        q_n = sb("q_n", [P, QT, D])
        pt = sb("pt", [P, 3, QT, D], BF16)
        dsum = sb("dsum", [P, B])
        dall = sb("dall", [P, 1])
        ctl = sb("ctl", [P, 16])
        notdone = sb("notdone", [P, 1], I32)
        rowmask = sb("rowmask", [P, QT])
        temps = sb("temps", [P, ITERS + 1])
        tsc = sb("tsc", [P, ITERS + 1])
        tsv = sb("tsv", [P, ITERS + 1])
        tst = sb("tst", [P, ITERS + 1])
        tsc_now = sb("tsc_now", [P, 1])
        zero_rows = sb("zero_rows", [P, 1], BF16)
        w_all = sb("w_all", [P, 4 * D])
        bias = sb("bias", [P, 4 * D])
        comp = e_sb[:, 6:8, :].rearrange("p a (b d) -> p (a b) d", d=D)
        wide = e_sb[:, 4:6, :].rearrange("p a (b d) -> p (a b) d", d=D)
        scl = sb("scl", [P, 2])
        ones = sb("ones", [P, P])
        ident_b = sb("ident_b", [P, P], BF16)
        hit_s = sb("hit_s", [P, P], BF16)
        lr_t = sb("lr_t", [DL + 1, NT * P])
        gm = sb("gm", [P, 2, D1])
        hot = sb("hot", [P, 2, GT, F], BF16)
        hot_t = sb("hot_t", [P, 2, GT * P], BF16)
        hh, mid, res_t = e_sb[:, 0:4, :], e_sb[:, 4:6, :], e_sb[:, 6:8, :]
        spare = hot[:, :, :, :].rearrange("p a n f -> p (a n f)").bitcast(F32)
        at_t = spare[:, 0:2 * GT * P].rearrange("p (a t) -> p a t", a=2)
        s_sb = spare[:, 2 * GT * P:3 * GT * P].rearrange("p (n d) -> p n d", n=GT)
        wo_s = sb("wo_s", [P, D])
        wq_s, wk_s, wv_s, lq_s, lk_s, lv_s, lvt_s = (layers[:, i, :] for i in range(7))
        col_s = sb("col_s", [P, len(COLS)])
        bo_s = sb("bo_s", [P, D])
        lnc_s, lnd_s = ge[:, 0, :], ge[:, 1, :]
        wkd = sb("wkd", [P, D])
        m1_s = sb("m1_s", [P, DL])
        m2_s = sb("m2_s", [DL + 1, F])
        w1_s = sb("w1_s", [P, F])
        w2_s = sb("w2_s", [P, FT, D])
        id_s = sb("id_s", [P, P])
        blk_s, cen_s = (tt[:, :, :, :].rearrange("p q h r -> p (q h r)")[:, i * P:(i + 1) * P] for i in range(2))
        pos_s = sb("pos_s", [P, QT])
        par_s = sb("par_s", [P, 2])

        q_scr = nc.dram_tensor("q_scr", [B, len(Q_PARTS), PAIR * H // 2, T], BF16, kind="Internal").ap()
        k_scr = nc.dram_tensor("k_scr", [B, len(K_PARTS), PAIR * H // 2, 2, T], BF16, kind="Internal").ap()

        s1 = psum("s1", [P, 4, 512])
        st = psum("st", [P, 2, 512])
        po = psum("po", [P, 512])
        px = psum("px", [P, 512])
        px_b = px[:, :].bitcast(BF16)

        col = {n: col_s[:, i:i + 1] for i, n in enumerate(COLS)}

        cols_in, layers_in, consts_in = sem("cols_in"), sem("layers_in"), sem("consts_in")
        x_in = sem("x_in")
        dve_step, pool_step, act_step = sem("dve_step"), sem("pool_step"), sem("act_step")
        pe_prep, act_prep, pool_prep = sem("pe_prep"), sem("act_prep"), sem("pool_prep")
        xn_ready, y2_ready, tsc_ready = sem("xn_ready"), sem("y2_ready"), sem("tsc_ready")
        xt_full, xt_copied = sem("xt_full"), sem("xt_copied")
        pj_full, pj_copied = sem("pj_full"), sem("pj_copied")
        k_squared, kvar_ready, k_guessed, kn_ready, kpart, ksub, kparts_ready = (
            sem(n) for n in ("k_squared", "kvar_ready", "k_guessed", "kn_ready", "kpart", "ksub", "kparts_ready"))
        kt_full, kt_copied = sem("kt_full"), sem("kt_copied")
        k0_loaded, k_loaded = sem("k0_loaded"), sem("k_loaded")
        kt_stored = [sem(f"kt_stored{i}") for i in range(2)]
        qt_full, qt_copied = sem("qt_full"), sem("qt_copied")
        q_stored = [sem(f"q_stored{i}") for i in range(2)]
        key_rows = sem("key_rows")
        q_loaded = [sem(f"q_loaded{i}") for i in range(QB // 2)]
        window_ready, window_rows = sem("window_ready"), sem("window_rows")
        s1_full, max_taken = sem("s1_full"), sem("max_taken")
        mp_ready, mt_full, mt_copied = sem("mp_ready"), sem("mt_full"), sem("mt_copied")
        st_full, exp_done = sem("st_full"), sem("exp_done")
        pv_done, o_copied = sem("pv_done"), sem("o_copied")
        tt_full, tt_copied = sem("tt_full"), sem("tt_copied")
        rden_ready, pool_out, pool_sq, var_ready, parts_ready = (
            sem(n) for n in ("rden_ready", "pool_out", "pool_sq", "var_ready", "parts_ready"))
        diff_ready, diff_full, dall_ready, attn_taken = (
            sem(n) for n in ("diff_ready", "diff_full", "dall_ready", "attn_taken"))
        guess_ready = sem("guess_ready")
        lr_full, lr_copied = sem("lr_full"), sem("lr_copied")
        lg_full, hot_ready, ht_full, ht_copied, mid_full, mid_copied, hit_full, h_ready, res_full, res_copied = (
            sem(n) for n in ("lg_full", "hot_ready", "ht_full", "ht_copied", "mid_full", "mid_copied", "hit_full",
                             "h_ready", "res_full", "res_copied"))
        r_full, r_copied = sem("r_full"), sem("r_copied")
        ge_exp, ge_plus, ge_inverse, gate_ready = (sem(n) for n in ("ge_exp", "ge_plus", "ge_inverse", "gate_ready"))
        at_full, at_copied, s_full, y_ready, y_stored = (
            sem(n) for n in ("at_full", "at_copied", "s_full", "y_ready", "y_stored"))

        block = ctx.enter_context(nc.Block())

        layer_loads = [(lq_s, lq), (blk_s, blocks), (lk_s, lk), (lv_s, lv), (lvt_s, lv_t), (cen_s, centre), (wq_s, wq),
                       (wk_s, wk), (wv_s, wv), (id_s[:, :], ident)]
        loads = [(lnc_s, lnc), (lnd_s, lnd), (m1_s[:, :], m1), (m2_s[0:DL, :], m2), (m2_s[DL:DL + 1, :], mb),
                 (ident_b[:, :], ident_bf), (w1_s[:, :], w1), (hit_s[:, :], first_hit), (w2_s[:, :, :], w2),
                 (par_s[:, :], parity), (wo_s[:, :], wo_t), (pos_s[:, :], token_pos), (bo_s[:, :], bo)]

        def in_body(n, c, last):
            b = n // 2
            found = []
            if n % 2 == 0 and c == 3 and b >= 1:
                found.append(("t", QT * (b - 1)))
            if n % 2 == 1 and c == 0 and b >= 1:
                found.append(("t", QT * (b - 1) + 1))
            if c == 1 and n + 1 < UNITS:
                found.append(("m", n + 1))
            if n % 2 == 1 and c == 3 and b >= 2 and not last:
                found.append(("q", b - 2))
            return found

        def misc_order(last):
            order = [("m", 0)]
            for n in range(UNITS):
                for c in range(CHUNKS):
                    order += in_body(n, c, last)
            return order + [("t", QT * (B - 1)), ("t", QT * (B - 1) + 1)]

        def in_slot(i):
            found = []
            if i % 2 == 0 and 0 <= i < 2 * B:
                found.append(("k", i // 2))
            if i % 2 == 1 and 0 <= i < 2 * B:
                found.append(("q", i // 2))
            if i >= FT + 2 and (i - FT - 2) % FT == 0 and (i - FT - 2) // FT < GROUPS:
                found.append(("r", (i - FT - 2) // FT))
            return found

        FIRST_SLOT, LAST_SLOT = -LEAD, SLOTS + 2
        PREP_ORDER = [u for i in range(FIRST_SLOT, LAST_SLOT + 1) for u in in_slot(i)]
        COPIED = {"m": (mt_copied, UNITS), "t": (tt_copied, NT), "q": (qt_copied, B)}

        @block.sync
        def _(sp):
            sp.dma_start(col_s[:, :], cols).then_inc(cols_in, 16)
            sp.dma_start(x_sb[:, :, :], x.rearrange("(n p) d -> p n d", p=P)).then_inc(x_in, 16)
            for dst, src in layer_loads:
                sp.dma_start(dst, src).then_inc(layers_in, 16)
            for dst, src in loads:
                sp.dma_start(dst, src).then_inc(consts_in, 16)
            sp.dma_start(k_res[WIN_ROW:STACK, :, :], key_side).then_inc(key_rows, 16)
            def store_k(b):
                sp.wait_ge(kt_copied, 2 * (b + 1))
                for first, count, part in BANDS:
                    sp.dma_start(k_scr[b, first:first + count].rearrange("j c e t -> c j (e t)"),
                                 tpk[:, part].rearrange("c e t -> c (e t)").unsqueeze(1).to_broadcast([P, count, 2 * T]))\
                      .then_inc(kt_stored[b % 2], 16)

            def load_k(b):
                sp.wait_ge(kt_stored[b % 2], 16 * 3 * (b // 2 + 1))
                sp.dma_start(k_res[0:WIN_ROW, b, :], k_scr[b].rearrange("j (r p) e t -> (j r) (p e t)", r=PAIR))\
                  .then_inc(k_loaded if b else k0_loaded, 16)

            def store_q(b, count):
                sp.wait_ge(qt_copied, count)
                for first, n, _ in BANDS:
                    sp.dma_start(q_scr[b, first:first + n].rearrange("j c t -> c j t"),
                                 tp[:, b % 2, 0:n, :]).then_inc(q_stored[b % 2], 16)

            def load_q(it, b, stored):
                buf = 2 * b % QB
                sp.wait_ge(q_stored[b % 2], stored)
                sp.dma_start(q_st[0:WIN_ROW, buf:buf + 2, :].rearrange("r u x -> r (u x)"),
                             q_scr[b].rearrange("j (r p) t -> (j r) (p t)", r=PAIR)).then_inc(q_loaded[b % BUFS], 16)

            for b in range(B + 1):
                if b < B:
                    store_k(b)
                if b >= 1:
                    load_k(b - 1)
                    store_q(b - 1, b)
                if b == BUFS + 1:
                    load_q(0, 0, 48 * 2)
                    load_q(0, 2, 48 * 2)
                if b == BUFS + 2:
                    load_q(0, 1, 48 * 2)

            def load_first(it):
                for b in (0, 2, 1):
                    used = max(range(b, B, BUFS))
                    sp.wait_ge(st_full, it * UNITS * UH - (B - 1 - used) * 2 * UH)
                    load_q(it, b, 48 * (it * (B // 2) + b // 2 + 1))

            def queries(it, last):
                for n in range(1, UNITS, 2):
                    b = n // 2
                    if b + BUFS < B:
                        sp.wait_ge(st_full, it * UNITS * UH + (n + 1) * UH)
                        load_q(it, b + BUFS, 48 * (it * (B // 2) + (b + BUFS) // 2 + 1))
                    if b >= 2 and not last:
                        store_q(b - 2, B + it * B + b - 1)
                if not last:
                    load_first(it + 1)
                    store_q(B - 2, B + it * B + B - 1)
                    store_q(B - 1, B + it * B + B)

            with sp.Fori(0, ITERS - 1) as it:
                queries(it, False)
            queries(ITERS - 1, True)
            for g in range(GROUPS):
                sp.wait_ge(y_ready, g + 1)
                sp.dma_start(out[g * GT * P:(g + 1) * GT * P, :].rearrange("(n p) d -> p n d", p=P),
                             gate[:, g * GT:(g + 1) * GT, :]).then_inc(y_stored, 16)
            sp.wait_ge(y_stored, 16 * GROUPS)
            for i in range(2):
                sp.wait_ge(q_stored[i], 48 * B // 2 * ITERS)

        def pairs(v):
            return v.rearrange("t q (p r) -> t q p r", r=PAIR)

        def pairs_turned(v):
            return v.rearrange("t q (r p) -> t q p r", r=PAIR)

        def rsqrt(eng, steps, v, yy, t):
            steps.done(eng.tensor_scalar(yy.bitcast(I32), v.bitcast(I32), 1, None, ALU.arith_shift_right))
            steps.wait()
            steps.done(eng.tensor_scalar(yy.bitcast(I32), yy.bitcast(I32), -1.0, float(RSQRT_SEED), ALU.mult, ALU.add))
            steps.done(eng.tensor_scalar(v, v, -0.5, None, ALU.mult))
            for _ in range(3):
                steps.wait()
                steps.done(eng.tensor_tensor(t, yy, yy, ALU.mult))
                steps.wait()
                steps.done(eng.tensor_tensor(t, t, v, ALU.mult))
                steps.wait()
                steps.done(eng.scalar_tensor_tensor(yy, t, 1.5, yy, ALU.add, ALU.mult))
            steps.wait()

        C_DIFF, C_RHS, C_CONV, C_DONE, C_GATE, C_UP, C_DOWN, C_IS, C_CW, C_T, C_PEN, C_DU, C_DD = range(13)

        def c(i):
            return ctl[:, i:i + 1]

        @block.vector
        def _(dve):
            steps = Steps(dve, dve_step)
            dve.memset(v_res[:, :, :, VC - 1:VC], 1.0)
            dve.memset(c(C_GATE), 0.0)
            dve.memset(c(C_DONE), 0.0)
            dve.memset(c(C_CW), float(CW0))
            dve.memset(dsum[:, :], 0.0)
            dve.memset(notdone[:, :], 1)
            dve.memset(mp[:, :, :, :, :], 0.0)
            dve.wait_ge(cols_in, 16)
            steps.done(dve.tensor_copy(temps[:, 0:1], col["temp"]))
            for i in range(ITERS):
                steps.wait()
                steps.done(dve.tensor_scalar(temps[:, i + 1:i + 2], temps[:, i:i + 1], TEMP_STEP, None, ALU.add))
            steps.wait()
            steps.done(dve.tensor_scalar(tsv[:, :], temps[:, :], 0.0, None, ALU.is_gt))
            steps.wait()
            steps.done(dve.tensor_tensor(temps[:, :], temps[:, :], tsv[:, :], ALU.mult))
            steps.done(dve.tensor_scalar(tst[:, :], tsv[:, :], -1.0, 1.0, ALU.mult, ALU.add))
            steps.wait()
            steps.done(dve.tensor_tensor(tsv[:, :], temps[:, :], tst[:, :], ALU.add))
            steps.wait()
            rsqrt(dve, steps, tsv[:, :], tsc[:, :], tst[:, :])
            dve.tensor_copy(tsc_now[:, :], tsc[:, 0:1]).then_inc(tsc_ready, 1)

            dve.wait_ge(x_in, 16)
            for t in range(NT):
                last = dve.bn_stats(stat[:, t, :], x_sb[:, t, :])
            steps.done(last)
            steps.wait()
            for t in range(NT):
                last = dve.bn_aggr(mv[:, t, :], stat[:, t, :])
            steps.done(last)
            steps.wait()
            steps.done(dve.tensor_scalar(v1[:, :], mv[:, :, 1], EPS, None, ALU.add))
            steps.wait()
            rsqrt(dve, steps, v1[:, :], y1[:, :], tmp[:, :])
            for t in range(NT):
                last = dve.tensor_scalar(xn[:, t, :], x_sb[:, t, :], mv[:, t, 0:1], y1[:, t:t + 1],
                                         ALU.subtract, ALU.mult)
                if t % GT == GT - 1:
                    last.then_inc(xn_ready, 1)
            steps.done(dve.tensor_tensor(v2[:, :], y1[:, :], y1[:, :], ALU.mult))
            steps.wait()
            steps.done(dve.tensor_tensor(v2[:, :], v2[:, :], mv[:, :, 1], ALU.mult))
            steps.wait()
            steps.done(dve.tensor_scalar(v2[:, :], v2[:, :], EPS, None, ALU.add))
            steps.wait()
            rsqrt(dve, steps, v2[:, :], y2[:, :], tmp[:, :])
            dve.wait_ge(act_prep, 9)
            for t in range(NT):
                dve.wait_ge(pj_full, t + 1)
                pj = s1[:, 2 + t % 2, :]
                dve.scalar_tensor_tensor(qk[:, :, t, :], pj[:, 0:2 * D].rearrange("p (a d) -> p a d", a=2),
                                         y2[:, t:t + 1], bias[:, 0:2 * D].rearrange("p (a d) -> p a d", a=2),
                                         ALU.mult, ALU.add)
                dve.scalar_tensor_tensor(v_res[:, t, :, 0:2 * HD],
                                         pj[:, 2 * D:].rearrange("p (h x) -> p h x", h=H), y2[:, t:t + 1],
                                         bias[:, 2 * D:].rearrange("p (h x) -> p h x", h=H),
                                         ALU.mult, ALU.add).then_inc(pj_copied, 1)

            def copy_q(b, full, stored):
                dve.wait_ge(qt_full, full)
                if stored is not None:
                    dve.wait_ge(q_stored[b % 2], stored)
                dve.tensor_copy(tp[:, b % 2, :, :], px_b[:, 0:3 * T].rearrange("p (s t) -> p s t", s=3))\
                   .then_inc(qt_copied, 1)

            def variance(r, b):
                dve.wait_ge(pool_sq, r * B + b + 1)
                dve.tensor_reduce(tvar[:, b % 2, :], r_new[:, :, :].rearrange("p q (h e) -> p (q h) e", h=H),
                                  AX_X, ALU.add).then_inc(var_ready, 1)

            dve.wait_ge(pool_prep, 3)
            for i in range(FIRST_SLOT, LAST_SLOT + 1):
                t = i + LEAD
                if t < NT:
                    g = t // GT
                    blockwise = s1[:, t % 2, :].rearrange("p (j q) -> p j q", j=D1)
                    dve.wait_ge(lg_full, t + 1)
                    steps.done(dve.tensor_reduce(gm[:, t % 2, :], blockwise, AX_X, ALU.max))
                    steps.wait()
                    if g >= 2 and t % GT == 0:
                        dve.wait_ge(ht_full, FT * (g - 1))
                    dve.tensor_tensor(hot[:, g % 2, t % GT, :].rearrange("p (j q) -> p j q", j=D1), blockwise,
                                      gm[:, t % 2, :].unsqueeze(2).to_broadcast([P, D1, D2]), ALU.is_equal)\
                       .then_inc(hot_ready, 1)
                if 0 <= i < SLOTS:
                    dve.wait_ge(hit_full, i + 1)
                    dve.wait_ge(mid_copied, i + 1)
                    if i >= 4:
                        dve.wait_ge(res_full, i - 3)
                    dve.scalar_tensor_tensor(hh[:, i % 4, :], st[:, 0, :], 1.0, mid[:, i % 2, :],
                                             ALU.is_equal, ALU.mult).then_inc(h_ready, 1)
                b = (i + 4) // 2
                if i % 2 == 0 and 0 <= b < B:
                    dve.wait_ge(k_squared, b + 1)
                    dve.tensor_reduce(kvar[:, b % 2, :], ksq[:, b % 2, :].rearrange("p (n e) -> p n e", e=HD),
                                      AX_X, ALU.add).then_inc(kvar_ready, 1)
                b = (i + 2) // 2
                if i % 2 == 0 and 0 <= b < B:
                    dve.wait_ge(kpart, 2 * b + 1)
                    dve.tensor_tensor(pairs(kn[:, b % 2]), pairs(kn[:, b % 2]), pairs_turned(kp[:, b % 2, 0]),
                                      ALU.subtract).then_inc(ksub, 1)
                b = (i + 3) // 2
                if i % 2 == 1 and 0 <= b < B:
                    dve.wait_ge(k_guessed, b + 1)
                    one = ky[:, b % 2, :]
                    steps.done(dve.tensor_scalar(khv[:, b % 2, :], kvar[:, b % 2, :], -0.5 / HD, -0.5 * EPS,
                                                 ALU.mult, ALU.add))
                    steps.done(dve.tensor_tensor(ktmp[:, b % 2, :], one, one, ALU.mult))
                    steps.wait()
                    steps.done(dve.tensor_tensor(ktmp[:, b % 2, :], ktmp[:, b % 2, :], khv[:, b % 2, :], ALU.mult))
                    steps.wait()
                    steps.done(dve.scalar_tensor_tensor(one, ktmp[:, b % 2, :], 1.5, one, ALU.add, ALU.mult))
                    steps.wait()
                    steps.done(dve.tensor_tensor(
                        kn[:, b % 2].rearrange("p q (h e) -> p (q h) e", h=H),
                        kc[:, QT * b:QT * b + QT, :].rearrange("p q (h e) -> p (q h) e", h=H),
                        one.unsqueeze(2).to_broadcast([P, QT * H, HD]), ALU.mult))
                    steps.wait()
                    dve.tensor_tensor(kn[:, b % 2], kn[:, b % 2],
                                      wkd[:, :].unsqueeze(1).to_broadcast([P, QT, D]), ALU.mult).then_inc(kn_ready, 1)
                    variance(0, b)
                b = (i + 1) // 2
                if i % 2 == 1 and 0 <= b < B:
                    dve.wait_ge(kpart, 2 * b + 2)
                    dve.tensor_tensor(pairs_turned(kp[:, b % 2, 2]), pairs(kn[:, b % 2]),
                                      pairs_turned(kp[:, b % 2, 1]), ALU.subtract).then_inc(kparts_ready, 1)
                b = (i - 2) // 2
                if i % 2 == 0 and 0 <= b < B:
                    copy_q(b, b + 1, 48 * (b // 2) if b >= 2 else None)
            before = steps.n

            def maxima(it, n, cc):
                i = n * CHUNKS + cc
                dve.wait_ge(s1_full, it * UNITS * CHUNKS + i + 1)
                if cc == 0 and n >= 2:
                    dve.wait_ge(mp_ready, it * UNITS + n - 1)
                dve.tensor_reduce(
                    mx[:, n % 2, :, CH * cc:CH * cc + CH].rearrange("p q h -> p h q"),
                    s1[:, 2 * (i % 2):2 * (i % 2) + 2, :].rearrange("p h (q k) -> p h q k", q=QT),
                    AX_X, ALU.max, negate=True).then_inc(max_taken, 1)

            def round_(it, last):
                rnd = Steps(dve, dve_step, before + it * VECTOR_STEPS)

                def inverse_sums(b):
                    dve.wait_ge(tt_copied, it * NT + QT * (b + 1))
                    dve.reciprocal(rden[:, :, :], tt[:, :, :, VC - 1]).then_inc(rden_ready, 1)

                def difference(b):
                    dve.wait_ge(pool_out, it * B + b + 1)
                    dve.tensor_reduce(dsum[:, b:b + 1], d_new[:, :, :].rearrange("p q d -> p (q d)"), AX_X,
                                      ALU.add, apply_absolute_value=True).then_inc(diff_ready, 1)

                def inverse_gate(t):
                    dve.wait_ge(ge_plus, t + 1)
                    dve.reciprocal(ge[:, t % 2, :], ge[:, t % 2, :]).then_inc(ge_inverse, 1)

                def keep(b):
                    if last:
                        dve.wait_ge(pool_out, it * B + b + 1)
                    dve.copy_predicated(attn[:, QT * b:QT * b + QT, :].rearrange("p q d -> p (q d)"),
                                        notdone[:, 0:1].to_broadcast([P, QT * D]),
                                        o_new[:, :, :].rearrange("p q d -> p (q d)")).then_inc(attn_taken, 1)

                def new_q(b):
                    copy_q(b, B + it * B + b + 1, 48 * (it * (B // 2) + (B + b) // 2))

                for n in range(UNITS):
                    b = n // 2
                    for cc in range(CHUNKS):
                        if n + 2 < UNITS:
                            maxima(it, n + 2, cc)
                        if n % 2 == 1 and b >= 1 and cc == 1:
                            inverse_sums(b - 1)
                        if n % 2 == 0 and b >= 3 and cc == 0 and not last:
                            new_q(b - 3)
                        if n % 2 == 0 and b >= 2 and cc == 1:
                            if not last:
                                difference(b - 2)
                                variance(it + 1, b - 2)
                        if n % 2 == 0 and b >= 2 and cc == 3:
                            keep(b - 2)
                        if last and cc == 2 and n >= 1:
                            inverse_gate(n - 1)
                if last:
                    keep(B - 2)
                    inverse_gate(NT - 1)
                    inverse_sums(B - 1)
                    return
                new_q(B - 3)
                difference(B - 2)
                variance(it + 1, B - 2)
                keep(B - 2)
                inverse_sums(B - 1)
                difference(B - 1)
                dve.wait_ge(diff_ready, it * B + B)
                dve.tensor_reduce(dall[:, :], dsum[:, :], AX_X, ALU.add).then_inc(dall_ready, 1)
                keep(B - 1)
                dve.wait_ge(diff_full, it + 1)
                rnd.done(dve.tensor_scalar(c(C_DIFF), px[:, 0:1], 1.0 / (B * T * D), None, ALU.mult))
                rnd.done(dve.tensor_scalar(c(C_IS), c(C_CW), float(T), None, ALU.is_lt))
                rnd.wait()
                rnd.done(dve.tensor_scalar(c(C_RHS), c(C_DIFF), col["fac"], col["thr"], ALU.mult, ALU.add))
                rnd.done(dve.tensor_scalar(c(C_UP), c(C_DIFF), UP_DIFF, float(CW_DOWN_UP - CW_DOWN),
                                           ALU.is_gt, ALU.mult))
                rnd.done(dve.tensor_scalar(c(C_DOWN), c(C_DIFF), DOWN_DIFF, None, ALU.is_lt))
                rnd.done(dve.tensor_scalar(c(C_DD), c(C_IS), float((CW_DOWN_DOWN - CW_DOWN) - (CW_DOWN - CW0)),
                                           float(CW_DOWN - CW0), ALU.mult, ALU.add))
                rnd.wait()
                rnd.done(dve.tensor_tensor(c(C_CONV), c(C_DIFF), c(C_RHS), ALU.is_lt))
                rnd.done(dve.scalar_tensor_tensor(c(C_CW), c(C_UP), c(C_IS), c(C_CW), ALU.mult, ALU.add))
                rnd.wait()
                rnd.done(dve.scalar_tensor_tensor(c(C_DONE), c(C_CONV), c(C_GATE), c(C_DONE), ALU.mult, ALU.max))
                rnd.done(dve.scalar_tensor_tensor(c(C_CW), c(C_DOWN), c(C_DD), c(C_CW), ALU.mult, ALU.add))
                rnd.wait()
                rnd.done(dve.memset(c(C_GATE), 1.0))
                rnd.done(dve.tensor_scalar(notdone[:, :], c(C_DONE), 0.0, None, ALU.is_equal))
                rnd.done(dve.tensor_scalar(rowmask[:, :], pos_s[:, :], c(C_CW), None, ALU.is_lt))
                rnd.done(dve.tensor_scalar(c(C_PEN), col["level"], c(C_CW), PENALTY, ALU.is_ge, ALU.mult))
                for i, level in enumerate(LEVELS):
                    rnd.done(dve.tensor_scalar(pen[:, i:i + 1], c(C_CW), float(level), PENALTY, ALU.is_le, ALU.mult))
                rnd.wait()
                rnd.done(dve.tensor_copy(mp[:, :, :, :, 0:len(LEVELS)].rearrange("p n q c r -> p (n q c) r"),
                                         pen[:, :].unsqueeze(1).to_broadcast([P, QT * UH, len(LEVELS)])))
                for i in range(2):
                    done = dve.tensor_scalar(q_st[WIN_ROW:MAX_ROW, i, :], zero_rows[WIN_ROW:MAX_ROW, :].to_broadcast([len(LEVELS), UH // 2 * T]),
                                             ctl[WIN_ROW:MAX_ROW, C_PEN:C_PEN + 1], None, ALU.add)
                done.then_inc(window_ready, 1)
                variance(it + 1, B - 1)
                for n in range(2):
                    for cc in range(CHUNKS):
                        maxima(it + 1, n, cc)
                    new_q(B - 2 + n)
                assert rnd.n == VECTOR_STEPS, rnd.n

            for n in range(2):
                for cc in range(CHUNKS):
                    maxima(0, n, cc)
            with dve.Fori(0, ITERS - 1) as it:
                round_(it, False)
            round_(ITERS - 1, True)

            out_steps = Steps(dve, dve_step, before + (ITERS - 1) * VECTOR_STEPS)
            for g in range(GROUPS):
                if g == GROUPS - 1:
                    dve.wait_ge(pool_out, ITERS * B)
                    dve.copy_predicated(attn[:, NT - QT:NT, :].rearrange("p q d -> p (q d)"),
                                        notdone[:, 0:1].to_broadcast([P, QT * D]),
                                        o_new[:, :, :].rearrange("p q d -> p (q d)")).then_inc(attn_taken, 1)
                tiles = slice(GT * g, GT * g + GT)
                dve.wait_ge(s_full, g + 1)
                bo_all = bo_s[:, :].unsqueeze(1).to_broadcast([P, GT, D])
                out_steps.done(dve.tensor_tensor(s_sb[:, :, :], s1[:, g % 4, :].rearrange("p (n d) -> p n d", n=GT),
                                                 bo_all, ALU.add))
                out_steps.wait()
                dve.wait_ge(gate_ready, GT * (g + 1))
                out_steps.done(dve.tensor_tensor(gate[:, tiles, :], s_sb[:, :, :], gate[:, tiles, :], ALU.mult))
                out_steps.wait()
                dve.tensor_tensor(gate[:, tiles, :], gate[:, tiles, :], x_sb[:, tiles, :], ALU.add).then_inc(y_ready, 1)

        @block.gpsimd
        def _(pool):
            heads = "p q (h e) -> p q h e"
            zeros = zero_rows[:, :].unsqueeze(2)
            pool.memset(ones[:, :], 1.0)
            pool.memset(zero_rows[:, :], 0.0)
            pool.memset(eps[:, :], EPS)
            pool.memset(eps_h[:, :], -0.5 * EPS)
            pool.memset(c15[:, :], 1.5)
            prep = Steps(pool, pool_step)
            prep.done(pool.memset(rowmask[:, :], 1.0))
            prep.wait()
            prep.done(pool.memset(lr_t[DL:DL + 1, :], 1.0))
            prep.wait()
            pool.memset(q_st[WIN_ROW:, 0:2, :], 0.0).then_inc(window_ready, 1)
            pool.wait_ge(window_ready, 1)
            pool.wait_ge(cols_in, 16)
            pool.wait_ge(layers_in, 16 * len(layer_loads))
            for i, w in enumerate((lq_s, lk_s, lv_s, lvt_s)):
                last = pool.tensor_tensor(comp[:, i, :], w[:, :], blk_s[:, :], ALU.mult)
            last.then_inc(pool_prep, 1)
            for i, name in enumerate(BIASES):
                last = pool.tensor_tensor(wide[:, i, :], ones[:, :], col[name].to_broadcast([P, P]), ALU.mult)
            prep.done(last)
            prep.wait()
            prep.done(pool.tensor_scalar(wide[:, 0, :], wide[:, 0, :], QK_SCALE, None, ALU.mult))
            prep.done(pool.tensor_scalar(scl[:, 0:1], col["lna"], QK_SCALE, None, ALU.mult))
            pool.tensor_scalar(scl[:, 1:2], col["lnb"], QK_SCALE, None, ALU.mult).then_inc(pool_prep, 1)
            pool.wait_ge(consts_in, 16 * len(loads))
            prep.done(pool.tensor_scalar(wkd[:, :], lnc_s[:, :], INV_SQRT_E, None, ALU.mult))
            prep.wait()
            pool.tensor_tensor(wkd[:, :], wkd[:, :], lnd_s[:, :], ALU.mult).then_inc(pool_prep, 1)
            pool.wait_ge(pool_prep, 3)
            pool.memset(q_st[WIN_ROW:, 2:QB, :], 0.0).then_inc(window_rows, 1)
            pool.wait_ge(window_rows, 1)

            def split_max(rnd, it, n):
                m, r = (v[:, n % 2].rearrange("p q (c e) -> p q c e", e=2) for v in (mx, mr))
                w = mp[:, n % 2, :, :, len(LEVELS):].rearrange("p q c (e s) -> p q c e s", e=2)
                pool.wait_ge(max_taken, it * UNITS * CHUNKS + (n + 1) * CHUNKS)
                if n >= 2:
                    pool.wait_ge(mt_full, it * UNITS + n - 1)
                no = zeros.unsqueeze(3).to_broadcast([P, QT, UH // 2, 2])
                rnd.done(pool.tensor_tensor(w[:, :, :, :, 0], m, no, ALU.add))
                rnd.wait()
                rnd.done(pool.tensor_tensor(r, m, w[:, :, :, :, 0], ALU.subtract))
                rnd.wait()
                rnd.done(pool.tensor_tensor(w[:, :, :, :, 1], r, no, ALU.add))
                rnd.wait()
                pool.tensor_tensor(w[:, :, :, :, 2], r, w[:, :, :, :, 1], ALU.subtract).then_inc(mp_ready, 1)

            def new_queries(rnd, r, b):
                tiles = slice(QT * b, QT * b + QT)
                pool.wait_ge(guess_ready, r * B + b + 1)
                rnd.done(pool.tensor_tensor(ttmp[:, :], ty[:, b % 2, :], ty[:, b % 2, :], ALU.mult))
                rnd.wait()
                rnd.done(pool.tensor_tensor(ttmp[:, :], ttmp[:, :], hv[:, b % 2, :], ALU.mult))
                rnd.wait()
                rnd.done(pool.tensor_tensor(ttmp[:, :], ttmp[:, :], c15[:, :].to_broadcast([P, QT * H]), ALU.add))
                rnd.wait()
                rnd.done(pool.tensor_tensor(ty[:, b % 2, :], ty[:, b % 2, :], ttmp[:, :], ALU.mult))
                rnd.wait()
                rnd.done(pool.tensor_tensor(ty[:, b % 2, :], ty[:, b % 2, :], tsc_now[:, :].to_broadcast([P, QT * H]), ALU.mult))
                rnd.wait()
                for e in range(2):
                    rnd.done(pool.tensor_tensor(
                        q_n[:, :, e * D // 2:(e + 1) * D // 2].rearrange("p q (d c) -> p q c d", d=HD),
                        qc[:, tiles, :].rearrange("p q (c e d) -> p q c e d", e=2, d=HD)[:, :, :, e, :],
                        ty[:, b % 2, :].rearrange("p (q c e) -> p q c e", q=QT, e=2)[:, :, :, e]
                        .unsqueeze(3).to_broadcast([P, QT, H // 2, HD]), ALU.mult))
                rnd.wait()

            def query_parts(rnd, r, b):
                if not (isinstance(r, int) and r * B + b == 0):
                    pool.wait_ge(qt_full, r * B + b)
                no = zeros.to_broadcast([P, QT, D])
                rnd.done(pool.tensor_tensor(pt[:, 0], q_n[:, :, :], no, ALU.add))
                rnd.wait()
                rnd.done(pool.tensor_tensor(q_n[:, :, :], q_n[:, :, :], pt[:, 0], ALU.subtract))
                rnd.wait()
                rnd.done(pool.tensor_tensor(pt[:, 1], q_n[:, :, :], no, ALU.add))
                rnd.wait()
                pool.tensor_tensor(pt[:, 2], q_n[:, :, :], pt[:, 1], ALU.subtract)\
                    .then_inc(parts_ready, 1)

            def round_(it, last):
                rnd = Steps(pool, pool_step, FIRST_POOL_STEPS + it * POOL_STEPS)

                def gated(t):
                    pool.wait_ge(ge_inverse, t + 1)
                    pool.tensor_tensor(gate[:, t, :], gate[:, t, :], ge[:, t % 2, :], ALU.mult).then_inc(gate_ready, 1)

                def new_outputs(b, then=None):
                    tiles = slice(QT * b, QT * b + QT)
                    pool.wait_ge(rden_ready, it * B + b + 1)
                    rnd.done(pool.tensor_tensor(rden[:, :, :], rden[:, :, :],
                                                rowmask[:, :].unsqueeze(2).to_broadcast([P, QT, H]), ALU.mult))
                    rnd.wait()
                    over = rden[:, :, :].unsqueeze(3).to_broadcast([P, QT, H, HD])
                    if b >= 1:
                        pool.wait_ge(attn_taken, it * B + b)
                    if last:
                        pool.tensor_tensor(o_new[:, :, :].rearrange(heads, h=H), tt[:, :, :, 0:HD], over,
                                           ALU.mult).then_inc(pool_out, 1)
                        return
                    rnd.done(pool.tensor_tensor(o_new[:, :, :].rearrange(heads, h=H), tt[:, :, :, 0:HD], over,
                                                ALU.mult))
                    rnd.wait()
                    pool.tensor_tensor(d_new[:, :, :], o_new[:, :, :], attn[:, tiles, :], ALU.subtract)\
                        .then_inc(pool_out, 1)
                    if then is not None:
                        split_max(rnd, it, then)
                    pool.wait_ge(var_ready, (it + 1) * B + b)
                    rnd.done(pool.tensor_tensor(r_new[:, :, :].rearrange(heads, h=H), tt[:, :, :, HD:2 * HD], over,
                                                ALU.mult))
                    rnd.wait()
                    rnd.done(pool.tensor_tensor(qc[:, tiles, :], qc[:, tiles, :], r_new[:, :, :], ALU.add))
                    rnd.wait()
                    pool.tensor_tensor(r_new[:, :, :], qc[:, tiles, :], qc[:, tiles, :], ALU.mult).then_inc(pool_sq, 1)

                if not last:
                    rnd.done(pool.tensor_copy(tsc_now[:, :], tsc[:, bass.ds(it + 1, 1)]))
                    rnd.wait()
                for n in range(UNITS):
                    b = n // 2
                    if n % 2 == 0 and b >= 2 and not last:
                        new_queries(rnd, it + 1, b - 2)
                    if n % 2 == 1:
                        if b >= 2 and not last:
                            query_parts(rnd, it + 1, b - 2)
                        between = n + 2 if b >= 1 and n + 2 < UNITS and not last else None
                        if b >= 1:
                            new_outputs(b - 1, between)
                    if n + 2 < UNITS and not (n % 2 == 1 and b >= 1 and not last):
                        split_max(rnd, it, n + 2)
                    if last:
                        if n >= 1:
                            gated(n - 1)
                        pool.wait_ge(ge_exp, n + 1)
                        pool.tensor_tensor(ge[:, n % 2, :], ge[:, n % 2, :], ones[:, :], ALU.add).then_inc(ge_plus, 1)
                if last:
                    gated(NT - 1)
                new_outputs(B - 1)
                if last:
                    return
                new_queries(rnd, it + 1, B - 2)
                query_parts(rnd, it + 1, B - 2)
                new_queries(rnd, it + 1, B - 1)
                split_max(rnd, it + 1, 0)
                query_parts(rnd, it + 1, B - 1)
                split_max(rnd, it + 1, 1)
                assert rnd.n == POOL_STEPS, rnd.n

            def square(b):
                pool.wait_ge(pj_copied, QT * (b + 1))
                if b >= 1:
                    pool.wait_ge(var_ready, b)
                tiles = slice(QT * b, QT * b + QT)
                pool.tensor_tensor(r_new[:, :, :], qc[:, tiles, :], qc[:, tiles, :], ALU.mult).then_inc(pool_sq, 1)

            pool.wait_ge(tsc_ready, 1)
            square(0)
            for b in range(B):
                if b + 1 < B:
                    square(b + 1)
                new_queries(prep, 0, b)
                query_parts(prep, 0, b)
            pool.wait_ge(mid_full, SLOTS)
            prep.done(pool.memset(attn[:, :, :], 0.0))
            prep.wait()
            for n in range(2):
                split_max(prep, 0, n)
            FIRST_POOL_STEPS = prep.n
            with pool.Fori(0, ITERS - 1) as it:
                round_(it, False)
            round_(ITERS - 1, True)

        @block.scalar
        def _(act):
            act.preload_act_table_set("natural_log_exp_and_others")
            steps = Steps(act, act_step)
            act.wait_ge(pe_prep, 1)
            act.activation(comp[:, 4:6, :], s1[:, 0, 0:2 * D].rearrange("p (a d) -> p a d", a=2), ACT.Copy)\
               .then_inc(act_prep, 1)
            act.wait_ge(pe_prep, 2)
            act.activation(comp[:, 7, :], s1[:, 1, 0:D], ACT.Copy).then_inc(act_prep, 1)
            act.wait_ge(pe_prep, 3)
            act.activation(w_all[:, 0:D], s1[:, 2, 0:D], ACT.Copy, scale=scl[:, 0:1]).then_inc(act_prep, 1)
            act.activation(w_all[:, D:2 * D], s1[:, 2, D:2 * D], ACT.Copy, scale=scl[:, 1:2]).then_inc(act_prep, 1)
            by_head = "p (h a e) -> p a h e"
            by_kind = "p (a h e) -> p a h e"
            for dst, src, scale in ((w_all, s1[:, 2, 2 * D:], col["lnb"]), (bias, s1[:, 3, 2 * D:], 1.0)):
                for a in range(2):
                    act.activation(dst[:, 2 * D:].rearrange(by_head, h=H, a=2)[:, a],
                                   src.rearrange(by_kind, h=H, a=2)[:, a], ACT.Copy, scale=scale).then_inc(act_prep, 1)
            act.activation(bias[:, 0:2 * D], s1[:, 3, 0:2 * D], ACT.Copy).then_inc(act_prep, 1)
            for g in range(GROUPS):
                group = slice(g * GT * P, (g + 1) * GT * P)
                act.wait_ge(xt_full, g + 1)
                act.activation(xn_t[:, group], (px, po)[g % 2][:, :], ACT.Copy).then_inc(xt_copied, 1)
                act.wait_ge(lr_full, g + 1)
                act.activation(lr_t[0:DL, group], st[0:DL, g % 2, :], ACT.Copy).then_inc(lr_copied, 1)

            def guess_of(v, ln, half, y, ready):
                if half is not None:
                    act.activation(half, v, ACT.Identity, scale=-0.5 / HD, bias=eps_h[:, :])
                steps.done(act.activation(ln, v, ACT.Ln, scale=1.0 / HD, bias=eps[:, :]))
                steps.wait()
                act.activation(y, ln, ACT.Exp, scale=-0.5).then_inc(ready, 1)

            for i in range(FIRST_SLOT, LAST_SLOT + 1):
                j = i + 1
                if 0 <= j < SLOTS:
                    act.wait_ge(ht_full, j + 1)
                    if j >= 2:
                        act.wait_ge(hit_full, j - 1)
                    act.activation(hot_t[:, j % 2, :], st[:, 1, :].bitcast(BF16)[:, 0:GT * P], ACT.Copy)\
                       .then_inc(ht_copied, 1)
                    act.wait_ge(mid_full, j + 1)
                    if j >= 2:
                        act.wait_ge(h_ready, j - 1)
                    act.activation(mid[:, j % 2, :], s1[:, 2 + j % 2, :], ACT.Relu).then_inc(mid_copied, 1)
                b = (i + 4) // 2
                if i % 2 == 0 and 0 <= b < B:
                    act.wait_ge(pj_copied, QT * (b + 1))
                    if b >= 2:
                        act.wait_ge(kvar_ready, b - 1)
                    act.activation(ksq[:, b % 2, :], kc[:, QT * b:QT * b + QT, :].rearrange("p q d -> p (q d)"),
                                   ACT.Square).then_inc(k_squared, 1)
                b = (i + 2) // 2
                if i % 2 == 0 and 0 <= b < B:
                    act.wait_ge(kn_ready, b + 1)
                    if b >= 2:
                        act.wait_ge(kt_full, b - 1)
                    act.activation(pairs_turned(kp[:, b % 2, 0]), pairs(kn[:, b % 2]), ACT.Copy).then_inc(kpart, 1)
                    act.wait_ge(var_ready, b + 1)
                    if b >= 2:
                        act.wait_ge(parts_ready, b - 1)
                    guess_of(tvar[:, b % 2, :], lnv[:, b % 2, :], hv[:, b % 2, :], ty[:, b % 2, :], guess_ready)
                b = (i + 3) // 2
                if i % 2 == 1 and 0 <= b < B:
                    act.wait_ge(kvar_ready, b + 1)
                    if b >= 2:
                        act.wait_ge(kn_ready, b - 1)
                    guess_of(kvar[:, b % 2, :], klnv[:, b % 2, :], None, ky[:, b % 2, :], k_guessed)
                b = (i + 1) // 2
                if i % 2 == 1 and 0 <= b < B:
                    act.wait_ge(ksub, b + 1)
                    act.activation(pairs_turned(kp[:, b % 2, 1]), pairs(kn[:, b % 2]), ACT.Copy).then_inc(kpart, 1)
                if i >= FT and i % FT == 0 and i // FT <= GROUPS:
                    g = i // FT - 1
                    act.wait_ge(res_full, FT * (g + 1))
                    if g >= 2:
                        act.wait_ge(r_full, g - 1)
                    act.activation(res_t[:, g % 2, :], po[:, :], ACT.Identity, bias=col["b2"]).then_inc(res_copied, 1)
                for kind, b in in_slot(i):
                    if kind == "k":
                        act.wait_ge(kt_full, b + 1)
                        if b >= 1:
                            act.wait_ge(kt_stored[(b - 1) % 2], 16 * 3 * ((b - 1) // 2 + 1))
                        for e in range(2):
                            act.activation(tpk[:, :, e, :], px_b[:, 0:3 * T].rearrange("p (s t) -> p s t", s=3),
                                           ACT.Copy, scale=par_s[:, e:e + 1]).then_inc(kt_copied, 1)
                    if kind == "r":
                        act.wait_ge(r_full, b + 1)
                        act.activation(gate[:, GT * b:GT * b + GT, :], px[:, :].rearrange("p (n d) -> p n d", n=GT),
                                       ACT.Copy).then_inc(r_copied, 1)
            first_steps = steps.n

            def copy_max(it, n, half):
                act.wait_ge(mt_full, it * UNITS + n + 1)
                cols = slice(half * UH // 4 * T, (half + 1) * UH // 4 * T)
                act.activation(q_st[WIN_ROW:STACK, n % QB, cols], px_b[WIN_ROW:STACK, cols], ACT.Copy)\
                   .then_inc(mt_copied, 1)

            def round_(it, last):
                def copy_outputs(n):
                    act.wait_ge(pv_done, it * 2 * UNITS + 2 * (n + 1))
                    if n >= 2:
                        act.wait_ge(tt_full, it * NT + QT * (n // 2))
                    act.activation(o_t[:, n % 2, :], po[:, :], ACT.Copy).then_inc(o_copied, 1)

                def copy_tokens(t):
                    act.wait_ge(tt_full, it * NT + t + 1)
                    if t % QT == 0 and t:
                        act.wait_ge(pool_out if last else pool_sq, (it if last else it + 1) * B + t // QT)
                    act.activation(tt[:, t % QT, :, :],
                                   px[:, :].rearrange("p (h r) -> p h r", h=H)[:, :, 0:VC], ACT.Copy)\
                       .then_inc(tt_copied, 1)

                def guess(b):
                    act.wait_ge(var_ready, (it + 1) * B + b + 1)
                    act.activation(lnv[:, b % 2, :], tvar[:, b % 2, :], ACT.Ln, scale=1.0 / HD, bias=eps[:, :]).then_inc(act_step, 1)
                    act.activation(hv[:, b % 2, :], tvar[:, b % 2, :], ACT.Identity, scale=-0.5 / HD, bias=eps_h[:, :])
                    act.wait_ge(act_step, first_steps + it * B + b + 1)
                    act.activation(ty[:, b % 2, :], lnv[:, b % 2, :], ACT.Exp, scale=-0.5).then_inc(guess_ready, 1)

                for n in range(UNITS):
                    for h in range(UH):
                        i = n * UH + h
                        act.wait_ge(st_full, it * UNITS * UH + i + 1)
                        if i >= EB and h % GH == 0:
                            act.wait_ge(pv_done, it * 2 * UNITS + (i - EB) // GH + 1)
                        act.activation(e_sb[:, i % EB, :], st[:, i % 2, :], ACT.Exp).then_inc(exp_done, 1)
                        if h == 1 and n % 2 == 1 and n >= 3:
                            copy_tokens(QT * (n // 2 - 1) + 1)
                        if h == 2 and last:
                            if n >= 2:
                                act.wait_ge(gate_ready, n - 1)
                            act.activation(ge[:, n % 2, :], gate[:, n, :], ACT.Exp, scale=-1.0).then_inc(ge_exp, 1)
                        if h == 3 and n >= 1:
                            copy_outputs(n - 1)
                        if h in (4, 5) and n + 1 < UNITS:
                            copy_max(it, n + 1, h - 4)
                        if h == 6 and n % 2 == 0 and n >= 4 and not last:
                            guess(n // 2 - 2)
                        if h == 7 and n % 2 == 0 and n >= 2:
                            copy_tokens(QT * (n // 2 - 1))
                copy_outputs(UNITS - 1)
                copy_tokens(NT - 2)
                copy_tokens(NT - 1)
                if last:
                    return
                guess(B - 2)
                act.wait_ge(window_ready, it + 2)
                for i in range(2, QB):
                    done = act.activation(q_st[WIN_ROW:MAX_ROW, i, :],
                                          zero_rows[WIN_ROW:MAX_ROW, :].to_broadcast([len(LEVELS), UH // 2 * T]),
                                          ACT.Identity, bias=ctl[WIN_ROW:MAX_ROW, C_PEN:C_PEN + 1])
                    if i == 2:
                        guess(B - 1)
                done.then_inc(window_rows, 1)
                for half in range(2):
                    copy_max(it + 1, 0, half)

            for half in range(2):
                copy_max(0, 0, half)
            with act.Fori(0, ITERS - 1) as it:
                round_(it, False)
            round_(ITERS - 1, True)
            for g in range(GROUPS):
                act.wait_ge(at_full, g + 1)
                if g >= 2:
                    act.wait_ge(s_full, g - 1)
                act.activation(at_t[:, g % 2, :], st[:, g % 2, :], ACT.Copy).then_inc(at_copied, 1)

        @block.tensor
        def _(pe):
            def mm(out_, l, r, start=True, stop=True):
                return pe.matmul(out_, l, r, start=start, stop=stop)

            bdq, bdk, bdv, bv_t, bq_c, bk_c, _, bvq = (comp[:, i, :] for i in range(8))
            wide_of = {n: wide[:, i, :] for i, n in enumerate(BIASES)}
            pe.wait_ge(pool_prep, 1)
            mm(s1[:, 0, 0:D], bdq, cen_s[:, :])
            mm(s1[:, 0, D:2 * D], bdk, cen_s[:, :]).then_inc(pe_prep, 1)
            pe.wait_ge(act_prep, 1)
            mm(s1[:, 1, 0:D], bdv, bq_c).then_inc(pe_prep, 1)
            mm(s1[:, 2, 0:D], wq_s[:, :], bq_c)
            mm(s1[:, 2, D:2 * D], wk_s[:, :], bk_c)
            mm(s1[:, 2, 2 * D:3 * D], wv_s[:, :], bv_t)
            pe.wait_ge(act_prep, 2)
            mm(s1[:, 2, 3 * D:4 * D], wv_s[:, :], bvq)
            pe.wait_ge(pool_prep, 2)
            for at, terms in enumerate(([("bq", bq_c), ("lqb", cen_s[:, :])], [("lkb", cen_s[:, :])],
                                        [("bv", bv_t), ("lvb", id_s[:, :])], [("bv", bvq), ("lvb", bq_c)])):
                for i, (name, layer) in enumerate(terms):
                    last = mm(s1[:, 3, at * D:(at + 1) * D], wide_of[name], layer, start=i == 0,
                              stop=i == len(terms) - 1)
            last.then_inc(pe_prep, 1)

            def project(t):
                if t >= 2:
                    pe.wait_ge(pj_copied, t - 1)
                mm(s1[:, 2 + t % 2, :], xn_t[:, t * P:(t + 1) * P], w_all[:, :]).then_inc(pj_full, 1)

            for g in range(GROUPS + 1):
                if g < GROUPS:
                    pe.wait_ge(xn_ready, g + 1)
                    if g >= 2:
                        pe.wait_ge(xt_copied, g - 1)
                    for i in range(GT):
                        last = pe.transpose((px, po)[g % 2][:, i * P:(i + 1) * P], xn[:, GT * g + i, :], id_s[:, :])
                    last.then_inc(xt_full, 1)
                if g >= 1:
                    pe.wait_ge(xt_copied, g)
                    if g == 1:
                        pe.wait_ge(consts_in, 16 * len(loads))
                    if g >= 3:
                        pe.wait_ge(lr_copied, g - 2)
                    mm(st[0:DL, (g - 1) % 2, :], m1_s[:, :], xn_t[:, (g - 1) * GT * P:g * GT * P]).then_inc(lr_full, 1)
                    if g == 1:
                        pe.wait_ge(act_prep, 9)
                    for t in range(GT * (g - 1), GT * g):
                        project(t)

            def by_feature(src, b, full):
                for i in range(3):
                    for q in range(QT):
                        last = pe.transpose(px_b[:, i * T + q * P:i * T + (q + 1) * P],
                                            src(i, q), ident_b[:, :])
                last.then_inc(full, 1)

            def logits(t):
                if t >= 2:
                    pe.wait_ge(hot_ready, t - 1)
                mm(s1[:, t % 2, :], lr_t[:, t * P:(t + 1) * P], m2_s[:, :]).then_inc(lg_full, 1)

            def hot_turned(j):
                g, f = j // FT, j % FT
                pe.wait_ge(hot_ready, GT * (g + 1))
                if j:
                    pe.wait_ge(ht_copied, j)
                for i in range(GT):
                    last = pe.transpose(st[:, 1, :].bitcast(BF16)[:, i * P:(i + 1) * P],
                                        hot[:, g % 2, i, f * P:(f + 1) * P], ident_b[:, :])
                last.then_inc(ht_full, 1)

            def middle(j):
                g, f = j // FT, j % FT
                if j >= 2:
                    pe.wait_ge(mid_copied, j - 1)
                mm(s1[:, 2 + j % 2, :], w1_s[:, f * P:(f + 1) * P], xn_t[:, g * GT * P:(g + 1) * GT * P])\
                    .then_inc(mid_full, 1)

            def hits(i):
                pe.wait_ge(ht_copied, i + 1)
                if i:
                    pe.wait_ge(h_ready, i)
                mm(st[:, 0, :], hit_s[:, :], hot_t[:, i % 2, :]).then_inc(hit_full, 1)

            def results(i):
                g, f = i // FT, i % FT
                pe.wait_ge(h_ready, i + 1)
                if f == 0 and g:
                    pe.wait_ge(res_copied, g)
                mm(po[:, :], w2_s[:, f, :], hh[:, i % 4, :], start=f == 0, stop=f == FT - 1).then_inc(res_full, 1)

            def px_free(order, at):
                kind, i = order[at - 1]
                if kind == "k":
                    pe.wait_ge(kt_copied, 2 * (i + 1))
                if kind == "q":
                    pe.wait_ge(qt_copied, i + 1)
                if kind == "r":
                    pe.wait_ge(r_copied, i + 1)

            pe.wait_ge(lr_copied, GROUPS)
            pe.wait_ge(pj_copied, NT)
            for i in range(FIRST_SLOT, LAST_SLOT + 1):
                if i + LEAD < NT:
                    logits(i + LEAD)
                if 0 <= i + 1 < SLOTS:
                    hot_turned(i + 1)
                    middle(i + 1)
                if 0 <= i < SLOTS:
                    hits(i)
                if 0 <= i - 1 < SLOTS:
                    results(i - 1)
                for kind, b in in_slot(i):
                    at = PREP_ORDER.index((kind, b))
                    if at:
                        px_free(PREP_ORDER, at)
                    if kind == "k":
                        pe.wait_ge(kparts_ready, b + 1)
                        by_feature(lambda s, q: kp[:, b % 2, s, q, :], b, kt_full)
                    if kind == "q":
                        pe.wait_ge(parts_ready, b + 1)
                        by_feature(lambda s, q: pt[:, s, q, :], b, qt_full)
                    if kind == "r":
                        pe.wait_ge(res_copied, b + 1)
                        for j in range(GT):
                            last = pe.transpose(px[:, j * P:(j + 1) * P], res_t[:, b % 2, j * P:(j + 1) * P],
                                                id_s[:, :])
                        last.then_inc(r_full, 1)

            pe.wait_ge(k0_loaded, 16)
            pe.wait_ge(key_rows, 16)
            def scores_by_query(it, n, cc):
                i = n * CHUNKS + cc
                b, buf = n // 2, n % QB
                if cc == 0 and n % 2 == 0:
                    bufs = QB // 2
                    in_round = len(range(b % bufs, B, bufs))
                    pe.wait_ge(q_loaded[b % bufs], 16 * (it * in_round + b // bufs + 1))
                if i >= 2:
                    pe.wait_ge(max_taken, it * UNITS * CHUNKS + i - 1)
                for hl in range(CH):
                    h = (n % 2) * UH + CH * cc + hl
                    for q in range(QT):
                        last = mm(s1[:, 2 * (i % 2) + hl, q * T:(q + 1) * T],
                                  q_st[0:MAX_ROW, buf, cc * T + q * P:cc * T + (q + 1) * P],
                                  k_res[0:MAX_ROW, b, h * T:(h + 1) * T])
                last.then_inc(s1_full, 1)

            def turn_max(it, n):
                pe.wait_ge(mp_ready, it * UNITS + n + 1)
                for pair in range(UH // 2):
                    for q in range(QT):
                        at = pair * T + q * P
                        last = pe.transpose(px_b[WIN_ROW:STACK, at:at + P], mp[:, n % 2, q, pair, :],
                                            ident_b[:, :])
                last.then_inc(mt_full, 1)

            def first_maxima(it, queries):
                scores_by_query(it, 1, 0)
                scores_by_query(it, 1, 1)
                pe.wait_ge(qt_copied, queries)
                turn_max(it, 0)
                scores_by_query(it, 1, 2)
                scores_by_query(it, 1, 3)

            def round_(it, last):
                order = misc_order(last)

                def misc_free(kind, i):
                    if (kind, i) == ("m", 1):
                        pe.wait_ge(qt_copied, B + it * B)
                    was, j = order[order.index((kind, i)) - 1]
                    s, per = COPIED[was]
                    count = (B if was == "q" else 0) + it * per + j + 1
                    pe.wait_ge(s, count * 2 if was == "m" else count)

                def scores_by_key(n, hl):
                    i = n * UH + hl
                    b, buf = n // 2, n % QB
                    h = (n % 2) * UH + hl
                    if hl == 0:
                        pe.wait_ge(mt_copied, 2 * (it * UNITS + n + 1))
                    if i >= 2:
                        pe.wait_ge(exp_done, it * UNITS * UH + i - 1)
                    for k in range(QT):
                        last = mm(st[:, i % 2, k * T:(k + 1) * T],
                                  k_res[0:STACK, b, h * T + k * P:h * T + (k + 1) * P],
                                  q_st[0:STACK, buf, hl // 2 * T:(hl // 2 + 1) * T])
                    last.then_inc(st_full, 1)

                def outputs(g):
                    b, n = g // 4, g // 2
                    pe.wait_ge(exp_done, it * UNITS * UH + GH * (g + 1))
                    if g % 2 == 0 and n >= 1:
                        pe.wait_ge(o_copied, it * UNITS + n)
                    for k in range(QT):
                        for j in range(GH):
                            h = (g % 4) * GH + j
                            last = pe.matmul(po[32 * j:32 * j + VC, (g % 2) * T:(g % 2 + 1) * T],
                                             v_res[:, QT * b + k, h, :],
                                             e_sb[:, (GH * g + j) % EB, k * T:(k + 1) * T],
                                             start=k == 0, stop=k == QT - 1)
                    last.then_inc(pv_done, 1)

                def misc(kind, i):
                    misc_free(kind, i)
                    if kind == "m":
                        turn_max(it, i)
                    if kind == "t":
                        pe.wait_ge(o_copied, it * UNITS + 2 * (i // QT + 1))
                        for g in range(4):
                            last = pe.transpose(
                                px[:, g * P:(g + 1) * P],
                                o_t[:, g // 2, (g % 2) * T + (i % QT) * P:(g % 2) * T + (i % QT + 1) * P], id_s[:, :])
                        last.then_inc(tt_full, 1)
                    if kind == "q":
                        pe.wait_ge(parts_ready, (it + 1) * B + i + 1)
                        by_feature(lambda s, q: pt[:, s, q, :], i, qt_full)

                for n in range(UNITS):
                    for cc in range(CHUNKS):
                        scores_by_key(n, 2 * cc)
                        if n + 2 < UNITS:
                            if n == 0 and cc == 0:
                                pe.wait_ge(window_rows, it + 1)
                            scores_by_query(it, n + 2, cc)
                        scores_by_key(n, 2 * cc + 1)
                        if cc == 1 and n >= 1:
                            outputs(2 * n - 1)
                        if cc == 3:
                            outputs(2 * n)
                        for kind, i in in_body(n, cc, last):
                            misc(kind, i)
                outputs(2 * UNITS - 1)
                misc("t", NT - 2)
                misc("t", NT - 1)
                if last:
                    return
                pe.wait_ge(dall_ready, it + 1)
                pe.wait_ge(tt_copied, (it + 1) * NT)
                mm(px[:, 0:1], ones[:, :], dall[:, :]).then_inc(diff_full, 1)
                pe.wait_ge(window_ready, it + 2)
                for cc in range(CHUNKS):
                    scores_by_query(it + 1, 0, cc)
                pe.wait_ge(parts_ready, (it + 1) * B + B - 1)
                by_feature(lambda s, q: pt[:, s, q, :], B - 2, qt_full)
                first_maxima(it + 1, B + it * B + B - 1)
                pe.wait_ge(parts_ready, (it + 1) * B + B)
                pe.wait_ge(mt_copied, 2 * (it + 1) * UNITS + 2)
                by_feature(lambda s, q: pt[:, s, q, :], B - 1, qt_full)

            pe.wait_ge(window_ready, 1)
            for cc in range(CHUNKS):
                scores_by_query(0, 0, cc)
            pe.wait_ge(r_copied, GROUPS)
            first_maxima(0, B)
            pe.wait_ge(k_loaded, 16 * (B - 1))
            with pe.Fori(0, ITERS - 1) as it:
                round_(it, False)
            round_(ITERS - 1, True)

            def attended(g):
                pe.wait_ge(attn_taken, (ITERS - 1) * B + GT // QT * (g + 1))
                if g >= 2:
                    pe.wait_ge(at_copied, g - 1)
                for i in range(GT):
                    last = pe.transpose(st[:, g % 2, i * P:(i + 1) * P], attn[:, GT * g + i, :], id_s[:, :])
                last.then_inc(at_full, 1)

            attended(0)
            for g in range(GROUPS):
                if g + 2 < GROUPS:
                    attended(g + 1)
                pe.wait_ge(at_copied, g + 1)
                for i in range(GT):
                    last = mm(s1[:, g % 4, i * P:(i + 1) * P], at_t[:, g % 2, i * P:(i + 1) * P], wo_s[:, :])
                last.then_inc(s_full, 1)
                if g + 2 == GROUPS:
                    attended(g + 1)


VECTOR_STEPS = 18
POOL_STEPS = 161


def kernel(**inputs):
    import concourse.bacc as bacc
    from concourse.bass_utils import run_bass_kernel_spmd

    a = {k.removeprefix("L0_attn_").removeprefix("L0_ffn_"): np.asarray(v) for k, v in inputs.items()}
    f32 = np.float32

    def rows(v):
        return np.ascontiguousarray(np.broadcast_to(v.reshape(1, -1), (P, v.size)))

    def heads(v):
        return np.tile(v, H)

    level = np.zeros(P, f32)
    level[WIN_ROW:MAX_ROW] = LEVELS
    columns = {"bq": a["bq"], "bv": a["bv"], "lna": a["lna_w"], "lnb": a["lnb_w"], "lqb": heads(a["lq_b"]),
               "lkb": heads(a["lk_b"]), "lvb": heads(a["lv_b"]), "level": level, "b2": a["b2"]}
    for n, k in (("thr", "threshold"), ("temp", "temp_base"), ("fac", "factor")):
        columns[n] = np.broadcast_to(a[k].reshape(1), (P,))
    blocks = np.kron(np.eye(H, dtype=f32), np.ones((HD, HD), f32))
    key_side = np.zeros((STACK - WIN_ROW, B, H, T), f32)
    for i, lv in enumerate(LEVELS):
        key_side[i, :, :, lv:] = 1
    for e in range(2):
        key_side[len(LEVELS) + 3 * e:len(LEVELS) + 3 * e + 3, :, e::2, :] = 1
    import ml_dtypes
    even = (np.arange(D) // (H // 2) < HD).astype(f32)

    arrays = {
        "x": a["x"].reshape(B * T, D), "wq": a["Wq"], "wk": a["Wk"], "wv": a["Wv"], "wo_t": a["Wo"].T,
        "lq": np.tile(a["lq_w"], (H, H)), "lk": np.tile(a["lk_w"], (H, H)), "lv": np.tile(a["lv_w"], (H, H)),
        "lv_t": np.tile(a["lv_w"].T, (H, H)),
        "cols": np.stack([columns[n] for n in COLS], axis=1),
        "lnc": rows(heads(a["lnc_w"])), "lnd": rows(heads(a["lnd_w"])), "bo": rows(a["bo"]),
        "m1": a["m1"], "m2": a["m2"].reshape(DL, F), "mb": a["mb"].reshape(1, F), "w1": a["w1"].reshape(D, F),
        "w2": a["w2"].transpose(1, 0, 2).reshape(FT, P, D).transpose(1, 0, 2),
        "ident": np.eye(P, dtype=f32), "ident_bf": np.eye(P, dtype=ml_dtypes.bfloat16), "blocks": blocks, "centre": np.eye(P, dtype=f32) - blocks / HD,
        "first_hit": (np.eye(P) + 2 * np.triu(np.kron(np.eye(P // D2), np.ones((D2, D2))), 1)).astype(ml_dtypes.bfloat16),
        "token_pos": np.arange(T, dtype=f32).reshape(QT, P).T,
        "key_side": key_side.reshape(STACK - WIN_ROW, B, H * T).astype(ml_dtypes.bfloat16),
        "parity": np.stack([even, 1 - even], axis=1),
    }
    arrays = {k: np.ascontiguousarray(v) for k, v in arrays.items()}
    nc = bacc.Bacc("TRN2", target_bir_lowering=False, num_devices=1)
    aps = [nc.dram_tensor(f"in_{n}", v.shape, mybir.dt.from_np(v.dtype), kind="ExternalInput").ap()
           for n, v in arrays.items()]
    out = nc.dram_tensor("out", (B * T, D), F32, kind="ExternalOutput").ap()
    build(nc, *aps, out)
    r = run_bass_kernel_spmd(nc, [{f"in_{n}": v for n, v in arrays.items()}], core_ids=[0])
    return r.results[0]["out"].reshape(B, T, D)
```

```python
from contextlib import ExitStack

import concourse.bass as bass
import numpy as np
from concourse import mybir

F32 = mybir.dt.float32
BF16 = mybir.dt.bfloat16
I32 = mybir.dt.int32
ALU = mybir.AluOpType
ACT = mybir.ActivationFunctionType
AX_X = mybir.AxisListType.X

P = 128
B, T, D = 8, 256, 128
H = 16
HD = D // H
QT = T // P
NT = B * QT
ITERS = 3
MIN_WIN, MAX_WIN = 64, 256
EPS = 1e-5
QK_SCALE = float(HD) ** -0.25
INV_SQRT_E = float(np.float32(1.0 / np.sqrt(HD)))
UP_DIFF, DOWN_DIFF = 0.05, 0.001
assert B * T * D & (B * T * D - 1) == 0
SUM_UP, SUM_DOWN = (float(np.float32(v)) * B * T * D for v in (UP_DIFF, DOWN_DIFF))
TEMP_STEP = 0.005
RSQRT_SEED = 0x5F3759DF
PENALTY = -1e30

D1, D2, DL = 8, 64, 64
F = D1 * D2
FT = F // P
GT = 4
GROUPS = NT // GT
SLOTS = GROUPS * FT
OUT_ORDER = [0, 1, 2, 3]
LEAD = FT + 1


def window_after(cw, factor):
    return int(np.clip(int(np.float32(cw) * np.float32(factor)), MIN_WIN, T))


CW0 = max(min(T, MAX_WIN), MIN_WIN)
CW_DOWN = window_after(CW0, 0.9)
CW_DOWN_UP = window_after(CW_DOWN, 1.1)
CW_DOWN_DOWN = window_after(CW_DOWN, 0.9)
assert window_after(CW0, 1.1) == CW0 == T and CW_DOWN > MIN_WIN
LEVELS = [CW_DOWN_DOWN, CW_DOWN, CW_DOWN_UP]
assert LEVELS == sorted(LEVELS) and LEVELS[-1] < T

Q_PARTS = [0, 1, 2, 0, 1, 0]
K_PARTS = [0, 0, 0, 1, 1, 2]
PAIR = 2 * HD
WIN_ROW = len(Q_PARTS) * PAIR
MAX_ROW = WIN_ROW + len(LEVELS)
STACK = MAX_ROW + 6
BANDS = [(0, 3, 0), (3, 2, 1), (5, 1, 2)]

UH = 8
UNITS = B * H // UH
CH = 2
CHUNKS = UH // CH
GH = 4
VC = 2 * HD + 1
QB = 6
BUFS = QB // 2
EB = 8

COLS = ["bq", "bv", "lna", "lnb", "lqb", "lkb", "lvb", "thr", "temp", "fac", "level", "b2", "bo"]
BIASES = ["bq", "lqb", "lkb", "bv", "lvb"]


class Steps:

    def __init__(self, eng, sem, base=0):
        self.eng, self.sem, self.base, self.n = eng, sem, base, 0

    def done(self, instruction):
        instruction.then_inc(self.sem, 1)
        self.n += 1

    def wait(self):
        self.eng.wait_ge(self.sem, self.base + self.n)


def build(nc, x, wq, wk, wv, wo_t, lq, lk, lv, lv_t, cols, lnc, lnd, m1, m2, mb, w1, w2,
          ident, ident_bf, blocks, centre, first_hit, token_pos, key_side, parity, out):
    ctx = ExitStack()
    with ctx:
        def sb(name, shape, dt=F32):
            return ctx.enter_context(nc.sbuf_tensor(name, shape, dt))

        def psum(name, shape, dt=F32):
            return ctx.enter_context(nc.psum_tensor(name, shape, dt))

        def sem(name):
            return ctx.enter_context(nc.semaphore(name))

        x_sb = sb("x_sb", [P, NT, D])
        qk = sb("qk", [P, 2, NT, D])
        qc, kc = qk[:, 0], qk[:, 1]
        xn = qc
        xn_t = sb("xn_t", [P, NT * P])
        attn = xn_t[:, :].rearrange("p (n d) -> p n d", n=NT)
        gate = sb("gate", [P, NT * P])
        k_res = sb("k_res", [P, B, H * T], BF16)
        v_res = sb("v_res", [P, NT, H, VC])
        q_st = sb("q_st", [P, QB, UH // 2 * T], BF16)
        e_sb = sb("e_sb", [P, EB, QT * T])
        o_t = sb("o_t", [P, 2, 2 * T])
        tt = sb("tt", [P, QT, H, VC])
        mx = sb("mx", [P, 2, QT, UH])
        mr = sb("mr", [P, 2, QT, UH])
        mp = sb("mp", [P, 2, QT, UH // 2, STACK - WIN_ROW], BF16)
        pen = sb("pen", [P, len(LEVELS)])
        tp = sb("tp", [P, 2, 3, T], BF16)
        tpk = sb("tpk", [P, 3, 2, T], BF16)
        stat = sb("stat", [P, NT, 6])
        mv = sb("mv", [P, NT, 2])
        v1, v2, y1, y2, tmp = (sb(n, [P, NT]) for n in ("v1", "v2", "y1", "y2", "tmp"))
        kn = o_t[:, 0, :].rearrange("p (b q d) -> p b q d", b=2, q=QT)
        ksq = o_t[:, 1, :].rearrange("p (b x) -> p b x", b=2)
        kvar, klnv, khv, ky, ktmp = (sb(n, [P, 2, QT * H]) for n in ("kvar", "klnv", "khv", "ky", "ktmp"))
        layers = sb("layers", [P, 7, D])
        kp = layers[:, 0:6, :].rearrange("p n d -> p (n d)").bitcast(BF16)\
            .rearrange("p (b s q d) -> p b s q d", b=2, s=3, q=QT)
        ge = sb("ge", [P, 2, D])
        tvar = sb("tvar", [P, 2, QT * H])
        ty = sb("ty", [P, 2, QT * H])
        ttmp = sb("ttmp", [P, QT * H])
        lnv = sb("lnv", [P, 2, QT * H])
        hv = sb("hv", [P, 2, QT * H])
        eps, eps_h, c15 = (sb(n, [P, 1]) for n in ("eps", "eps_h", "c15"))
        rden = sb("rden", [P, QT, H])
        o_new = sb("o_new", [P, QT, D])
        d_new = sb("d_new", [P, QT, D])
        r_new = sb("r_new", [P, QT, D])
        q_n = sb("q_n", [P, QT, D])
        pt = sb("pt", [P, 3, QT, D], BF16)
        dsum = sb("dsum", [P, B])
        dall = sb("dall", [P, 1])
        ctl = sb("ctl", [P, 16])
        notdone = sb("notdone", [P, 1], I32)
        rowmask = sb("rowmask", [P, QT])
        temps = sb("temps", [P, ITERS + 1])
        tsc = sb("tsc", [P, ITERS + 1])
        tsv = sb("tsv", [P, ITERS + 1])
        tst = sb("tst", [P, ITERS + 1])
        tsc_now = sb("tsc_now", [P, 1])
        zero_rows = sb("zero_rows", [P, 1], BF16)
        w_all = sb("w_all", [P, 4 * D])
        bias = sb("bias", [P, 4 * D])
        comp = e_sb[:, 6:8, :].rearrange("p a (b d) -> p (a b) d", d=D)
        wide = e_sb[:, 4:6, :].rearrange("p a (b d) -> p (a b) d", d=D)
        scl = sb("scl", [P, 2])
        ones = sb("ones", [P, P])
        ident_b = sb("ident_b", [P, P], BF16)
        hit_s = sb("hit_s", [P, P], BF16)
        lr_t = sb("lr_t", [DL + 1, NT * P])
        gm = sb("gm", [P, 2, D1])
        hot = sb("hot", [P, 2, GT, F], BF16)
        hot_t = sb("hot_t", [P, 2, GT * P], BF16)
        hh, mid = e_sb[:, 0:4, :], e_sb[:, 4:6, :]
        spare = hot[:, :, :, :].rearrange("p a n f -> p (a n f)").bitcast(F32)
        at_t = spare[:, 0:2 * GT * P].rearrange("p (a t) -> p a t", a=2)
        s_sb = spare[:, 2 * GT * P:4 * GT * P].rearrange("p (a t) -> p a t", a=2)
        wo_s = sb("wo_s", [P, D])
        wq_s, wk_s, wv_s, lq_s, lk_s, lv_s, lvt_s = (layers[:, i, :] for i in range(7))
        col_s = sb("col_s", [P, len(COLS)])
        lnc_s, lnd_s = ge[:, 0, :], ge[:, 1, :]
        wkd = sb("wkd", [P, D])
        m1_s = sb("m1_s", [P, DL])
        m2_s = sb("m2_s", [DL + 1, F])
        w1_s = sb("w1_s", [P, F])
        w2_s = sb("w2_s", [P, FT, D])
        id_s = sb("id_s", [P, P])
        blk_s, cen_s = (tt[:, :, :, :].rearrange("p q h r -> p (q h r)")[:, i * P:(i + 1) * P] for i in range(2))
        pos_s = sb("pos_s", [P, QT])
        par_s = sb("par_s", [P, 2])

        q_scr = nc.dram_tensor("q_scr", [B, len(Q_PARTS), PAIR * H // 2, T], BF16, kind="Internal").ap()
        k_scr = nc.dram_tensor("k_scr", [B, len(K_PARTS), PAIR * H // 2, 2, T], BF16, kind="Internal").ap()

        s1 = psum("s1", [P, 4, 512])
        st = psum("st", [P, 2, 512])
        po = psum("po", [P, 512])
        px = psum("px", [P, 512])
        px_b = px[:, :].bitcast(BF16)

        col = {n: col_s[:, i:i + 1] for i, n in enumerate(COLS)}

        cols_in, layers_in, consts_in = sem("cols_in"), sem("layers_in"), sem("consts_in")
        x_in = sem("x_in")
        dve_step, pool_step, act_step = sem("dve_step"), sem("pool_step"), sem("act_step")
        pe_prep, act_prep, pool_prep = sem("pe_prep"), sem("act_prep"), sem("pool_prep")
        xn_ready, tsc_ready = sem("xn_ready"), sem("tsc_ready")
        xt_full, xt_copied = sem("xt_full"), sem("xt_copied")
        pj_full, pj_copied = sem("pj_full"), sem("pj_copied")
        k_squared, kvar_ready, k_guessed, kn_ready, kpart, ksub, kparts_ready = (
            sem(n) for n in ("k_squared", "kvar_ready", "k_guessed", "kn_ready", "kpart", "ksub", "kparts_ready"))
        kt_full, kt_copied = sem("kt_full"), sem("kt_copied")
        k_loaded = [sem(f"k_loaded{b}") for b in range(B)]
        kt_stored = [sem(f"kt_stored{i}") for i in range(2)]
        qt_full, qt_copied = sem("qt_full"), sem("qt_copied")
        q_stored = [sem(f"q_stored{i}") for i in range(2)]
        key_rows = sem("key_rows")
        q_loaded = [sem(f"q_loaded{i}") for i in range(QB // 2)]
        window_ready, first_rows, second_rows, window_rows, masks_ready = (
            sem(n) for n in ("window_ready", "first_rows", "second_rows", "window_rows", "masks_ready"))
        s1_full, max_taken = sem("s1_full"), sem("max_taken")
        mp_ready, mt_full, mt_copied = sem("mp_ready"), sem("mt_full"), sem("mt_copied")
        st_full, exp_done = sem("st_full"), sem("exp_done")
        pv_done, o_copied = sem("pv_done"), sem("o_copied")
        tt_full, tt_copied = sem("tt_full"), sem("tt_copied")
        rden_ready, out_ready, pool_sq, var_ready, parts_ready = (
            sem(n) for n in ("rden_ready", "out_ready", "pool_sq", "var_ready", "parts_ready"))
        diff_ready, diff_full, dall_ready, attn_taken = (
            sem(n) for n in ("diff_ready", "diff_full", "dall_ready", "attn_taken"))
        guess_ready = sem("guess_ready")
        lr_full, lr_copied = sem("lr_full"), sem("lr_copied")
        lg_full, hot_ready, ht_full, ht_copied, mid_full, mid_copied, hit_full, h_ready, res_full, res_copied = (
            sem(n) for n in ("lg_full", "hot_ready", "ht_full", "ht_copied", "mid_full", "mid_copied", "hit_full",
                             "h_ready", "res_full", "res_copied"))
        ge_exp, ge_plus, ge_inverse, gate_ready = (sem(n) for n in ("ge_exp", "ge_plus", "ge_inverse", "gate_ready"))
        at_full, at_copied, s_full, sg_ready, y_full, y_ready, y_stored = (
            sem(n) for n in ("at_full", "at_copied", "s_full", "sg_ready", "y_full", "y_ready", "y_stored"))

        block = ctx.enter_context(nc.Block())

        layer_loads = [(lq_s, lq), (blk_s, blocks), (lk_s, lk), (lv_s, lv), (lvt_s, lv_t), (cen_s, centre), (wq_s, wq),
                       (wk_s, wk), (wv_s, wv), (id_s[:, :], ident)]
        loads = [(lnc_s, lnc), (lnd_s, lnd), (m1_s[:, :], m1), (m2_s[0:DL, :], m2), (m2_s[DL:DL + 1, :], mb),
                 (ident_b[:, :], ident_bf), (w1_s[:, :], w1), (hit_s[:, :], first_hit), (w2_s[:, :, :], w2),
                 (par_s[:, :], parity), (wo_s[:, :], wo_t), (pos_s[:, :], token_pos)]

        def in_body(n, c, last):
            b = n // 2
            found = []
            if n % 2 == 0 and c == 3 and b >= 1:
                found.append(("t", QT * (b - 1)))
            if n % 2 == 1 and c == 0 and b >= 1:
                found.append(("t", QT * (b - 1) + 1))
            if c == 1 and n + 1 < UNITS:
                found.append(("m", n + 1))
            if n % 2 == 1 and c == 3 and b >= 2 and not last:
                found.append(("q", b - 2))
            return found

        def misc_order(last):
            order = [("m", 0)]
            for n in range(UNITS):
                for c in range(CHUNKS):
                    order += in_body(n, c, last)
            return order + [("t", QT * (B - 1)), ("t", QT * (B - 1) + 1)]

        def in_slot(i):
            found = []
            if i % 2 == 0 and 0 <= i < 2 * B:
                found.append(("k", i // 2))
            if i % 2 == 1 and 0 <= i < 2 * B - 1:
                found.append(("q", i // 2))
            return found

        FIRST_SLOT, LAST_SLOT = -LEAD, SLOTS
        PREP_ORDER = [u for i in range(FIRST_SLOT, LAST_SLOT + 1) for u in in_slot(i)]
        COPIED = {"m": (mt_copied, UNITS), "t": (tt_copied, NT), "q": (qt_copied, B)}

        @block.sync
        def _(sp):
            sp.dma_start(col_s[:, :], cols).then_inc(cols_in, 16)
            sp.dma_start(x_sb[:, :, :], x.rearrange("(n p) d -> p n d", p=P)).then_inc(x_in, 16)
            for dst, src in layer_loads:
                sp.dma_start(dst, src).then_inc(layers_in, 16)
            for dst, src in loads:
                sp.dma_start(dst, src).then_inc(consts_in, 16)
            sp.dma_start(k_res[WIN_ROW:STACK, :, :], key_side).then_inc(key_rows, 16)

            def store_k(b):
                sp.wait_ge(kt_copied, 2 * (b + 1))
                for first, count, part in BANDS:
                    rows = tpk[:, part].rearrange("c e t -> c (e t)").unsqueeze(1)
                    sp.dma_start(k_scr[b, first:first + count].rearrange("j c e t -> c j (e t)"),
                                 rows.to_broadcast([P, count, 2 * T])).then_inc(kt_stored[b % 2], 16)

            def load_k(b):
                sp.wait_ge(kt_stored[b % 2], 16 * 3 * (b // 2 + 1))
                sp.dma_start(k_res[0:WIN_ROW, b, :], k_scr[b].rearrange("j (r p) e t -> (j r) (p e t)", r=PAIR))\
                  .then_inc(k_loaded[b], 16)

            def store_q(b, count):
                sp.wait_ge(qt_copied, count)
                for first, n, _ in BANDS:
                    sp.dma_start(q_scr[b, first:first + n].rearrange("j c t -> c j t"),
                                 tp[:, b % 2, 0:n, :]).then_inc(q_stored[b % 2], 16)

            def load_q(it, b, stored):
                buf = 2 * b % QB
                sp.wait_ge(q_stored[b % 2], stored)
                sp.dma_start(q_st[0:WIN_ROW, buf:buf + 2, :].rearrange("r u x -> r (u x)"),
                             q_scr[b].rearrange("j (r p) t -> (j r) (p t)", r=PAIR)).then_inc(q_loaded[b % BUFS], 16)

            for b in range(B + 1):
                if b < B:
                    store_k(b)
                if b >= 1:
                    load_k(b - 1)
                if 1 <= b < B:
                    store_q(b - 1, b)
                if b == BUFS + 1:
                    load_q(0, 0, 48 * 2)
                    load_q(0, 2, 48 * 2)
                if b == BUFS + 2:
                    load_q(0, 1, 48 * 2)

            def load_first(it):
                for b in (0, 2, 1):
                    used = max(range(b, B, BUFS))
                    sp.wait_ge(st_full, it * UNITS * UH - (B - 1 - used) * 2 * UH)
                    load_q(it, b, 48 * (it * (B // 2) + b // 2 + 1))

            def queries(it, last):
                store_q(B - 1, (it + 1) * B)
                for n in range(1, UNITS, 2):
                    b = n // 2
                    if b + BUFS < B:
                        sp.wait_ge(st_full, it * UNITS * UH + (n + 1) * UH)
                        load_q(it, b + BUFS, 48 * (it * (B // 2) + (b + BUFS) // 2 + 1))
                    if b >= 2 and not last:
                        store_q(b - 2, B + it * B + b - 1)
                if not last:
                    load_first(it + 1)
                    store_q(B - 2, B + it * B + B - 1)

            with sp.Fori(0, ITERS - 1) as it:
                queries(it, False)
            queries(ITERS - 1, True)
            for i, g in enumerate(OUT_ORDER):
                sp.wait_ge(y_ready, i + 1)
                sp.dma_start(out[g * GT * P:(g + 1) * GT * P, :].rearrange("(n p) d -> p n d", p=P),
                             x_sb[:, g * GT:(g + 1) * GT, :]).then_inc(y_stored, 16)
            sp.wait_ge(y_stored, 16 * GROUPS)
            for i in range(2):
                sp.wait_ge(q_stored[i], 48 * B // 2 * ITERS)

        def pairs(v):
            return v.rearrange("t q (p r) -> t q p r", r=PAIR)

        def pairs_turned(v):
            return v.rearrange("t q (r p) -> t q p r", r=PAIR)

        def rsqrt(eng, steps, v, yy, t):
            steps.done(eng.tensor_scalar(yy.bitcast(I32), v.bitcast(I32), 1, None, ALU.arith_shift_right))
            steps.wait()
            steps.done(eng.tensor_scalar(yy.bitcast(I32), yy.bitcast(I32), -1.0, float(RSQRT_SEED), ALU.mult, ALU.add))
            steps.done(eng.tensor_scalar(v, v, -0.5, None, ALU.mult))
            for _ in range(3):
                steps.wait()
                steps.done(eng.tensor_tensor(t, yy, yy, ALU.mult))
                steps.wait()
                steps.done(eng.tensor_tensor(t, t, v, ALU.mult))
                steps.wait()
                steps.done(eng.scalar_tensor_tensor(yy, t, 1.5, yy, ALU.add, ALU.mult))
            steps.wait()

        C_DIFF, C_RHS, C_CONV, C_DONE, C_GATE, C_UP, C_DOWN, C_IS, C_CW, C_PEN, C_STEP_UP, C_STEP_DOWN = range(12)

        def c(i):
            return ctl[:, i:i + 1]

        @block.vector
        def _(dve):
            steps = Steps(dve, dve_step)
            dve.memset(v_res[:, :, :, VC - 1:VC], 1.0)
            dve.memset(c(C_GATE), 0.0)
            dve.memset(c(C_DONE), 0.0)
            dve.memset(c(C_CW), float(CW0))
            dve.memset(dsum[:, :], 0.0)
            dve.memset(notdone[:, :], 1)
            dve.memset(mp[:, :, :, :, :], 0.0).then_inc(masks_ready, 1)
            dve.wait_ge(cols_in, 16)
            steps.done(dve.tensor_copy(temps[:, 0:1], col["temp"]))
            for i in range(ITERS):
                steps.wait()
                steps.done(dve.tensor_scalar(temps[:, i + 1:i + 2], temps[:, i:i + 1], TEMP_STEP, None, ALU.add))
            steps.wait()
            steps.done(dve.tensor_scalar(tsv[:, :], temps[:, :], 0.0, None, ALU.is_gt))
            steps.wait()
            steps.done(dve.tensor_tensor(temps[:, :], temps[:, :], tsv[:, :], ALU.mult))
            steps.done(dve.tensor_scalar(tst[:, :], tsv[:, :], -1.0, 1.0, ALU.mult, ALU.add))
            steps.wait()
            steps.done(dve.tensor_tensor(tsv[:, :], temps[:, :], tst[:, :], ALU.add))
            steps.wait()
            rsqrt(dve, steps, tsv[:, :], tsc[:, :], tst[:, :])
            dve.tensor_copy(tsc_now[:, :], tsc[:, 0:1]).then_inc(tsc_ready, 1)

            dve.wait_ge(x_in, 16)
            for t in range(NT):
                last = dve.bn_stats(stat[:, t, :], x_sb[:, t, :])
            steps.done(last)
            steps.wait()
            for t in range(NT):
                last = dve.bn_aggr(mv[:, t, :], stat[:, t, :])
            steps.done(last)
            steps.wait()
            steps.done(dve.tensor_scalar(v1[:, :], mv[:, :, 1], EPS, None, ALU.add))
            steps.wait()
            rsqrt(dve, steps, v1[:, :], y1[:, :], tmp[:, :])
            for t in range(NT):
                last = dve.tensor_scalar(xn[:, t, :], x_sb[:, t, :], mv[:, t, 0:1], y1[:, t:t + 1],
                                         ALU.subtract, ALU.mult)
                if t % GT == GT - 1:
                    last.then_inc(xn_ready, 1)
            steps.done(dve.tensor_tensor(v2[:, :], y1[:, :], y1[:, :], ALU.mult))
            steps.wait()
            steps.done(dve.tensor_tensor(v2[:, :], v2[:, :], mv[:, :, 1], ALU.mult))
            steps.wait()
            steps.done(dve.tensor_scalar(v2[:, :], v2[:, :], EPS, None, ALU.add))
            steps.wait()
            rsqrt(dve, steps, v2[:, :], y2[:, :], tmp[:, :])
            dve.wait_ge(act_prep, 9)
            for t in range(NT):
                dve.wait_ge(pj_full, t + 1)
                pj = s1[:, 2 + t % 2, :]
                dve.scalar_tensor_tensor(qk[:, :, t, :], pj[:, 0:2 * D].rearrange("p (a d) -> p a d", a=2),
                                         y2[:, t:t + 1], bias[:, 0:2 * D].rearrange("p (a d) -> p a d", a=2),
                                         ALU.mult, ALU.add)
                dve.scalar_tensor_tensor(v_res[:, t, :, 0:2 * HD],
                                         pj[:, 2 * D:].rearrange("p (h x) -> p h x", h=H), y2[:, t:t + 1],
                                         bias[:, 2 * D:].rearrange("p (h x) -> p h x", h=H),
                                         ALU.mult, ALU.add).then_inc(pj_copied, 1)

            def copy_q(b, full, stored):
                dve.wait_ge(qt_full, full)
                if stored is not None:
                    dve.wait_ge(q_stored[b % 2], stored)
                dve.tensor_copy(tp[:, b % 2, :, :], px_b[:, 0:3 * T].rearrange("p (s t) -> p s t", s=3))\
                   .then_inc(qt_copied, 1)

            def variance(r, b):
                dve.wait_ge(pool_sq, r * B + b + 1)
                dve.tensor_reduce(tvar[:, b % 2, :], r_new[:, :, :].rearrange("p q (h e) -> p (q h) e", h=H),
                                  AX_X, ALU.add).then_inc(var_ready, 1)

            dve.wait_ge(pool_prep, 3)
            for i in range(FIRST_SLOT, LAST_SLOT + 1):
                b = (i - 2) // 2
                if i % 2 == 0 and 0 <= b < B - 1:
                    copy_q(b, b + 1, 48 * (b // 2) if b >= 2 else None)
                t = i + LEAD
                if t < NT:
                    g = t // GT
                    blockwise = s1[:, t % 2, :].rearrange("p (j q) -> p j q", j=D1)
                    dve.wait_ge(lg_full, t + 1)
                    steps.done(dve.tensor_reduce(gm[:, t % 2, :], blockwise, AX_X, ALU.max))
                    steps.wait()
                    if g >= 2 and t % GT == 0:
                        dve.wait_ge(ht_full, FT * (g - 1))
                    dve.tensor_tensor(hot[:, g % 2, t % GT, :].rearrange("p (j q) -> p j q", j=D1), blockwise,
                                      gm[:, t % 2, :].unsqueeze(2).to_broadcast([P, D1, D2]), ALU.is_equal)\
                       .then_inc(hot_ready, 1)
                if 0 <= i < SLOTS:
                    dve.wait_ge(hit_full, i + 1)
                    dve.wait_ge(mid_copied, i + 1)
                    if i >= 4:
                        dve.wait_ge(res_full, i - 3)
                    dve.scalar_tensor_tensor(hh[:, i % 4, :], st[:, 0, :], 1.0, mid[:, i % 2, :],
                                             ALU.is_equal, ALU.mult).then_inc(h_ready, 1)
                b = (i + 4) // 2
                if i % 2 == 0 and 0 <= b < B:
                    dve.wait_ge(k_squared, b + 1)
                    dve.tensor_reduce(kvar[:, b % 2, :], ksq[:, b % 2, :].rearrange("p (n e) -> p n e", e=HD),
                                      AX_X, ALU.add).then_inc(kvar_ready, 1)
                b = (i + 2) // 2
                if i % 2 == 0 and 0 <= b < B:
                    dve.wait_ge(kpart, 2 * b + 1)
                    dve.tensor_tensor(pairs(kn[:, b % 2]), pairs(kn[:, b % 2]), pairs_turned(kp[:, b % 2, 0]),
                                      ALU.subtract).then_inc(ksub, 1)
                b = (i + 3) // 2
                if i % 2 == 1 and 0 <= b < B:
                    dve.wait_ge(k_guessed, b + 1)
                    one = ky[:, b % 2, :]
                    steps.done(dve.tensor_scalar(khv[:, b % 2, :], kvar[:, b % 2, :], -0.5 / HD, -0.5 * EPS,
                                                 ALU.mult, ALU.add))
                    steps.done(dve.tensor_tensor(ktmp[:, b % 2, :], one, one, ALU.mult))
                    steps.wait()
                    steps.done(dve.tensor_tensor(ktmp[:, b % 2, :], ktmp[:, b % 2, :], khv[:, b % 2, :], ALU.mult))
                    steps.wait()
                    steps.done(dve.scalar_tensor_tensor(one, ktmp[:, b % 2, :], 1.5, one, ALU.add, ALU.mult))
                    steps.wait()
                    steps.done(dve.tensor_tensor(
                        kn[:, b % 2].rearrange("p q (h e) -> p (q h) e", h=H),
                        kc[:, QT * b:QT * b + QT, :].rearrange("p q (h e) -> p (q h) e", h=H),
                        one.unsqueeze(2).to_broadcast([P, QT * H, HD]), ALU.mult))
                    steps.wait()
                    dve.tensor_tensor(kn[:, b % 2], kn[:, b % 2],
                                      wkd[:, :].unsqueeze(1).to_broadcast([P, QT, D]), ALU.mult).then_inc(kn_ready, 1)
                    variance(0, b)
                b = (i + 1) // 2
                if i % 2 == 1 and 0 <= b < B:
                    dve.wait_ge(kpart, 2 * b + 2)
                    dve.tensor_tensor(pairs_turned(kp[:, b % 2, 2]), pairs(kn[:, b % 2]),
                                      pairs_turned(kp[:, b % 2, 1]), ALU.subtract).then_inc(kparts_ready, 1)
            before = steps.n

            def maxima(it, n, cc):
                i = n * CHUNKS + cc
                dve.wait_ge(s1_full, it * UNITS * CHUNKS + i + 1)
                if cc == 0 and n >= 2:
                    dve.wait_ge(mp_ready, it * UNITS + n - 1)
                dve.tensor_reduce(
                    mx[:, n % 2, :, CH * cc:CH * cc + CH].rearrange("p q h -> p h q"),
                    s1[:, 2 * (i % 2):2 * (i % 2) + 2, :].rearrange("p h (q k) -> p h q k", q=QT),
                    AX_X, ALU.max, negate=True).then_inc(max_taken, 1)

            def round_(it, last):
                rnd = Steps(dve, dve_step, before + it * VECTOR_STEPS)

                def inverse_sums(b):
                    dve.wait_ge(tt_copied, it * NT + QT * (b + 1))
                    dve.reciprocal(rden[:, :, :], tt[:, :, :, VC - 1]).then_inc(rden_ready, 1)

                def last_outputs():
                    dve.wait_ge(tt_copied, (it + 1) * NT)
                    rnd.done(dve.reciprocal(rden[:, :, :], tt[:, :, :, VC - 1]))
                    rnd.wait()
                    dve.tensor_tensor(rden[:, :, :], rden[:, :, :],
                                      rowmask[:, :].unsqueeze(2).to_broadcast([P, QT, H]), ALU.mult)\
                       .then_inc(rden_ready, 1)
                    dve.wait_ge(rden_ready, (it + 1) * B)
                    dve.wait_ge(attn_taken, it * B + B - 1)
                    outputs = dve.tensor_tensor(o_new[:, :, :].rearrange("p q (h e) -> p q h e", h=H),
                                                tt[:, :, :, 0:HD],
                                                rden[:, :, :].unsqueeze(3).to_broadcast([P, QT, H, HD]), ALU.mult)
                    if last:
                        outputs.then_inc(out_ready, 1)
                        return
                    rnd.done(outputs)
                    rnd.wait()
                    dve.tensor_tensor(d_new[:, :, :], o_new[:, :, :], attn[:, NT - QT:NT, :], ALU.subtract)\
                       .then_inc(out_ready, 1)

                def difference(b):
                    dve.wait_ge(out_ready, it * B + b + 1)
                    dve.tensor_reduce(dsum[:, b:b + 1], d_new[:, :, :].rearrange("p q d -> p (q d)"), AX_X,
                                      ALU.add, apply_absolute_value=True).then_inc(diff_ready, 1)

                def inverse_gate(t):
                    dve.wait_ge(ge_plus, t + 1)
                    dve.reciprocal(ge[:, t % 2, :], ge[:, t % 2, :]).then_inc(ge_inverse, 1)

                def keep(b):
                    if last:
                        dve.wait_ge(out_ready, it * B + b + 1)
                    dve.copy_predicated(attn[:, QT * b:QT * b + QT, :].rearrange("p q d -> p (q d)"),
                                        notdone[:, 0:1].to_broadcast([P, QT * D]),
                                        o_new[:, :, :].rearrange("p q d -> p (q d)")).then_inc(attn_taken, 1)

                def new_q(b):
                    copy_q(b, B + it * B + b + 1, 48 * (it * (B // 2) + (B + b) // 2))

                copy_q(B - 1, (it + 1) * B, 48 * (it * (B // 2) + (B - 1) // 2))
                for n in range(UNITS):
                    b = n // 2
                    for cc in range(CHUNKS):
                        if n + 2 < UNITS:
                            maxima(it, n + 2, cc)
                        if n % 2 == 1 and b >= 1 and cc == 1:
                            inverse_sums(b - 1)
                        if n % 2 == 0 and b >= 3 and cc == 0 and not last:
                            new_q(b - 3)
                        if n % 2 == 0 and b >= 2 and cc == 1:
                            if not last:
                                difference(b - 2)
                                variance(it + 1, b - 2)
                        if n % 2 == 0 and b >= 2 and cc == 3:
                            keep(b - 2)
                        if last and cc == 2 and n >= 1:
                            inverse_gate(n - 1)
                if last:
                    keep(B - 2)
                    inverse_gate(NT - 1)
                    last_outputs()
                    return
                new_q(B - 3)
                difference(B - 2)
                variance(it + 1, B - 2)
                keep(B - 2)
                last_outputs()
                difference(B - 1)
                dve.wait_ge(diff_ready, it * B + B)
                dve.tensor_reduce(dall[:, :], dsum[:, :], AX_X, ALU.add).then_inc(dall_ready, 1)
                keep(B - 1)
                rnd.done(dve.tensor_scalar(c(C_IS), c(C_CW), float(T), None, ALU.is_lt))
                rnd.wait()
                rnd.done(dve.tensor_scalar(c(C_STEP_UP), c(C_IS), float(CW_DOWN_UP - CW_DOWN), None, ALU.mult))
                rnd.done(dve.tensor_scalar(c(C_STEP_DOWN), c(C_IS),
                                           float((CW_DOWN_DOWN - CW_DOWN) - (CW_DOWN - CW0)),
                                           float(CW_DOWN - CW0), ALU.mult, ALU.add))
                rnd.wait()
                dve.wait_ge(diff_full, it + 1)
                rnd.done(dve.scalar_tensor_tensor(c(C_UP), px[:, 0:1], SUM_UP, c(C_STEP_UP), ALU.is_gt, ALU.mult))
                rnd.done(dve.scalar_tensor_tensor(c(C_DOWN), px[:, 0:1], SUM_DOWN, c(C_STEP_DOWN),
                                                  ALU.is_lt, ALU.mult))
                rnd.done(dve.tensor_scalar(c(C_DIFF), px[:, 0:1], 1.0 / (B * T * D), None, ALU.mult))
                rnd.wait()
                rnd.done(dve.scalar_tensor_tensor(c(C_CW), c(C_UP), c(C_DOWN), c(C_CW), ALU.add, ALU.add))
                rnd.wait()
                rnd.done(dve.tensor_scalar(c(C_PEN), col["level"], c(C_CW), PENALTY, ALU.is_ge, ALU.mult))
                rnd.wait()
                dve.tensor_scalar(q_st[WIN_ROW:MAX_ROW, 0, 0:T],
                                  zero_rows[WIN_ROW:MAX_ROW, :].to_broadcast([len(LEVELS), T]),
                                  ctl[WIN_ROW:MAX_ROW, C_PEN:C_PEN + 1], None, ALU.add).then_inc(window_ready, 1)
                rnd.done(dve.tensor_scalar(c(C_RHS), c(C_DIFF), col["fac"], col["thr"], ALU.mult, ALU.add))
                for i, level in enumerate(LEVELS):
                    rnd.done(dve.tensor_scalar(pen[:, i:i + 1], c(C_CW), float(level), PENALTY, ALU.is_le, ALU.mult))
                rnd.wait()
                rnd.done(dve.tensor_copy(mp[:, :, :, :, 0:len(LEVELS)].rearrange("p n q c r -> p (n q c) r"),
                                         pen[:, :].unsqueeze(1).to_broadcast([P, QT * UH, len(LEVELS)])))
                rnd.done(dve.tensor_tensor(c(C_CONV), c(C_DIFF), c(C_RHS), ALU.is_lt))
                maxima(it + 1, 0, 0)
                rnd.wait()
                rnd.done(dve.scalar_tensor_tensor(c(C_DONE), c(C_CONV), c(C_GATE), c(C_DONE), ALU.mult, ALU.max))
                variance(it + 1, B - 1)
                rnd.done(dve.tensor_scalar(rowmask[:, :], pos_s[:, :], c(C_CW), None, ALU.is_lt))
                rnd.wait()
                rnd.done(dve.tensor_scalar(notdone[:, :], c(C_DONE), 0.0, None, ALU.is_equal))
                rnd.wait()
                dve.memset(c(C_GATE), 1.0).then_inc(masks_ready, 1)
                for cc in range(1, CHUNKS):
                    maxima(it + 1, 0, cc)
                new_q(B - 2)
                for cc in range(CHUNKS):
                    maxima(it + 1, 1, cc)
                assert rnd.n == VECTOR_STEPS, rnd.n

            for n in range(2):
                for cc in range(CHUNKS):
                    maxima(0, n, cc)
            with dve.Fori(0, ITERS - 1) as it:
                round_(it, False)
            round_(ITERS - 1, True)

            dve.wait_ge(out_ready, ITERS * B)
            dve.copy_predicated(attn[:, NT - QT:NT, :].rearrange("p q d -> p (q d)"),
                                notdone[:, 0:1].to_broadcast([P, QT * D]),
                                o_new[:, :, :].rearrange("p q d -> p (q d)")).then_inc(attn_taken, 1)

            def gated_rows(i):
                g = OUT_ORDER[i]
                dve.wait_ge(s_full, i + 1)
                dve.wait_ge(gate_ready, GT * (g + 1))
                dve.scalar_tensor_tensor(s_sb[:, i % 2, :], s1[:, i % 2, :], col["bo"],
                                         gate[:, g * GT * P:(g + 1) * GT * P],
                                         ALU.add, ALU.mult).then_inc(sg_ready, 1)

            gated_rows(0)
            for i, g in enumerate(OUT_ORDER):
                if i + 1 < GROUPS:
                    gated_rows(i + 1)
                dve.wait_ge(y_full, i + 1)
                tiles = slice(GT * g, GT * g + GT)
                dve.tensor_tensor(x_sb[:, tiles, :], s1[:, 2 + i % 2, :].rearrange("p (n d) -> p n d", n=GT),
                                  x_sb[:, tiles, :], ALU.add).then_inc(y_ready, 1)

        @block.gpsimd
        def _(pool):
            heads = "p q (h e) -> p q h e"
            zeros = zero_rows[:, :].unsqueeze(2)
            pool.memset(ones[:, :], 1.0)
            pool.memset(zero_rows[:, :], 0.0)
            pool.memset(eps[:, :], EPS)
            pool.memset(eps_h[:, :], -0.5 * EPS)
            pool.memset(c15[:, :], 1.5)
            prep = Steps(pool, pool_step)
            prep.done(pool.memset(rowmask[:, :], 1.0))
            prep.wait()
            prep.done(pool.memset(lr_t[DL:DL + 1, :], 1.0))
            prep.wait()
            pool.memset(q_st[WIN_ROW:, 0, :], 0.0).then_inc(window_ready, 1)
            pool.wait_ge(window_ready, 1)
            pool.memset(q_st[WIN_ROW:, 1, :], 0.0).then_inc(second_rows, 1)
            pool.wait_ge(second_rows, 1)
            pool.wait_ge(cols_in, 16)
            pool.wait_ge(layers_in, 16 * len(layer_loads))
            for i, w in enumerate((lq_s, lk_s, lv_s, lvt_s)):
                last = pool.tensor_tensor(comp[:, i, :], w[:, :], blk_s[:, :], ALU.mult)
            last.then_inc(pool_prep, 1)
            for i, name in enumerate(BIASES):
                last = pool.tensor_tensor(wide[:, i, :], ones[:, :], col[name].to_broadcast([P, P]), ALU.mult)
            prep.done(last)
            prep.wait()
            prep.done(pool.tensor_scalar(wide[:, 0, :], wide[:, 0, :], QK_SCALE, None, ALU.mult))
            prep.done(pool.tensor_scalar(scl[:, 0:1], col["lna"], QK_SCALE, None, ALU.mult))
            pool.tensor_scalar(scl[:, 1:2], col["lnb"], QK_SCALE, None, ALU.mult).then_inc(pool_prep, 1)
            pool.wait_ge(consts_in, 16 * len(loads))
            prep.done(pool.tensor_scalar(wkd[:, :], lnc_s[:, :], INV_SQRT_E, None, ALU.mult))
            prep.wait()
            pool.tensor_tensor(wkd[:, :], wkd[:, :], lnd_s[:, :], ALU.mult).then_inc(pool_prep, 1)
            pool.wait_ge(pool_prep, 3)
            pool.memset(q_st[WIN_ROW:, 2:QB, :], 0.0).then_inc(window_rows, 1)
            pool.wait_ge(window_rows, 1)

            def split_max(rnd, it, n):
                m, r = (v[:, n % 2].rearrange("p q (c e) -> p q c e", e=2) for v in (mx, mr))
                w = mp[:, n % 2, :, :, len(LEVELS):].rearrange("p q c (e s) -> p q c e s", e=2)
                pool.wait_ge(max_taken, it * UNITS * CHUNKS + (n + 1) * CHUNKS)
                if n >= 2:
                    pool.wait_ge(mt_full, it * UNITS + n - 1)
                no = zeros.unsqueeze(3).to_broadcast([P, QT, UH // 2, 2])
                rnd.done(pool.tensor_tensor(w[:, :, :, :, 0], m, no, ALU.add))
                rnd.wait()
                rnd.done(pool.tensor_tensor(r, m, w[:, :, :, :, 0], ALU.subtract))
                rnd.wait()
                rnd.done(pool.tensor_tensor(w[:, :, :, :, 1], r, no, ALU.add))
                rnd.wait()
                pool.tensor_tensor(w[:, :, :, :, 2], r, w[:, :, :, :, 1], ALU.subtract).then_inc(mp_ready, 1)

            def new_queries(rnd, r, b):
                tiles = slice(QT * b, QT * b + QT)
                pool.wait_ge(guess_ready, r * B + b + 1)
                rnd.done(pool.tensor_tensor(ttmp[:, :], ty[:, b % 2, :], ty[:, b % 2, :], ALU.mult))
                rnd.wait()
                rnd.done(pool.tensor_tensor(ttmp[:, :], ttmp[:, :], hv[:, b % 2, :], ALU.mult))
                rnd.wait()
                rnd.done(pool.tensor_tensor(ttmp[:, :], ttmp[:, :], c15[:, :].to_broadcast([P, QT * H]), ALU.add))
                rnd.wait()
                rnd.done(pool.tensor_tensor(ty[:, b % 2, :], ty[:, b % 2, :], ttmp[:, :], ALU.mult))
                rnd.wait()
                rnd.done(pool.tensor_tensor(ty[:, b % 2, :], ty[:, b % 2, :],
                                            tsc_now[:, :].to_broadcast([P, QT * H]), ALU.mult))
                rnd.wait()
                for e in range(2):
                    rnd.done(pool.tensor_tensor(
                        q_n[:, :, e * D // 2:(e + 1) * D // 2].rearrange("p q (d c) -> p q c d", d=HD),
                        qc[:, tiles, :].rearrange("p q (c e d) -> p q c e d", e=2, d=HD)[:, :, :, e, :],
                        ty[:, b % 2, :].rearrange("p (q c e) -> p q c e", q=QT, e=2)[:, :, :, e]
                        .unsqueeze(3).to_broadcast([P, QT, H // 2, HD]), ALU.mult))
                rnd.wait()

            def query_parts(rnd, r, b, first=False):
                if not first:
                    pool.wait_ge(qt_full, r * B + b)
                no = zeros.to_broadcast([P, QT, D])
                rnd.done(pool.tensor_tensor(pt[:, 0], q_n[:, :, :], no, ALU.add))
                rnd.wait()
                rnd.done(pool.tensor_tensor(q_n[:, :, :], q_n[:, :, :], pt[:, 0], ALU.subtract))
                rnd.wait()
                rnd.done(pool.tensor_tensor(pt[:, 1], q_n[:, :, :], no, ALU.add))
                rnd.wait()
                pool.tensor_tensor(pt[:, 2], q_n[:, :, :], pt[:, 1], ALU.subtract)\
                    .then_inc(parts_ready, 1)

            def round_(it, last):
                rnd = Steps(pool, pool_step, FIRST_POOL_STEPS + it * POOL_STEPS)

                def gated(t):
                    pool.wait_ge(ge_inverse, t + 1)
                    tokens = slice(t * P, (t + 1) * P)
                    pool.tensor_tensor(gate[:, tokens], gate[:, tokens], ge[:, t % 2, :], ALU.mult)\
                        .then_inc(gate_ready, 1)

                def new_outputs(b, then=None):
                    tiles = slice(QT * b, QT * b + QT)
                    pool.wait_ge(rden_ready, it * B + b + 1)
                    over = rden[:, :, :].unsqueeze(3).to_broadcast([P, QT, H, HD])
                    if b < B - 1:
                        rnd.done(pool.tensor_tensor(rden[:, :, :], rden[:, :, :],
                                                    rowmask[:, :].unsqueeze(2).to_broadcast([P, QT, H]), ALU.mult))
                        rnd.wait()
                    if 1 <= b < B - 1:
                        pool.wait_ge(attn_taken, it * B + b)
                    if last:
                        pool.tensor_tensor(o_new[:, :, :].rearrange(heads, h=H), tt[:, :, :, 0:HD], over,
                                           ALU.mult).then_inc(out_ready, 1)
                        return
                    if b < B - 1:
                        rnd.done(pool.tensor_tensor(o_new[:, :, :].rearrange(heads, h=H), tt[:, :, :, 0:HD], over,
                                                    ALU.mult))
                        rnd.wait()
                        pool.tensor_tensor(d_new[:, :, :], o_new[:, :, :], attn[:, tiles, :], ALU.subtract)\
                            .then_inc(out_ready, 1)
                    if then is not None:
                        split_max(rnd, it, then)
                    pool.wait_ge(var_ready, (it + 1) * B + b)
                    rnd.done(pool.tensor_tensor(r_new[:, :, :].rearrange(heads, h=H), tt[:, :, :, HD:2 * HD], over,
                                                ALU.mult))
                    rnd.wait()
                    rnd.done(pool.tensor_tensor(qc[:, tiles, :], qc[:, tiles, :], r_new[:, :, :], ALU.add))
                    rnd.wait()
                    pool.tensor_tensor(r_new[:, :, :], qc[:, tiles, :], qc[:, tiles, :], ALU.mult).then_inc(pool_sq, 1)

                if not last:
                    rnd.done(pool.tensor_copy(tsc_now[:, :], tsc[:, bass.ds(it + 1, 1)]))
                    rnd.wait()
                for n in range(UNITS):
                    b = n // 2
                    if n % 2 == 0 and b >= 2 and not last:
                        new_queries(rnd, it + 1, b - 2)
                    if n % 2 == 1:
                        if b >= 2 and not last:
                            query_parts(rnd, it + 1, b - 2)
                        between = n + 2 if b >= 1 and n + 2 < UNITS and not last else None
                        if b >= 1:
                            new_outputs(b - 1, between)
                    if n + 2 < UNITS and not (n % 2 == 1 and b >= 1 and not last):
                        split_max(rnd, it, n + 2)
                    if last:
                        if n >= 1:
                            gated(n - 1)
                        pool.wait_ge(ge_exp, n + 1)
                        pool.tensor_tensor(ge[:, n % 2, :], ge[:, n % 2, :], ones[:, :], ALU.add).then_inc(ge_plus, 1)
                if last:
                    gated(NT - 1)
                if last:
                    return
                new_outputs(B - 1)
                new_queries(rnd, it + 1, B - 2)
                query_parts(rnd, it + 1, B - 2)
                new_queries(rnd, it + 1, B - 1)
                split_max(rnd, it + 1, 0)
                query_parts(rnd, it + 1, B - 1)
                split_max(rnd, it + 1, 1)
                assert rnd.n == POOL_STEPS, rnd.n

            def square(b):
                pool.wait_ge(pj_copied, QT * (b + 1))
                if b >= 1:
                    pool.wait_ge(var_ready, b)
                tiles = slice(QT * b, QT * b + QT)
                pool.tensor_tensor(r_new[:, :, :], qc[:, tiles, :], qc[:, tiles, :], ALU.mult).then_inc(pool_sq, 1)

            pool.wait_ge(tsc_ready, 1)
            square(0)
            for b in range(B):
                if b + 1 < B:
                    square(b + 1)
                new_queries(prep, 0, b)
                query_parts(prep, 0, b, first=b == 0)
            pool.wait_ge(mid_full, SLOTS)
            prep.done(pool.memset(attn[:, :, :], 0.0))
            prep.wait()
            for n in range(2):
                split_max(prep, 0, n)
            FIRST_POOL_STEPS = prep.n
            with pool.Fori(0, ITERS - 1) as it:
                round_(it, False)
            round_(ITERS - 1, True)

        @block.scalar
        def _(act):
            act.preload_act_table_set("natural_log_exp_and_others")
            steps = Steps(act, act_step)

            def copy_x(g):
                act.wait_ge(xt_full, g + 1)
                act.activation(xn_t[:, g * GT * P:(g + 1) * GT * P], (px, po)[g % 2][:, :], ACT.Copy)\
                   .then_inc(xt_copied, 1)

            act.wait_ge(pe_prep, 1)
            act.activation(comp[:, 4:6, :], s1[:, 0, 0:2 * D].rearrange("p (a d) -> p a d", a=2), ACT.Copy)\
               .then_inc(act_prep, 1)
            act.wait_ge(pe_prep, 2)
            act.activation(comp[:, 7, :], s1[:, 1, 0:D], ACT.Copy).then_inc(act_prep, 1)
            act.wait_ge(pe_prep, 3)
            act.wait_ge(pool_prep, 2)
            act.activation(w_all[:, 0:D], s1[:, 2, 0:D], ACT.Copy, scale=scl[:, 0:1]).then_inc(act_prep, 1)
            act.activation(w_all[:, D:2 * D], s1[:, 2, D:2 * D], ACT.Copy, scale=scl[:, 1:2]).then_inc(act_prep, 1)
            by_head = "p (h a e) -> p a h e"
            by_kind = "p (a h e) -> p a h e"
            for dst, src, scale in ((w_all, s1[:, 2, 2 * D:], col["lnb"]), (bias, s1[:, 3, 2 * D:], 1.0)):
                if dst is bias:
                    copy_x(0)
                    act.wait_ge(pe_prep, 4)
                for a in range(2):
                    act.activation(dst[:, 2 * D:].rearrange(by_head, h=H, a=2)[:, a],
                                   src.rearrange(by_kind, h=H, a=2)[:, a], ACT.Copy, scale=scale).then_inc(act_prep, 1)
            act.activation(bias[:, 0:2 * D], s1[:, 3, 0:2 * D], ACT.Copy).then_inc(act_prep, 1)
            for g in range(GROUPS):
                group = slice(g * GT * P, (g + 1) * GT * P)
                if g:
                    copy_x(g)
                act.wait_ge(lr_full, g + 1)
                act.activation(lr_t[0:DL, group], st[0:DL, g % 2, :], ACT.Copy).then_inc(lr_copied, 1)

            def guess_of(v, ln, half, y, ready):
                if half is not None:
                    act.activation(half, v, ACT.Identity, scale=-0.5 / HD, bias=eps_h[:, :])
                steps.done(act.activation(ln, v, ACT.Ln, scale=1.0 / HD, bias=eps[:, :]))
                steps.wait()
                act.activation(y, ln, ACT.Exp, scale=-0.5).then_inc(ready, 1)

            for i in range(FIRST_SLOT, LAST_SLOT + 1):
                j = i + 1
                if 0 <= j < SLOTS:
                    act.wait_ge(ht_full, j + 1)
                    if j >= 2:
                        act.wait_ge(hit_full, j - 1)
                    act.activation(hot_t[:, j % 2, :], st[:, 1, :].bitcast(BF16)[:, 0:GT * P], ACT.Copy)\
                       .then_inc(ht_copied, 1)
                    act.wait_ge(mid_full, j + 1)
                    if j >= 2:
                        act.wait_ge(h_ready, j - 1)
                    act.activation(mid[:, j % 2, :], s1[:, 2 + j % 2, :], ACT.Relu).then_inc(mid_copied, 1)
                b = (i + 4) // 2
                if i % 2 == 0 and 0 <= b < B:
                    act.wait_ge(pj_copied, QT * (b + 1))
                    if b >= 2:
                        act.wait_ge(kvar_ready, b - 1)
                    act.activation(ksq[:, b % 2, :], kc[:, QT * b:QT * b + QT, :].rearrange("p q d -> p (q d)"),
                                   ACT.Square).then_inc(k_squared, 1)
                b = (i + 2) // 2
                if i % 2 == 0 and 0 <= b < B:
                    act.wait_ge(kn_ready, b + 1)
                    if b >= 2:
                        act.wait_ge(kt_full, b - 1)
                    act.activation(pairs_turned(kp[:, b % 2, 0]), pairs(kn[:, b % 2]), ACT.Copy).then_inc(kpart, 1)
                    act.wait_ge(var_ready, b + 1)
                    if b >= 2:
                        act.wait_ge(parts_ready, b - 1)
                    guess_of(tvar[:, b % 2, :], lnv[:, b % 2, :], hv[:, b % 2, :], ty[:, b % 2, :], guess_ready)
                b = (i + 3) // 2
                if i % 2 == 1 and 0 <= b < B:
                    act.wait_ge(kvar_ready, b + 1)
                    if b >= 2:
                        act.wait_ge(kn_ready, b - 1)
                    guess_of(kvar[:, b % 2, :], klnv[:, b % 2, :], None, ky[:, b % 2, :], k_guessed)
                b = (i + 1) // 2
                if i % 2 == 1 and 0 <= b < B:
                    act.wait_ge(ksub, b + 1)
                    act.activation(pairs_turned(kp[:, b % 2, 1]), pairs(kn[:, b % 2]), ACT.Copy).then_inc(kpart, 1)
                if i >= FT and i % FT == 0 and i // FT <= GROUPS:
                    g = i // FT - 1
                    act.wait_ge(res_full, FT * (g + 1))
                    act.activation(gate[:, g * GT * P:(g + 1) * GT * P], po[:, :], ACT.Identity, bias=col["b2"])\
                       .then_inc(res_copied, 1)
                for kind, b in in_slot(i):
                    if kind == "k":
                        act.wait_ge(kt_full, b + 1)
                        if b >= 1:
                            act.wait_ge(kt_stored[(b - 1) % 2], 16 * 3 * ((b - 1) // 2 + 1))
                        for e in range(2):
                            act.activation(tpk[:, :, e, :], px_b[:, 0:3 * T].rearrange("p (s t) -> p s t", s=3),
                                           ACT.Copy, scale=par_s[:, e:e + 1]).then_inc(kt_copied, 1)
            first_steps = steps.n

            def copy_max(it, n, half):
                act.wait_ge(mt_full, it * UNITS + n + 1)
                cols = slice(half * UH // 4 * T, (half + 1) * UH // 4 * T)
                act.activation(q_st[WIN_ROW:STACK, n % QB, cols], px_b[WIN_ROW:STACK, cols], ACT.Copy)\
                   .then_inc(mt_copied, 1)

            def round_(it, last):
                def copy_outputs(n):
                    act.wait_ge(pv_done, it * 2 * UNITS + 2 * (n + 1))
                    if n >= 2:
                        act.wait_ge(tt_full, it * NT + QT * (n // 2))
                    act.activation(o_t[:, n % 2, :], po[:, :], ACT.Copy).then_inc(o_copied, 1)

                def copy_tokens(t, bank=px):
                    act.wait_ge(tt_full, it * NT + t + 1)
                    if t % QT == 0 and t:
                        if last:
                            act.wait_ge(out_ready, it * B + t // QT)
                        else:
                            act.wait_ge(pool_sq, (it + 1) * B + t // QT)
                    act.activation(tt[:, t % QT, :, :],
                                   bank[:, :].rearrange("p (h r) -> p h r", h=H)[:, :, 0:VC], ACT.Copy)\
                       .then_inc(tt_copied, 1)

                def guess(b):
                    act.wait_ge(var_ready, (it + 1) * B + b + 1)
                    act.activation(lnv[:, b % 2, :], tvar[:, b % 2, :], ACT.Ln, scale=1.0 / HD, bias=eps[:, :])\
                       .then_inc(act_step, 1)
                    act.activation(hv[:, b % 2, :], tvar[:, b % 2, :], ACT.Identity, scale=-0.5 / HD, bias=eps_h[:, :])
                    act.wait_ge(act_step, first_steps + it * B + b + 1)
                    act.activation(ty[:, b % 2, :], lnv[:, b % 2, :], ACT.Exp, scale=-0.5).then_inc(guess_ready, 1)

                for n in range(UNITS):
                    for h in range(UH):
                        i = n * UH + h
                        act.wait_ge(st_full, it * UNITS * UH + i + 1)
                        if i >= EB and h % GH == 0:
                            act.wait_ge(pv_done, it * 2 * UNITS + (i - EB) // GH + 1)
                        act.activation(e_sb[:, i % EB, :], st[:, i % 2, :], ACT.Exp).then_inc(exp_done, 1)
                        if h == 1 and n % 2 == 1 and n >= 3:
                            copy_tokens(QT * (n // 2 - 1) + 1)
                        if h == 2 and last:
                            if n >= 2:
                                act.wait_ge(gate_ready, n - 1)
                            act.activation(ge[:, n % 2, :], gate[:, n * P:(n + 1) * P], ACT.Exp, scale=-1.0)\
                               .then_inc(ge_exp, 1)
                        if h == 3 and n >= 1:
                            copy_outputs(n - 1)
                        if h in (4, 5) and n + 1 < UNITS:
                            copy_max(it, n + 1, h - 4)
                        if h == 6 and n % 2 == 0 and n >= 4 and not last:
                            guess(n // 2 - 2)
                        if h == 7 and n % 2 == 0 and n >= 2:
                            copy_tokens(QT * (n // 2 - 1))
                copy_outputs(UNITS - 1)
                copy_tokens(NT - 2)
                copy_tokens(NT - 1, st[:, 0, :])
                if last:
                    return
                guess(B - 2)
                act.wait_ge(window_ready, it + 2)
                for i in range(QB):
                    start = 0 if i else T
                    zeros = zero_rows[WIN_ROW:MAX_ROW, :].to_broadcast([len(LEVELS), UH // 2 * T - start])
                    done = act.activation(q_st[WIN_ROW:MAX_ROW, i, start:], zeros, ACT.Identity,
                                          bias=ctl[WIN_ROW:MAX_ROW, C_PEN:C_PEN + 1])
                    if i == 0:
                        done.then_inc(first_rows, 1)
                    if i == 1:
                        done.then_inc(second_rows, 1)
                        guess(B - 1)
                done.then_inc(window_rows, 1)
                for half in range(2):
                    copy_max(it + 1, 0, half)

            for half in range(2):
                copy_max(0, 0, half)
            with act.Fori(0, ITERS - 1) as it:
                round_(it, False)
            round_(ITERS - 1, True)
            for i in range(GROUPS):
                act.wait_ge(at_full, i + 1)
                if i >= 2:
                    act.wait_ge(s_full, i - 1)
                act.activation(at_t[:, i % 2, :], st[:, 1 - i % 2, :], ACT.Copy).then_inc(at_copied, 1)

        @block.tensor
        def _(pe):
            def mm(out_, l, r, start=True, stop=True):
                return pe.matmul(out_, l, r, start=start, stop=stop)

            def turn_x(g):
                pe.wait_ge(xn_ready, g + 1)
                if g >= 2:
                    pe.wait_ge(xt_copied, g - 1)
                for i in range(GT):
                    last = pe.transpose((px, po)[g % 2][:, i * P:(i + 1) * P], xn[:, GT * g + i, :], id_s[:, :])
                last.then_inc(xt_full, 1)

            bdq, bdk, bdv, bv_t, bq_c, bk_c, _, bvq = (comp[:, i, :] for i in range(8))
            wide_of = {n: wide[:, i, :] for i, n in enumerate(BIASES)}
            pe.wait_ge(pool_prep, 1)
            mm(s1[:, 0, 0:D], bdq, cen_s[:, :])
            mm(s1[:, 0, D:2 * D], bdk, cen_s[:, :]).then_inc(pe_prep, 1)
            pe.wait_ge(act_prep, 1)
            mm(s1[:, 1, 0:D], bdv, bq_c).then_inc(pe_prep, 1)
            mm(s1[:, 2, 0:D], wq_s[:, :], bq_c)
            mm(s1[:, 2, D:2 * D], wk_s[:, :], bk_c)
            mm(s1[:, 2, 2 * D:3 * D], wv_s[:, :], bv_t)
            pe.wait_ge(act_prep, 2)
            mm(s1[:, 2, 3 * D:4 * D], wv_s[:, :], bvq).then_inc(pe_prep, 1)
            pe.wait_ge(pool_prep, 2)
            for g in range(2):
                turn_x(g)
            for at, terms in enumerate(([("bq", bq_c), ("lqb", cen_s[:, :])], [("lkb", cen_s[:, :])],
                                        [("bv", bv_t), ("lvb", id_s[:, :])], [("bv", bvq), ("lvb", bq_c)])):
                for i, (name, layer) in enumerate(terms):
                    last = mm(s1[:, 3, at * D:(at + 1) * D], wide_of[name], layer, start=i == 0,
                              stop=i == len(terms) - 1)
            last.then_inc(pe_prep, 1)

            def project(t):
                if t >= 2:
                    pe.wait_ge(pj_copied, t - 1)
                mm(s1[:, 2 + t % 2, :], xn_t[:, t * P:(t + 1) * P], w_all[:, :]).then_inc(pj_full, 1)

            for g in range(GROUPS + 1):
                if 2 <= g < GROUPS:
                    turn_x(g)
                if g >= 1:
                    pe.wait_ge(xt_copied, g)
                    if g == 1:
                        pe.wait_ge(consts_in, 16 * len(loads))
                    if g >= 3:
                        pe.wait_ge(lr_copied, g - 2)
                    mm(st[0:DL, (g - 1) % 2, :], m1_s[:, :], xn_t[:, (g - 1) * GT * P:g * GT * P]).then_inc(lr_full, 1)
                    if g == 1:
                        pe.wait_ge(act_prep, 9)
                    for t in range(GT * (g - 1), GT * g):
                        project(t)

            def by_feature(src, b, full):
                for i in range(3):
                    for q in range(QT):
                        last = pe.transpose(px_b[:, i * T + q * P:i * T + (q + 1) * P],
                                            src(i, q), ident_b[:, :])
                last.then_inc(full, 1)

            def logits(t):
                if t >= 2:
                    pe.wait_ge(hot_ready, t - 1)
                mm(s1[:, t % 2, :], lr_t[:, t * P:(t + 1) * P], m2_s[:, :]).then_inc(lg_full, 1)

            def hot_turned(j):
                g, f = j // FT, j % FT
                pe.wait_ge(hot_ready, GT * (g + 1))
                if j:
                    pe.wait_ge(ht_copied, j)
                for i in range(GT):
                    last = pe.transpose(st[:, 1, :].bitcast(BF16)[:, i * P:(i + 1) * P],
                                        hot[:, g % 2, i, f * P:(f + 1) * P], ident_b[:, :])
                last.then_inc(ht_full, 1)

            def middle(j):
                g, f = j // FT, j % FT
                if j >= 2:
                    pe.wait_ge(mid_copied, j - 1)
                mm(s1[:, 2 + j % 2, :], w1_s[:, f * P:(f + 1) * P], xn_t[:, g * GT * P:(g + 1) * GT * P])\
                    .then_inc(mid_full, 1)

            def hits(i):
                pe.wait_ge(ht_copied, i + 1)
                if i:
                    pe.wait_ge(h_ready, i)
                mm(st[:, 0, :], hit_s[:, :], hot_t[:, i % 2, :]).then_inc(hit_full, 1)

            def results(i):
                g, f = i // FT, i % FT
                pe.wait_ge(h_ready, i + 1)
                if f == 0 and g:
                    pe.wait_ge(res_copied, g)
                mm(po[:, :], w2_s[:, f, :], hh[:, i % 4, :], start=f == 0, stop=f == FT - 1).then_inc(res_full, 1)

            def px_free(order, at):
                kind, i = order[at - 1]
                if kind == "k":
                    pe.wait_ge(kt_copied, 2 * (i + 1))
                if kind == "q":
                    pe.wait_ge(qt_copied, i + 1)

            pe.wait_ge(lr_copied, GROUPS)
            pe.wait_ge(pj_copied, NT)
            for i in range(FIRST_SLOT, LAST_SLOT + 1):
                if i + LEAD < NT:
                    logits(i + LEAD)
                if 0 <= i + 1 < SLOTS:
                    hot_turned(i + 1)
                    middle(i + 1)
                if 0 <= i < SLOTS:
                    hits(i)
                if 0 <= i - 1 < SLOTS:
                    results(i - 1)
                for kind, b in in_slot(i):
                    at = PREP_ORDER.index((kind, b))
                    if at:
                        px_free(PREP_ORDER, at)
                    if kind == "k":
                        pe.wait_ge(kparts_ready, b + 1)
                        by_feature(lambda s, q: kp[:, b % 2, s, q, :], b, kt_full)
                    if kind == "q":
                        pe.wait_ge(parts_ready, b + 1)
                        by_feature(lambda s, q: pt[:, s, q, :], b, qt_full)

            pe.wait_ge(key_rows, 16)

            def scores_by_query(it, n, cc):
                i = n * CHUNKS + cc
                b, buf = n // 2, n % QB
                if cc == 0 and n % 2 == 0:
                    pe.wait_ge(k_loaded[b], 16)
                    bufs = QB // 2
                    in_round = len(range(b % bufs, B, bufs))
                    pe.wait_ge(q_loaded[b % bufs], 16 * (it * in_round + b // bufs + 1))
                if i >= 2:
                    pe.wait_ge(max_taken, it * UNITS * CHUNKS + i - 1)
                for hl in range(CH):
                    h = (n % 2) * UH + CH * cc + hl
                    for q in range(QT):
                        last = mm(s1[:, 2 * (i % 2) + hl, q * T:(q + 1) * T],
                                  q_st[0:MAX_ROW, buf, cc * T + q * P:cc * T + (q + 1) * P],
                                  k_res[0:MAX_ROW, b, h * T:(h + 1) * T])
                last.then_inc(s1_full, 1)

            def turn_max(it, n):
                pe.wait_ge(mp_ready, it * UNITS + n + 1)
                for pair in range(UH // 2):
                    for q in range(QT):
                        at = pair * T + q * P
                        last = pe.transpose(px_b[WIN_ROW:STACK, at:at + P], mp[:, n % 2, q, pair, :],
                                            ident_b[:, :])
                last.then_inc(mt_full, 1)

            def first_maxima(it, queries):
                pe.wait_ge(second_rows, it + 1)
                scores_by_query(it, 1, 0)
                scores_by_query(it, 1, 1)
                pe.wait_ge(qt_copied, queries)
                pe.wait_ge(masks_ready, it + 1)
                turn_max(it, 0)
                scores_by_query(it, 1, 2)
                scores_by_query(it, 1, 3)

            def round_(it, last):
                order = misc_order(last)

                def misc_free(kind, i):
                    if (kind, i) == ("m", 1):
                        pe.wait_ge(qt_copied, B + it * B)
                    was, j = order[order.index((kind, i)) - 1]
                    s, per = COPIED[was]
                    count = (B if was == "q" else 0) + it * per + j + 1
                    pe.wait_ge(s, count * 2 if was == "m" else count)

                def scores_by_key(n, hl):
                    i = n * UH + hl
                    b, buf = n // 2, n % QB
                    h = (n % 2) * UH + hl
                    if hl == 0:
                        pe.wait_ge(mt_copied, 2 * (it * UNITS + n + 1))
                    if i >= 2:
                        pe.wait_ge(exp_done, it * UNITS * UH + i - 1)
                    for k in range(QT):
                        last = mm(st[:, i % 2, k * T:(k + 1) * T],
                                  k_res[0:STACK, b, h * T + k * P:h * T + (k + 1) * P],
                                  q_st[0:STACK, buf, hl // 2 * T:(hl // 2 + 1) * T])
                    last.then_inc(st_full, 1)

                def outputs(g):
                    b, n = g // 4, g // 2
                    pe.wait_ge(exp_done, it * UNITS * UH + GH * (g + 1))
                    if g % 2 == 0 and n >= 1:
                        pe.wait_ge(o_copied, it * UNITS + n)
                    for k in range(QT):
                        for j in range(GH):
                            h = (g % 4) * GH + j
                            last = pe.matmul(po[32 * j:32 * j + VC, (g % 2) * T:(g % 2 + 1) * T],
                                             v_res[:, QT * b + k, h, :],
                                             e_sb[:, (GH * g + j) % EB, k * T:(k + 1) * T],
                                             start=k == 0, stop=k == QT - 1)
                    last.then_inc(pv_done, 1)

                def misc(kind, i, bank=px):
                    if bank is px:
                        misc_free(kind, i)
                    if kind == "m":
                        turn_max(it, i)
                    if kind == "t":
                        pe.wait_ge(o_copied, it * UNITS + 2 * (i // QT + 1))
                        for g in range(4):
                            last = pe.transpose(
                                bank[:, g * P:(g + 1) * P],
                                o_t[:, g // 2, (g % 2) * T + (i % QT) * P:(g % 2) * T + (i % QT + 1) * P], id_s[:, :])
                        last.then_inc(tt_full, 1)
                    if kind == "q":
                        pe.wait_ge(parts_ready, (it + 1) * B + i + 1)
                        by_feature(lambda s, q: pt[:, s, q, :], i, qt_full)

                for n in range(UNITS):
                    for cc in range(CHUNKS):
                        scores_by_key(n, 2 * cc)
                        if n + 2 < UNITS:
                            if n == 0 and cc == 0:
                                pe.wait_ge(window_rows, it + 1)
                            scores_by_query(it, n + 2, cc)
                        scores_by_key(n, 2 * cc + 1)
                        if cc == 1 and n >= 1:
                            outputs(2 * n - 1)
                        if cc == 3:
                            outputs(2 * n)
                        if n == 0 and cc == 0:
                            pe.wait_ge(parts_ready, (it + 1) * B)
                            pe.wait_ge(mt_copied, 2 * it * UNITS + 2)
                            by_feature(lambda s, q: pt[:, s, q, :], B - 1, qt_full)
                        for kind, i in in_body(n, cc, last):
                            misc(kind, i)
                outputs(2 * UNITS - 1)
                misc("t", NT - 2)
                misc("t", NT - 1, st[:, 0, :])
                if last:
                    return
                pe.wait_ge(dall_ready, it + 1)
                pe.wait_ge(tt_copied, (it + 1) * NT)
                mm(px[:, 0:1], ones[:, :], dall[:, :]).then_inc(diff_full, 1)
                pe.wait_ge(window_ready, it + 2)
                for cc in range(CHUNKS):
                    if cc == 1:
                        pe.wait_ge(first_rows, it + 1)
                    scores_by_query(it + 1, 0, cc)
                pe.wait_ge(parts_ready, (it + 1) * B + B - 1)
                by_feature(lambda s, q: pt[:, s, q, :], B - 2, qt_full)
                first_maxima(it + 1, B + it * B + B - 1)

            pe.wait_ge(window_ready, 1)
            for cc in range(CHUNKS):
                scores_by_query(0, 0, cc)
            pe.wait_ge(kt_copied, 2 * B)
            first_maxima(0, B - 1)
            with pe.Fori(0, ITERS - 1) as it:
                round_(it, False)
            round_(ITERS - 1, True)

            def attended(i):
                g = OUT_ORDER[i]
                pe.wait_ge(attn_taken, (ITERS - 1) * B + (B if g == GROUPS - 1 else GT // QT * (g + 1)))
                if i == 1:
                    pe.wait_ge(tt_copied, ITERS * NT)
                if i >= 2:
                    pe.wait_ge(at_copied, i - 1)
                for j in range(GT):
                    last = pe.transpose(st[:, 1 - i % 2, j * P:(j + 1) * P], attn[:, GT * g + j, :], id_s[:, :])
                last.then_inc(at_full, 1)

            def projected(i):
                pe.wait_ge(at_copied, i + 1)
                if i >= 2:
                    pe.wait_ge(sg_ready, i - 1)
                mm(s1[:, i % 2, :], wo_s[:, :], at_t[:, i % 2, :]).then_inc(s_full, 1)

            def by_token(i):
                pe.wait_ge(sg_ready, i + 1)
                if i >= 2:
                    pe.wait_ge(y_ready, i - 1)
                for j in range(GT):
                    last = pe.transpose(s1[:, 2 + i % 2, j * P:(j + 1) * P], s_sb[:, i % 2, j * P:(j + 1) * P],
                                        id_s[:, :])
                last.then_inc(y_full, 1)

            attended(0)
            attended(1)
            projected(0)
            for i in range(GROUPS):
                if i + 2 < GROUPS:
                    attended(i + 2)
                if i + 1 < GROUPS:
                    projected(i + 1)
                by_token(i)


VECTOR_STEPS = 19
POOL_STEPS = 159


def kernel(**inputs):
    import concourse.bacc as bacc
    from concourse.bass_utils import run_bass_kernel_spmd

    a = {k.removeprefix("L0_attn_").removeprefix("L0_ffn_"): np.asarray(v) for k, v in inputs.items()}
    f32 = np.float32

    def rows(v):
        return np.ascontiguousarray(np.broadcast_to(v.reshape(1, -1), (P, v.size)))

    def heads(v):
        return np.tile(v, H)

    level = np.zeros(P, f32)
    level[WIN_ROW:MAX_ROW] = LEVELS
    columns = {"bq": a["bq"], "bv": a["bv"], "lna": a["lna_w"], "lnb": a["lnb_w"], "lqb": heads(a["lq_b"]),
               "lkb": heads(a["lk_b"]), "lvb": heads(a["lv_b"]), "level": level, "b2": a["b2"], "bo": a["bo"]}
    for n, k in (("thr", "threshold"), ("temp", "temp_base"), ("fac", "factor")):
        columns[n] = np.broadcast_to(a[k].reshape(1), (P,))
    blocks = np.kron(np.eye(H, dtype=f32), np.ones((HD, HD), f32))
    key_side = np.zeros((STACK - WIN_ROW, B, H, T), f32)
    for i, lv in enumerate(LEVELS):
        key_side[i, :, :, lv:] = 1
    for e in range(2):
        key_side[len(LEVELS) + 3 * e:len(LEVELS) + 3 * e + 3, :, e::2, :] = 1
    import ml_dtypes
    even = (np.arange(D) // (H // 2) < HD).astype(f32)

    arrays = {
        "x": a["x"].reshape(B * T, D), "wq": a["Wq"], "wk": a["Wk"], "wv": a["Wv"], "wo_t": a["Wo"].T,
        "lq": np.tile(a["lq_w"], (H, H)), "lk": np.tile(a["lk_w"], (H, H)), "lv": np.tile(a["lv_w"], (H, H)),
        "lv_t": np.tile(a["lv_w"].T, (H, H)),
        "cols": np.stack([columns[n] for n in COLS], axis=1),
        "lnc": rows(heads(a["lnc_w"])), "lnd": rows(heads(a["lnd_w"])),
        "m1": a["m1"], "m2": a["m2"].reshape(DL, F), "mb": a["mb"].reshape(1, F), "w1": a["w1"].reshape(D, F),
        "w2": a["w2"].transpose(1, 0, 2).reshape(FT, P, D).transpose(1, 0, 2),
        "ident": np.eye(P, dtype=f32), "ident_bf": np.eye(P, dtype=ml_dtypes.bfloat16), "blocks": blocks,
        "centre": np.eye(P, dtype=f32) - blocks / HD,
        "first_hit": (np.eye(P) + 2 * np.triu(np.kron(np.eye(P // D2), np.ones((D2, D2))), 1))
        .astype(ml_dtypes.bfloat16),
        "token_pos": np.arange(T, dtype=f32).reshape(QT, P).T,
        "key_side": key_side.reshape(STACK - WIN_ROW, B, H * T).astype(ml_dtypes.bfloat16),
        "parity": np.stack([even, 1 - even], axis=1),
    }
    arrays = {k: np.ascontiguousarray(v) for k, v in arrays.items()}
    nc = bacc.Bacc("TRN2", target_bir_lowering=False, num_devices=1)
    aps = [nc.dram_tensor(f"in_{n}", v.shape, mybir.dt.from_np(v.dtype), kind="ExternalInput").ap()
           for n, v in arrays.items()]
    out = nc.dram_tensor("out", (B * T, D), F32, kind="ExternalOutput").ap()
    build(nc, *aps, out)
    r = run_bass_kernel_spmd(nc, [{f"in_{n}": v for n, v in arrays.items()}], core_ids=[0])
    return r.results[0]["out"].reshape(B, T, D)
```
